# Optimizing a Trainium2 kernel written in Bass

```python
import numpy as np
import jax
import jax.numpy as jnp

def _softmax(x, axis=-1):
    return jax.nn.softmax(x, axis=axis)

def _gelu(x):
    return jax.nn.gelu(x, approximate=True)

def _silu(x):
    return jax.nn.silu(x)

def _sigmoid(x):
    return jax.nn.sigmoid(x)

def _layernorm(x, axis=-1, eps=1e-05):
    m = jnp.mean(x, axis=axis, keepdims=True)
    v = jnp.var(x, axis=axis, keepdims=True)
    return (x - m) / jnp.sqrt(v + eps)

def _scatter_add(tgt, idx, src, axis=0):
    return tgt.at[idx].add(src)

def _segment_sum(src, seg, n):
    return jax.ops.segment_sum(src, seg, n)
kernel_name = 'mk_decoder_postln_d2_seqx_r4_df61c3'

def setup_inputs(seed: int=0):
    np.random.seed(seed)
    _w = jnp.asarray

    def _rec_inputs():
        import jax
        import jax.numpy as jnp
        _rk = jax.random.key(seed)
        x = -0.0002928 + 1 * jax.random.normal(jax.random.fold_in(_rk, 1), (8, 256, 256), jnp.float32)
        _lenS = 256 - jax.random.randint(jax.random.fold_in(_rk, 7), (8,), 0, max(1, 256 // 4) + 1, jnp.int32)
        _lenS2 = 256 - jax.random.randint(jax.random.fold_in(_rk, 8), (8,), 0, max(1, 256 // 4) + 1, jnp.int32)
        _ctx_1024P = jax.random.normal(jax.random.fold_in(_rk, 11), (8, 16, 256), jnp.float32)
        _ctx_1024c = jax.random.dirichlet(jax.random.fold_in(_rk, 511), 0.3 * jnp.ones((16,), jnp.float32), (8, 256))
        _ctx_1024t = jnp.einsum('bsk,bkd->bsd', _ctx_1024c, _ctx_1024P)
        _ctx_1024t = _ctx_1024t * jax.lax.rsqrt(jnp.mean(jnp.square(_ctx_1024t)) + 1e-12) * 0.953939
        ctx_1024 = -1.39393e-06 + 0.999914 * (_ctx_1024t + 0.3 * jax.random.normal(jax.random.fold_in(_rk, 611), (8, 256, 256), jnp.float32))
        _validS = jnp.arange(256)[None, :] < _lenS[:, None]
        _validS2 = jnp.arange(256)[None, :] < _lenS2[:, None]
        _causal = jnp.tril(jnp.ones((256, 256), dtype=bool))
        mask_BxS2_bf1 = jnp.ones((8, 256), dtype=bool)
        return (x, ctx_1024, mask_BxS2_bf1)
    x, ctx_1024, mask_BxS2_bf1 = _rec_inputs()

    def _L0_attn_setup():
        import jax, jax.numpy as jnp
        import numpy as np
        B, T, C = (4, 512, 256)
        H = 16
        D = C // H
        EPS = 1e-05

        def _rwkv_scan(r, k, v, w):
            b, t, c = r.shape
            wh = w.reshape(H, D)

            def split(u):
                return u.reshape(b, t, H, D).transpose(1, 0, 2, 3)
            rT, kT, vT = (split(r), split(k), split(v))

            def step(state, inp):
                kt, vt, rt = inp
                state = state * wh[None, :, :, None] + kt[..., :, None] * vt[..., None, :]
                out = jnp.einsum('bhij,bhj->bhi', state, rt)
                return (state, out)
            state0 = jnp.zeros((b, H, D, D), r.dtype)
            _, outs = jax.lax.scan(step, state0, (kT, vT, rT))
            return outs.transpose(1, 0, 2, 3).reshape(b, t, c)
        key = jax.random.key(seed)
        ks = jax.random.split(key, 14)
        std = 1.0 / np.sqrt(C)
        inp = {'x': jax.random.normal(ks[0], (B, T, C), jnp.float32), 'time_decay': jax.random.uniform(ks[1], (C,), jnp.float32, -0.1, -0.01), 'time_mix_k': jax.random.uniform(ks[2], (C,), jnp.float32, -0.1, 0.1), 'time_mix_v': jax.random.uniform(ks[3], (C,), jnp.float32, -0.1, 0.1), 'time_mix_r': jax.random.uniform(ks[4], (C,), jnp.float32, -0.1, 0.1), 'time_mix_g': jax.random.uniform(ks[5], (C,), jnp.float32, -0.1, 0.1), 'W_r': jax.random.normal(ks[6], (C, C), jnp.float32) * std, 'W_k': jax.random.normal(ks[7], (C, C), jnp.float32) * std, 'W_v': jax.random.normal(ks[8], (C, C), jnp.float32) * std, 'W_g': jax.random.normal(ks[9], (C, C), jnp.float32) * std, 'W_o': jax.random.normal(ks[10], (C, C), jnp.float32) * std, 'ln_gamma': jnp.ones((C,), jnp.float32), 'ln_beta': jnp.zeros((C,), jnp.float32)}
        return inp
    _L0_attn_all = _L0_attn_setup()
    _L0_attn_in = {k: v for k, v in _L0_attn_all.items() if k in ('time_decay', 'time_mix_k', 'time_mix_v', 'time_mix_r', 'time_mix_g', 'W_r', 'W_k', 'W_v', 'W_g', 'W_o', 'ln_gamma', 'ln_beta')}
    del _L0_attn_all

    def _L0_xattn_setup():
        import jax, jax.numpy as jnp
        import numpy as np
        N_HEADS = 16
        HEAD_DIM = 64
        EMB = 256
        B, S = (2, 512)
        key = jax.random.key(seed)
        ks = jax.random.split(key, 8)
        inner = N_HEADS * HEAD_DIM
        return {'query': jax.random.normal(ks[0], (B, S, EMB), dtype=jnp.float32), 'key': jax.random.normal(ks[1], (B, S, EMB), dtype=jnp.float32), 'value': jax.random.normal(ks[2], (B, S, EMB), dtype=jnp.float32), 'positional_mask': jnp.ones((B, S), dtype=bool), 'future_mask': 1, 'Wq': jax.random.normal(ks[3], (inner, EMB), dtype=jnp.float32) * 0.02, 'Wk': jax.random.normal(ks[4], (inner, EMB), dtype=jnp.float32) * 0.02, 'Wv': jax.random.normal(ks[5], (inner, EMB), dtype=jnp.float32) * 0.02, 'Wo': jax.random.normal(ks[6], (EMB, inner), dtype=jnp.float32) * 0.02, 'bo': jax.random.normal(ks[7], (EMB,), dtype=jnp.float32) * 0.02}
    _L0_xattn_all = _L0_xattn_setup()
    _L0_xattn_in = {k: v for k, v in _L0_xattn_all.items() if k in ('Wq', 'Wk', 'Wv', 'Wo', 'bo')}
    del _L0_xattn_all

    def _L0_ffn_setup():
        import jax, jax.numpy as jnp
        import numpy as np
        H_DIM, E_DIM = (256, 128)
        N_SHARED, N_ROUTED, TOP_K = (2, 16, 4)
        B, S = (4, 512)
        key = jax.random.key(seed)
        ks = jax.random.split(key, 6)
        sc = 1.0 / np.sqrt(H_DIM)
        ec = 1.0 / np.sqrt(E_DIM)
        return {'x': jax.random.normal(ks[0], (B, S, H_DIM), dtype=jnp.float32), 'shared_up': jax.random.uniform(ks[1], (N_SHARED, E_DIM, H_DIM), jnp.float32, -sc, sc), 'shared_down': jax.random.uniform(ks[2], (N_SHARED, H_DIM, E_DIM), jnp.float32, -ec, ec), 'routed_up': jax.random.uniform(ks[3], (N_ROUTED, E_DIM, H_DIM), jnp.float32, -sc, sc), 'routed_down': jax.random.uniform(ks[4], (N_ROUTED, H_DIM, E_DIM), jnp.float32, -ec, ec), 'router_w': jax.random.uniform(ks[5], (N_ROUTED, H_DIM), jnp.float32, -sc, sc)}
    _L0_ffn_all = _L0_ffn_setup()
    _L0_ffn_in = {k: v for k, v in _L0_ffn_all.items() if k in ('shared_up', 'shared_down', 'routed_up', 'routed_down', 'router_w')}
    del _L0_ffn_all

    def _L1_attn_setup():
        import jax, jax.numpy as jnp
        import numpy as np
        from jax import lax
        D_MODEL, D_STATE, D_CONV, EXPAND, HEADDIM = (256, 128, 4, 2, 64)
        D_INNER = EXPAND * D_MODEL
        NHEADS = D_INNER // HEADDIM
        CONV_DIM = D_INNER + 2 * D_STATE
        D_IN_PROJ = 2 * D_INNER + 2 * D_STATE + NHEADS

        def _mamba2(x, in_proj_w, conv_w, conv_b, dt_bias, A_log, D, norm_w, out_proj_w):
            b, l, _ = x.shape
            zxbcdt = x @ in_proj_w.T
            z = zxbcdt[..., :D_INNER]
            xBC = zxbcdt[..., D_INNER:D_INNER + CONV_DIM]
            dt = zxbcdt[..., D_INNER + CONV_DIM:]
            xBC_pad = jnp.pad(xBC, ((0, 0), (D_CONV - 1, 0), (0, 0)))
            windows = jnp.stack([xBC_pad[:, k:k + l, :] for k in range(D_CONV)], axis=-1)
            xBC = jax.nn.silu(jnp.einsum('blck,ck->blc', windows, conv_w) + conv_b)
            xs = xBC[..., :D_INNER]
            B = xBC[..., D_INNER:D_INNER + D_STATE]
            C = xBC[..., D_INNER + D_STATE:]
            xh = xs.reshape(b, l, NHEADS, HEADDIM)
            dt = jax.nn.softplus(dt + dt_bias)
            A = -jnp.exp(A_log)
            dA = jnp.exp(dt * A)
            xdt = xh * dt[..., None]

            def step(S, inp):
                dA_t, xdt_t, B_t, C_t = inp
                S = dA_t[:, :, None, None] * S + xdt_t[..., None] * B_t[:, None, None, :]
                y_t = jnp.einsum('bhpn,bn->bhp', S, C_t)
                return (S, y_t)
            S0 = jnp.zeros((b, NHEADS, HEADDIM, D_STATE), x.dtype)
            _, y = lax.scan(step, S0, (dA.transpose(1, 0, 2), xdt.transpose(1, 0, 2, 3), B.transpose(1, 0, 2), C.transpose(1, 0, 2)))
            y = y.transpose(1, 0, 2, 3) + D[None, None, :, None] * xh
            y = y.reshape(b, l, D_INNER)
            y = y * jax.nn.silu(z)
            y = y * lax.rsqrt(jnp.mean(y * y, axis=-1, keepdims=True) + 1e-05) * norm_w
            return y @ out_proj_w.T
        key = jax.random.key(seed)
        ks = jax.random.split(key, 9)
        b, l = (2, 512)
        x = jax.random.normal(ks[0], (b, l, D_MODEL), jnp.float32)
        in_proj_w = jax.random.normal(ks[1], (D_IN_PROJ, D_MODEL), jnp.float32) * 0.02
        conv_w = jax.random.normal(ks[2], (CONV_DIM, D_CONV), jnp.float32) * 0.2
        conv_b = jax.random.normal(ks[3], (CONV_DIM,), jnp.float32) * 0.02
        dt_bias = jnp.log(jnp.expm1(jax.random.uniform(ks[4], (NHEADS,), jnp.float32, 0.001, 0.1)))
        A_log = jnp.log(jax.random.uniform(ks[5], (NHEADS,), jnp.float32, 1.0, 16.0))
        D = jax.random.normal(ks[6], (NHEADS,), jnp.float32)
        norm_w = jnp.ones((D_INNER,), jnp.float32)
        out_proj_w = jax.random.normal(ks[7], (D_MODEL, D_INNER), jnp.float32) * 0.02
        return {'x': x, 'in_proj_w': in_proj_w, 'conv_w': conv_w, 'conv_b': conv_b, 'dt_bias': dt_bias, 'A_log': A_log, 'D': D, 'norm_w': norm_w, 'out_proj_w': out_proj_w}
    _L1_attn_all = _L1_attn_setup()
    _L1_attn_in = {k: v for k, v in _L1_attn_all.items() if k in ('in_proj_w', 'conv_w', 'conv_b', 'dt_bias', 'A_log', 'D', 'norm_w', 'out_proj_w')}
    del _L1_attn_all

    def _L1_xattn_setup():
        import jax, jax.numpy as jnp
        import numpy as np
        B, S, H, NH = (2, 512, 256, 4)
        DH = H // NH
        EPS_BACKEND = 1e-06
        EPS_LN = 1e-06

        def _mlstm_parallel_stabilized(q, k, v, igate_preact, fgate_preact):
            b, nh, s, dh = q.shape
            log_fg = jax.nn.log_sigmoid(fgate_preact)
            cs = jnp.concatenate([jnp.zeros((b, nh, 1), q.dtype), jnp.cumsum(log_fg[..., 0], axis=2)], axis=2)
            fg_matrix = cs[:, :, :, None] - cs[:, :, None, :]
            fg_matrix = fg_matrix[:, :, 1:, 1:]
            causal = jnp.tril(jnp.ones((s, s), dtype=bool))
            log_fg_matrix = jnp.where(causal, fg_matrix, -jnp.inf)
            log_D = log_fg_matrix + jnp.swapaxes(igate_preact, -2, -1)
            max_log_D = jnp.max(log_D, axis=-1, keepdims=True)
            D = jnp.exp(log_D - max_log_D)
            qk = jnp.einsum('bhsd,bhtd->bhst', q, k) / jnp.sqrt(jnp.asarray(dh, q.dtype))
            C = qk * D
            normalizer = jnp.maximum(jnp.abs(jnp.sum(C, axis=-1, keepdims=True)), jnp.exp(-max_log_D))
            C_norm = C / (normalizer + EPS_BACKEND)
            return jnp.einsum('bhst,bhtd->bhsd', C_norm, v)

        def _multihead_layernorm(x, scale):
            mean = jnp.mean(x, axis=-1, keepdims=True)
            var = jnp.var(x, axis=-1, keepdims=True)
            xn = (x - mean) * jax.lax.rsqrt(var + EPS_LN)
            return xn * scale.reshape(NH, 1, DH)
        key = jax.random.key(seed)
        kq, kk, kv, kib = jax.random.split(key, 4)
        q = jax.random.normal(kq, (B, S, H), dtype=jnp.float32)
        k = jax.random.normal(kk, (B, S, H), dtype=jnp.float32)
        v = jax.random.normal(kv, (B, S, H), dtype=jnp.float32)
        igate_kernel = jnp.zeros((3 * H, NH), dtype=jnp.float32)
        igate_bias = 0.1 * jax.random.normal(kib, (NH,), dtype=jnp.float32)
        fgate_kernel = jnp.zeros((3 * H, NH), dtype=jnp.float32)
        fgate_bias = jnp.linspace(3.0, 6.0, NH, dtype=jnp.float32)
        outnorm_scale = jnp.ones((H,), dtype=jnp.float32)
        return {'q': q, 'k': k, 'v': v, 'igate_kernel': igate_kernel, 'igate_bias': igate_bias, 'fgate_kernel': fgate_kernel, 'fgate_bias': fgate_bias, 'outnorm_scale': outnorm_scale}
    _L1_xattn_all = _L1_xattn_setup()
    _L1_xattn_in = {k: v for k, v in _L1_xattn_all.items() if k in ('igate_kernel', 'igate_bias', 'fgate_kernel', 'fgate_bias', 'outnorm_scale')}
    del _L1_xattn_all

    def _L1_ffn_setup():
        import jax, jax.numpy as jnp
        import numpy as np

        def _binarize(w):
            alpha = jax.lax.stop_gradient(jnp.mean(jnp.abs(w), axis=1, keepdims=True))
            bw = alpha * jnp.sign(w)
            return w + jax.lax.stop_gradient(bw - w)
        key = jax.random.key(seed)
        k1, k2, k3, k4, k5 = jax.random.split(key, 5)
        D, H = (256, 1024)
        x = jax.random.normal(k1, (64, 196, D), dtype=jnp.float32)
        w1 = jax.random.normal(k2, (H, D), dtype=jnp.float32) * 0.02
        b1 = jax.random.normal(k3, (H,), dtype=jnp.float32) * 0.02
        w2 = jax.random.normal(k4, (D, H), dtype=jnp.float32) * 0.02
        b2 = jax.random.normal(k5, (D,), dtype=jnp.float32) * 0.02
        return {'x': x, 'w1': w1, 'b1': b1, 'w2': w2, 'b2': b2}
    _L1_ffn_all = _L1_ffn_setup()
    _L1_ffn_in = {k: v for k, v in _L1_ffn_all.items() if k in ('w1', 'b1', 'w2', 'b2')}
    del _L1_ffn_all
    return {'x': x, 'ctx_1024': ctx_1024, 'mask_BxS2_bf1': mask_BxS2_bf1, 'L0_attn_time_decay': _L0_attn_in['time_decay'], 'L0_attn_time_mix_k': _L0_attn_in['time_mix_k'], 'L0_attn_time_mix_v': _L0_attn_in['time_mix_v'], 'L0_attn_time_mix_r': _L0_attn_in['time_mix_r'], 'L0_attn_time_mix_g': _L0_attn_in['time_mix_g'], 'L0_attn_W_r': _L0_attn_in['W_r'], 'L0_attn_W_k': _L0_attn_in['W_k'], 'L0_attn_W_v': _L0_attn_in['W_v'], 'L0_attn_W_g': _L0_attn_in['W_g'], 'L0_attn_W_o': _L0_attn_in['W_o'], 'L0_attn_ln_gamma': _L0_attn_in['ln_gamma'], 'L0_attn_ln_beta': _L0_attn_in['ln_beta'], 'L0_xattn_Wq': _L0_xattn_in['Wq'], 'L0_xattn_Wk': _L0_xattn_in['Wk'], 'L0_xattn_Wv': _L0_xattn_in['Wv'], 'L0_xattn_Wo': _L0_xattn_in['Wo'], 'L0_xattn_bo': _L0_xattn_in['bo'], 'L0_ffn_shared_up': _L0_ffn_in['shared_up'], 'L0_ffn_shared_down': _L0_ffn_in['shared_down'], 'L0_ffn_routed_up': _L0_ffn_in['routed_up'], 'L0_ffn_routed_down': _L0_ffn_in['routed_down'], 'L0_ffn_router_w': _L0_ffn_in['router_w'], 'L1_attn_in_proj_w': _L1_attn_in['in_proj_w'], 'L1_attn_conv_w': _L1_attn_in['conv_w'], 'L1_attn_conv_b': _L1_attn_in['conv_b'], 'L1_attn_dt_bias': _L1_attn_in['dt_bias'], 'L1_attn_A_log': _L1_attn_in['A_log'], 'L1_attn_D': _L1_attn_in['D'], 'L1_attn_norm_w': _L1_attn_in['norm_w'], 'L1_attn_out_proj_w': _L1_attn_in['out_proj_w'], 'L1_xattn_igate_kernel': _L1_xattn_in['igate_kernel'], 'L1_xattn_igate_bias': _L1_xattn_in['igate_bias'], 'L1_xattn_fgate_kernel': _L1_xattn_in['fgate_kernel'], 'L1_xattn_fgate_bias': _L1_xattn_in['fgate_bias'], 'L1_xattn_outnorm_scale': _L1_xattn_in['outnorm_scale'], 'L1_ffn_w1': _L1_ffn_in['w1'], 'L1_ffn_b1': _L1_ffn_in['b1'], 'L1_ffn_w2': _L1_ffn_in['w2'], 'L1_ffn_b2': _L1_ffn_in['b2']}

def reference(x, ctx_1024, mask_BxS2_bf1, L0_attn_time_decay, L0_attn_time_mix_k, L0_attn_time_mix_v, L0_attn_time_mix_r, L0_attn_time_mix_g, L0_attn_W_r, L0_attn_W_k, L0_attn_W_v, L0_attn_W_g, L0_attn_W_o, L0_attn_ln_gamma, L0_attn_ln_beta, L0_xattn_Wq, L0_xattn_Wk, L0_xattn_Wv, L0_xattn_Wo, L0_xattn_bo, L0_ffn_shared_up, L0_ffn_shared_down, L0_ffn_routed_up, L0_ffn_routed_down, L0_ffn_router_w, L1_attn_in_proj_w, L1_attn_conv_w, L1_attn_conv_b, L1_attn_dt_bias, L1_attn_A_log, L1_attn_D, L1_attn_norm_w, L1_attn_out_proj_w, L1_xattn_igate_kernel, L1_xattn_igate_bias, L1_xattn_fgate_kernel, L1_xattn_fgate_bias, L1_xattn_outnorm_scale, L1_ffn_w1, L1_ffn_b1, L1_ffn_w2, L1_ffn_b2):
    import jax
    import jax.numpy as jnp

    def _L0_attn_ref(x, time_decay, time_mix_k, time_mix_v, time_mix_r, time_mix_g, W_r, W_k, W_v, W_g, W_o, ln_gamma, ln_beta):
        import jax, jax.numpy as jnp
        import numpy as np
        B, T, C = (4, 512, 256)
        H = 16
        D = C // H
        EPS = 1e-05

        def _rwkv_scan(r, k, v, w):
            b, t, c = r.shape
            wh = w.reshape(H, D)

            def split(u):
                return u.reshape(b, t, H, D).transpose(1, 0, 2, 3)
            rT, kT, vT = (split(r), split(k), split(v))

            def step(state, inp):
                kt, vt, rt = inp
                state = state * wh[None, :, :, None] + kt[..., :, None] * vt[..., None, :]
                out = jnp.einsum('bhij,bhj->bhi', state, rt)
                return (state, out)
            state0 = jnp.zeros((b, H, D, D), r.dtype)
            _, outs = jax.lax.scan(step, state0, (kT, vT, rT))
            return outs.transpose(1, 0, 2, 3).reshape(b, t, c)
        xx = jnp.concatenate([x[:, 1:2, :], x[:, :-1, :]], axis=1) - x
        xk = x + xx * time_mix_k
        xv = x + xx * time_mix_v
        xr = x + xx * time_mix_r
        xg = x + xx * time_mix_g
        r = xr @ W_r.T
        k = xk @ W_k.T
        v = xv @ W_v.T
        g = jax.nn.sigmoid(xg @ W_g.T)
        w = jnp.exp(-jnp.exp(time_decay))
        attn = _rwkv_scan(r, k, v, w)
        y = attn * g @ W_o.T
        mu = jnp.mean(y, axis=-1, keepdims=True)
        var = jnp.mean(jnp.square(y - mu), axis=-1, keepdims=True)
        return (y - mu) / jnp.sqrt(var + EPS) * ln_gamma + ln_beta

    def _L0_xattn_ref(query, key, value, positional_mask, future_mask, Wq, Wk, Wv, Wo, bo):
        import jax, jax.numpy as jnp
        import numpy as np
        N_HEADS = 16
        HEAD_DIM = 64
        EMB = 256
        B, S = (2, 512)
        batch, seq = query.shape[:2]
        q = (query @ Wq.T).reshape(batch, seq, N_HEADS, HEAD_DIM)
        k = (key @ Wk.T).reshape(batch, seq, N_HEADS, HEAD_DIM)
        v = (value @ Wv.T).reshape(batch, seq, N_HEADS, HEAD_DIM)
        scale = 1.0 / np.sqrt(HEAD_DIM).astype(np.float32)
        weights = jnp.einsum('bqhd,bkhd->bhqk', q, k) * scale
        neg_inf = jnp.float32(-jnp.inf)
        reweight = jnp.where(positional_mask, jnp.float32(0.0), neg_inf)
        weights = weights + reweight[:, None, None, :]
        if future_mask:
            causal = jnp.triu(jnp.full((seq, seq), neg_inf, dtype=weights.dtype), k=1)
            weights = weights + causal
        weights = jax.nn.softmax(weights, axis=-1)
        out = jnp.einsum('bhqk,bkhd->bqhd', weights, v).reshape(batch, seq, -1)
        return out @ Wo.T + bo

    def _L0_ffn_ref(x, shared_up, shared_down, routed_up, routed_down, router_w):
        import jax, jax.numpy as jnp
        import numpy as np
        H_DIM, E_DIM = (256, 128)
        N_SHARED, N_ROUTED, TOP_K = (2, 16, 4)
        B, S = (4, 512)
        b, s, h = x.shape
        xt = x.reshape(-1, h)
        up_s = jnp.einsum('th,seh->tse', xt, shared_up)
        shared = jnp.einsum('tse,she->th', jax.nn.gelu(up_s, approximate=False), shared_down)
        probs = jax.nn.softmax(xt @ router_w.T, axis=-1)
        topk_p, topk_i = jax.lax.top_k(probs, TOP_K)
        gate = jnp.zeros_like(probs).at[jnp.arange(xt.shape[0])[:, None], topk_i].add(topk_p)
        up_r = jnp.einsum('th,reh->tre', xt, routed_up)
        act = jax.nn.gelu(up_r, approximate=False) * gate[:, :, None]
        routed = jnp.einsum('tre,rhe->th', act, routed_down)
        return (shared + routed).reshape(b, s, h)

    def _L1_attn_ref(x, in_proj_w, conv_w, conv_b, dt_bias, A_log, D, norm_w, out_proj_w):
        import jax, jax.numpy as jnp
        import numpy as np
        from jax import lax
        D_MODEL, D_STATE, D_CONV, EXPAND, HEADDIM = (256, 128, 4, 2, 64)
        D_INNER = EXPAND * D_MODEL
        NHEADS = D_INNER // HEADDIM
        CONV_DIM = D_INNER + 2 * D_STATE
        D_IN_PROJ = 2 * D_INNER + 2 * D_STATE + NHEADS

        def _mamba2(x, in_proj_w, conv_w, conv_b, dt_bias, A_log, D, norm_w, out_proj_w):
            b, l, _ = x.shape
            zxbcdt = x @ in_proj_w.T
            z = zxbcdt[..., :D_INNER]
            xBC = zxbcdt[..., D_INNER:D_INNER + CONV_DIM]
            dt = zxbcdt[..., D_INNER + CONV_DIM:]
            xBC_pad = jnp.pad(xBC, ((0, 0), (D_CONV - 1, 0), (0, 0)))
            windows = jnp.stack([xBC_pad[:, k:k + l, :] for k in range(D_CONV)], axis=-1)
            xBC = jax.nn.silu(jnp.einsum('blck,ck->blc', windows, conv_w) + conv_b)
            xs = xBC[..., :D_INNER]
            B = xBC[..., D_INNER:D_INNER + D_STATE]
            C = xBC[..., D_INNER + D_STATE:]
            xh = xs.reshape(b, l, NHEADS, HEADDIM)
            dt = jax.nn.softplus(dt + dt_bias)
            A = -jnp.exp(A_log)
            dA = jnp.exp(dt * A)
            xdt = xh * dt[..., None]

            def step(S, inp):
                dA_t, xdt_t, B_t, C_t = inp
                S = dA_t[:, :, None, None] * S + xdt_t[..., None] * B_t[:, None, None, :]
                y_t = jnp.einsum('bhpn,bn->bhp', S, C_t)
                return (S, y_t)
            S0 = jnp.zeros((b, NHEADS, HEADDIM, D_STATE), x.dtype)
            _, y = lax.scan(step, S0, (dA.transpose(1, 0, 2), xdt.transpose(1, 0, 2, 3), B.transpose(1, 0, 2), C.transpose(1, 0, 2)))
            y = y.transpose(1, 0, 2, 3) + D[None, None, :, None] * xh
            y = y.reshape(b, l, D_INNER)
            y = y * jax.nn.silu(z)
            y = y * lax.rsqrt(jnp.mean(y * y, axis=-1, keepdims=True) + 1e-05) * norm_w
            return y @ out_proj_w.T
        return x + _mamba2(x, in_proj_w, conv_w, conv_b, dt_bias, A_log, D, norm_w, out_proj_w)

    def _L1_xattn_ref(q, k, v, igate_kernel, igate_bias, fgate_kernel, fgate_bias, outnorm_scale):
        import jax, jax.numpy as jnp
        import numpy as np
        B, S, H, NH = (2, 512, 256, 4)
        DH = H // NH
        EPS_BACKEND = 1e-06
        EPS_LN = 1e-06

        def _mlstm_parallel_stabilized(q, k, v, igate_preact, fgate_preact):
            b, nh, s, dh = q.shape
            log_fg = jax.nn.log_sigmoid(fgate_preact)
            cs = jnp.concatenate([jnp.zeros((b, nh, 1), q.dtype), jnp.cumsum(log_fg[..., 0], axis=2)], axis=2)
            fg_matrix = cs[:, :, :, None] - cs[:, :, None, :]
            fg_matrix = fg_matrix[:, :, 1:, 1:]
            causal = jnp.tril(jnp.ones((s, s), dtype=bool))
            log_fg_matrix = jnp.where(causal, fg_matrix, -jnp.inf)
            log_D = log_fg_matrix + jnp.swapaxes(igate_preact, -2, -1)
            max_log_D = jnp.max(log_D, axis=-1, keepdims=True)
            D = jnp.exp(log_D - max_log_D)
            qk = jnp.einsum('bhsd,bhtd->bhst', q, k) / jnp.sqrt(jnp.asarray(dh, q.dtype))
            C = qk * D
            normalizer = jnp.maximum(jnp.abs(jnp.sum(C, axis=-1, keepdims=True)), jnp.exp(-max_log_D))
            C_norm = C / (normalizer + EPS_BACKEND)
            return jnp.einsum('bhst,bhtd->bhsd', C_norm, v)

        def _multihead_layernorm(x, scale):
            mean = jnp.mean(x, axis=-1, keepdims=True)
            var = jnp.var(x, axis=-1, keepdims=True)
            xn = (x - mean) * jax.lax.rsqrt(var + EPS_LN)
            return xn * scale.reshape(NH, 1, DH)
        b, s, h = q.shape
        gate_in = jnp.concatenate([q, k, v], axis=-1)
        ig = gate_in @ igate_kernel + igate_bias
        fg = gate_in @ fgate_kernel + fgate_bias
        ig = jnp.transpose(ig, (0, 2, 1))[..., None]
        fg = jnp.transpose(fg, (0, 2, 1))[..., None]
        qh = jnp.transpose(q.reshape(b, s, NH, DH), (0, 2, 1, 3))
        kh = jnp.transpose(k.reshape(b, s, NH, DH), (0, 2, 1, 3))
        vh = jnp.transpose(v.reshape(b, s, NH, DH), (0, 2, 1, 3))
        hs = _mlstm_parallel_stabilized(qh, kh, vh, ig, fg)
        hn = _multihead_layernorm(hs, outnorm_scale)
        return jnp.transpose(hn, (0, 2, 1, 3)).reshape(b, s, h)

    def _L1_ffn_ref(x, w1, b1, w2, b2):
        import jax, jax.numpy as jnp
        import numpy as np

        def _binarize(w):
            alpha = jax.lax.stop_gradient(jnp.mean(jnp.abs(w), axis=1, keepdims=True))
            bw = alpha * jnp.sign(w)
            return w + jax.lax.stop_gradient(bw - w)
        bw1 = _binarize(w1)
        h = jnp.einsum('bsd,hd->bsh', x, bw1) + b1
        h = jax.nn.gelu(h, approximate=False)
        bw2 = _binarize(w2)
        out = jnp.einsum('bsh,dh->bsd', h, bw2) + b2
        return out
    x = _layernorm(x + _L0_attn_ref(x, L0_attn_time_decay, L0_attn_time_mix_k, L0_attn_time_mix_v, L0_attn_time_mix_r, L0_attn_time_mix_g, L0_attn_W_r, L0_attn_W_k, L0_attn_W_v, L0_attn_W_g, L0_attn_W_o, L0_attn_ln_gamma, L0_attn_ln_beta), axis=-1)
    x = _layernorm(x + _L0_xattn_ref(x, ctx_1024, ctx_1024, mask_BxS2_bf1, 1, L0_xattn_Wq, L0_xattn_Wk, L0_xattn_Wv, L0_xattn_Wo, L0_xattn_bo), axis=-1)
    x = _layernorm(x + _L0_ffn_ref(x, L0_ffn_shared_up, L0_ffn_shared_down, L0_ffn_routed_up, L0_ffn_routed_down, L0_ffn_router_w), axis=-1)
    x = _layernorm(x + _L1_attn_ref(x, L1_attn_in_proj_w, L1_attn_conv_w, L1_attn_conv_b, L1_attn_dt_bias, L1_attn_A_log, L1_attn_D, L1_attn_norm_w, L1_attn_out_proj_w), axis=-1)
    x = _layernorm(x + _L1_xattn_ref(x, ctx_1024, ctx_1024, L1_xattn_igate_kernel, L1_xattn_igate_bias, L1_xattn_fgate_kernel, L1_xattn_fgate_bias, L1_xattn_outnorm_scale), axis=-1)
    x = _layernorm(x + _L1_ffn_ref(x, L1_ffn_w1, L1_ffn_b1, L1_ffn_w2, L1_ffn_b2), axis=-1)
    return x

_drawn_inputs = setup_inputs


def setup_inputs(seed=0):
    import zlib

    import numpy as np

    out = dict(_drawn_inputs(seed))
    spreads = {'L0_attn_ln_gamma': (1.0, 0.2),
     'L0_attn_ln_beta': (0.0, 0.1),
     'L1_attn_norm_w': (1.0, 0.2),
     'L1_xattn_igate_kernel': (0.0, 0.1),
     'L1_xattn_fgate_kernel': (0.0, 0.1),
     'L1_xattn_outnorm_scale': (1.0, 0.2)}
    factors = {'L0_attn_time_decay': 3.133,
     'L0_xattn_Wq': 5.515,
     'L0_xattn_Wk': 6.074,
     'L1_attn_dt_bias': 8.0,
     'L1_attn_A_log': 8.0,
     'L1_xattn_igate_bias': 8.0,
     'L1_ffn_b1': 8.0,
     'L1_ffn_b2': 2.923}
    for name, (base, spread) in spreads.items():
        noise = np.random.default_rng([zlib.crc32(name.encode()), seed]).standard_normal(out[name].shape)
        drawn = base * np.exp(spread * noise) if base else spread * noise
        out[name] = jnp.asarray(drawn.astype(out[name].dtype))
    for name, factor in factors.items():
        out[name] = (out[name] * factor).astype(out[name].dtype)
    return out
```

```python
from contextlib import ExitStack

import concourse.bass as bass
from concourse import mybir

ALU = mybir.AluOpType
ACT = mybir.ActivationFunctionType
AXX = mybir.AxisListType.X
F32 = mybir.dt.float32
F16 = mybir.dt.float16
BF16 = mybir.dt.bfloat16
U8 = mybir.dt.uint8
I32 = mybir.dt.int32

P = 128
B, T, C = 8, 256, 256
NS = 2
TURNS = B // NS
TT = T // P
KC = C // P
LN_EPS, ML_EPS, RMS_EPS = 1e-5, 1e-6, 1e-5
RH, RD = 16, 16
AH, AD = 16, 64
INNER = AH * AD
AM = INNER // P
NSH, NR, ED, TOPK = 2, 16, 128, 4
NE = NSH + NR
DI, DS, MH, MD, TAPS = 512, 128, 8, 64, 4
CONV = DI + 2 * DS
CM = CONV // P
DM = DI // P
LH, LD = 4, 64
FH = 1024
FM = FH // P
BIG = 1e30
MID = P // 2
SBLK = 3 * P


class Book:

    def __init__(self, known=None):
        self.total, self.marks, self.banks = {}, {}, {}
        self.known = known


class Lane:

    def __init__(self, nc, eng, who, book, sems, ctx):
        self.nc, self.eng, self.who, self.book, self.sems, self.ctx = nc, eng, who, book, sems, ctx
        self.turn, self.met, self.cur, self.last = None, {}, None, None

    def sem(self, name):
        if name not in self.sems:
            self.sems[name] = self.ctx.enter_context(self.nc.semaphore(name))
        return self.sems[name]

    def stage(self, name):
        self.cur = f"{name}_{self.who}"

    def up(self, mark=None, by=1, sem=None):
        name = sem or self.cur
        n = self.book.total[name] = self.book.total.get(name, 0) + by
        self.last = (name, n, self.turn is not None)
        if mark is not None:
            self.mark(mark)
        return self.sem(name), by

    def mark(self, mark):
        mark = mark if isinstance(mark, tuple) else (mark,)
        assert mark not in self.book.marks, mark
        self.book.marks[mark] = self.last

    def at(self, *mark):
        return self.value(self.book.marks.get(mark) or (
            self.book.known.marks[mark] if self.book.known else ("ready_pool", 1, False)))

    def own(self):
        return self.value(self.last)

    def value(self, place):
        name, n, turned = place
        n = self.met[name] = max(n, self.met.get(name, 0))
        if turned and self.turn is not None:
            total = self.book.known.total.get(name, 1) if self.book.known else 1
            n = self.turn * total + n
        return self.sem(name), n


ENGINES = ("pe", "act", "dve", "pool")


def build(nc, a, out, xmid, book, stop=9):
    known = book.known
    with ExitStack() as ctx:
        sems = {}

        def sb(name, shape, dt=F32):
            return ctx.enter_context(nc.sbuf_tensor(name, shape, dt))

        ps = ctx.enter_context(nc.psum_tensor("ps", [P, 8, 512], F32))

        def bank(mark):
            return (book.banks.get(mark) if mark in book.banks else known.banks[mark] if known else 0)

        ident = sb("ident", [P, P])
        identb = sb("identb", [P, P], BF16)
        onesq = sb("onesq", [P, P])
        le = sb("le", [P, SBLK])
        qneg = sb("qneg", [P, P], BF16)
        sbig = sb("sbig", [P, SBLK], BF16)
        hcol = sb("hcol", [P, 8])
        srow = sb("srow", [8, 8, P])
        pcol = sb("pcol", [P, 4])
        pint = sb("pint", [P, 1], I32)
        eps = sb("eps", [P, 4])
        zrow = sb("zrow", [8, T])
        tick = sb("tick", [1, 2])
        onesb = sb("onesb", [1, P], BF16)
        xT = [sb(f"xT{s}", [P, KC, T]) for s in range(NS)]
        xin = [sb(f"xin{s}", [P, TT, C]) for s in range(NS)]
        cT = [sb(f"cT{s}", [P, KC, T]) for s in range(NS)]
        z = [sb(f"z{s}", [P, TT, C]) for s in range(NS)]
        zT = [sb(f"zT{s}", [P, KC, T]) for s in range(NS)]
        z2 = [sb(f"z2{s}", [P, TT, C]) for s in range(NS)]
        st6 = [sb(f"st6{s}", [P, 8, 6]) for s in range(NS)]
        mv = [sb(f"mv{s}", [P, 8, 2]) for s in range(NS)]
        lnv = [sb(f"lnv{s}", [P, 8]) for s in range(NS)]
        rstd = [sb(f"rstd{s}", [P, 8]) for s in range(NS)]
        ARENA = 2 * AM * T + TT * AH * (AD + 1) + TT * INNER
        arena = [sb(f"arena{s}", [P, ARENA]) for s in range(NS)]
        small = [sb(f"small{s}", [P, 256]) for s in range(NS)]
        WORDS = 21536
        wts = sb("wts", [P, WORDS])


        pq = sb("pq", [P, 12 * SBLK])
        rot = pq[:, 0:8 * T].rearrange("p (h t) -> p h t", h=8)
        nms = sb("nms", [P, 16])
        mb_ = [sb(f"mb{s}", [P, SBLK], BF16) for s in range(NS)]
        mr_ = [sb(f"mr{s}", [1, T], BF16) for s in range(NS)]
        m8_ = [sb(f"m8{s}", [1, T], U8) for s in range(NS)]

        def mbias(s):
            return mb_[s][:, :]

        def mrowb(s):
            return mr_[s][:, :]

        def m8(s):
            return m8_[s][:, :]

        def nmax(n):
            return nms[:, 2 * (n % 8):2 * (n % 8) + 2]

        def pbuf(n):
            return pq[:, (n % 6) * SBLK:(n % 6 + 1) * SBLK]

        def ptbuf(n):
            return pq[:, (6 + n % 6) * SBLK:(7 + n % 6) * SBLK]

        def atb(h):
            return pq[:, (6 + h % 4) * SBLK:(7 + h % 4) * SBLK]

        def abuf(s, e):
            i = s * 2 + e // 2 % 2
            return pq[:, i * 2 * T:(i + 1) * 2 * T].rearrange("p (j t) -> p j t", j=2)

        def flat(x):
            return x.rearrange("p a b -> p (a b)") if len(x.shape) == 3 else x

        def diag(x, at=0):
            return x[:, at:at + 2 * T].rearrange("p (a b) -> p a b", b=T)[:, :, 0:P]

        def dyn(ap, b):
            return ap[bass.ds(b, 1)].rearrange("a p q r -> (a p) q r") if len(ap.shape) == 4 else ap[bass.ds(b, 1)]

        def carve_r(s):
            return carve(arena[s], [(KC, T)] * 7 + [(TT, C), (C,), (TT, C), (TT, C), (KC, T)])

        def carve_m(s):
            return carve(arena[s], [(CM, T + TAPS - 1), (CM, T), (TT, DI), (TT, DI), (TT, DI), (TT, DI), (DM, T)])[0]

        def ebuf(n):
            i = n % 6
            return pq[:, i * 2 * SBLK:(i + 1) * 2 * SBLK]

        def hTb(s):
            n = CM * (T + TAPS - 1)
            return arena[s][:, n:n + FM * T].rearrange("p (m t) -> p m t", m=FM)

        def sm(s, i, n=16):
            return small[s][:, 16 * i:16 * i + n]

        def th(x, n):
            return x.rearrange("p (t h) -> p t h", t=TT)

        def carve_a(s):
            (q, k, o, v), n = carve(arena[s], [(AM, T), (AM, T), (TT, INNER), (TT * AH * (AD + 1),)])
            return (q, k, v, o), n

        def carve(base, sizes):
            at, got = 0, []
            for shape in sizes:
                n = 1
                for d in shape:
                    n *= d
                v = base[:, at:at + n]
                if len(shape) == 2:
                    v = v.rearrange("p (a b) -> p a b", a=shape[0])
                if len(shape) == 3:
                    v = v.rearrange("p (a b c) -> p a b c", a=shape[0], b=shape[1])
                got.append(v)
                at += n
            return got, at

        (wr, wk, wv, wg, wo, wq, wkk, wvv, woo, up, down, rw, gam, bet, bo_, t1, t2, to_), n0 = carve(wts, [
            (KC, C)] * 5 + [(KC, INNER)] * 3 + [(AM, C), (NE * KC, ED), (NE, C), (KC, NR),
            (C,), (C,), (C,), (C,), (C,), (C,)])
        assert n0 <= WORDS, n0
        mix = sb("mix", [P, 4, KC])
        (win, wout, ck, cb, w1T, w2T, Arow, dtb, drow, nw, gk, gb, onorm, b1, al1, al2, al2r, b2r, spare1, tmpw), n1 = carve(wts, [
            (KC, 2 * DI + 2 * DS + MH), (DM, C), (CM, TAPS), (CM,), (KC, FH), (FM, C), (MH,), (MH,), (DI,),
            (DM,), (3 * KC, 2 * LH), (2 * LH,), (C,), (FM,), (FM,), (KC,), (C,), (C,), (2,), (2, FM, C)])
        ((cbm0, cbm1, ct0, ct1, v10, v11, dx0, dx1), n2) = carve(wts[:, n1:], [
            (SBLK,)] * 2 + [(T,)] * 2 + [(TT * LH * (LD + 1),)] * 2 + [(TT, DI)] * 2)
        assert n1 + n2 <= WORDS, (n1, n2)
        cbm, csT, v1, dxs = (cbm0, cbm1), (ct0, ct1), (v10, v11), (dx0, dx1)

        block = ctx.enter_context(nc.Block())

        def lane(eng, who):
            return Lane(nc, eng, who, book, sems, ctx)

        def gate(ln, phase):
            ln.met = {}
            count = ln.turn + 1
            for e in ENGINES:
                ln.eng.wait_ge(ln.sem(f"turned{phase}_{e}"), count)

        def loaded(ln, phase):
            ln.eng.wait_ge(ln.sem(f"turned{phase}_sp"), 1)

        def done(ln, phase):
            ln.eng.drain().then_inc(ln.sem(f"turned{phase}_{ln.who}"), 1)

        @block.tensor
        def _(eng):
            pe = lane(eng, "pe")
            mm = nc.tensor.matmul
            pending = {}
            spin, NB = [0], [6]

            def take(mark, drained, b=None):
                if b is None:
                    b = spin[0] % NB[0]
                    spin[0] += 1
                book.banks[mark] = b
                if b in pending:
                    for mark in pending[b]:
                        eng.wait_ge(*pe.at(*mark))
                pending[b] = drained if isinstance(drained, list) else [drained]
                return ps[:, b, :]

            def group(out_, pairs):
                for n, (l, r) in enumerate(pairs):
                    ins = mm(out_, l, r, start=(n == 0), stop=(n == len(pairs) - 1))
                return ins

            def transposes(s, key, src, srcmark):
                eng.wait_ge(*pe.at(*srcmark))
                o = take((key, s), (key, s, "out"))
                for k in range(KC):
                    for t in range(TT):
                        ins = nc.tensor.transpose(o[:, k * T + t * P:k * T + t * P + P],
                                                  src[:, t, k * P:k * P + P], ident[:, :])
                ins.then_inc(*pe.up((key, s)))

            def colproj(s, key, w, src, srcmark, m0, m1):
                for mark in srcmark:
                    eng.wait_ge(*pe.at(*mark))
                for m in range(m0, m1, 2):
                    o = take((key, s, m), (key, s, m, "out"))
                    for j in range(2):
                        ins = group(o[:, j * T:j * T + T],
                                    [(w[:, k, (m + j) * P:(m + j) * P + P], src[:, k, :]) for k in range(KC)])
                    ins.then_inc(*pe.up((key, s, m)))

            def rowproj(s, key, w, src, srcmark, b=None, kc=KC):
                for mark in srcmark:
                    eng.wait_ge(*pe.at(*mark))
                o = take((key, s), (key, s, "out"), b)
                for t in range(TT):
                    ins = group(o[:, t * C:t * C + C],
                                [(src[:, k, t * P:t * P + P], w[:, k, :]) for k in range(kc)])
                ins.then_inc(*pe.up((key, s)))

            def rwkv_proj(s):
                (xx, xr, xk, xv, xg, rT, vT, *_), _ = carve_r(s)
                colproj(s, "rT", wr, xr, [("mix_r", s)], 0, 2)
                colproj(s, "vT", wv, xv, [("mix_v", s)], 0, 2)
                rowproj(s, "k", wk, xk, [("mix_k", s)])
                rowproj(s, "g", wg, xg, [("mix_g", s)])

            def rwkv_scores(s, h):
                rT = carve_r(s)[0][5]
                eng.wait_ge(*pe.at("rT", s, 0, "out"))
                eng.wait_ge(*pe.at("vh", s, h))
                o = take(("A", s, h), ("A", s, h, "out2"))
                vh = rot[:, h % 8, :]
                m = h // 8
                mm(o[:, 0:T], vh[:, 0:P], rT[:, m, :], start=True, stop=True)
                ins = mm(o[:, T:T + P], vh[:, P:T], rT[:, m, P:T], start=True, stop=True)
                ins.then_inc(*pe.up(("A", s, h)))

            def rwkv_mix(s, h):
                eng.wait_ge(*pe.at("ks", s))
                eng.wait_ge(*pe.at("A", s, h, "out"))
                eng.wait_ge(*pe.at("A", s, h, "out2"))
                Ks, Kc = carve_r(s)[0][7:9]
                if h == 0:
                    take(("attn", s), ("attn", s, "out"), 6 + s)
                o = ps[:, 6 + s, :]
                at = atb(h)
                c = slice(h * RD, h * RD + RD)
                mm(o[:, h * RD:h * RD + RD], at[:, 0:P], Ks[:, 0, c], start=True, stop=True)
                mm(o[:, C + h * RD:C + h * RD + RD], at[:, P:T], Kc[:, c], start=True, stop=False)
                ins = mm(o[:, C + h * RD:C + h * RD + RD], at[:, T:SBLK], Ks[:, 1, c], start=False, stop=True)
                ins.then_inc(*pe.up(("attn", s) if h == RH - 1 else ("mixed", s, h)))

            def attn_scores(n, s, h):
                QT, KT = carve_a(s)[0][0:2]
                m, r = h // 2, slice(64 * (h % 2), 64 * (h % 2) + 64)
                eng.wait_ge(*pe.at("Q", s, m - m % 2, "out"))
                eng.wait_ge(*pe.at("K", s, m - m % 2, "out"))
                eng.wait_ge(*pe.at("bias", s))
                o = take(("S", s, h), ("E", s, h), n % 4)
                mm(o[:, 0:SBLK], identb[:, :], mbias(s), start=True, stop=False)
                mm(o[:, 0:P], QT[r, m, 0:P], KT[r, m, 0:P], start=False, stop=False)
                ins = mm(o[:, P:SBLK], QT[r, m, P:T], KT[r, m, :], start=False, stop=True)
                ins.then_inc(*pe.up(("S", s, h)))

            def attn_turn(n, s, h):
                eng.wait_ge(*pe.at("E", s, h))
                o = take(("PT", s, h), ("PT", s, h, "out"), 4 + n % 2)
                for j in range(3):
                    ins = nc.tensor.transpose(o[:, j * P:j * P + P], pbuf(n)[:, j * P:j * P + P], ident[:, :])
                ins.then_inc(*pe.up(("PT", s, h)))

            def attn_values(n, s, h):
                V = carve_a(s)[0][2]
                eng.wait_ge(*pe.at("PT", s, h, "out"))
                eng.wait_ge(*pe.at("V", s, "out"))
                if h % 2 == 0:
                    take(("O", s, h // 2), ("O", s, h // 2, "out"), 6 + (n // 2) % 2)
                o = ps[:, 6 + (n // 2) % 2, :]
                c0 = (h % 2) * (AD + 1)
                c1 = 2 * (AD + 1) + c0
                pt = ptbuf(n)
                v0 = V[:, h * (AD + 1):(h + 1) * (AD + 1)]
                v1 = V[:, (AH + h) * (AD + 1):(AH + h + 1) * (AD + 1)]
                mm(o[:, c0:c0 + AD + 1], pt[:, 0:P], v0, start=True, stop=True)
                mm(o[:, c1:c1 + AD + 1], pt[:, P:T], v0, start=True, stop=False)
                ins = mm(o[:, c1:c1 + AD + 1], pt[:, T:SBLK], v1, start=False, stop=True)
                ins.then_inc(*pe.up(("pv", s, h)))
                if h % 2:
                    pe.mark(("O", s, h // 2))

            def val_proj(s):
                eng.wait_ge(*pe.at("cT", s))
                for t in range(TT):
                    for j in range(2):
                        o = take(("Vp", s, t, j), ("Vp", s, t, j, "out"))
                        ins = group(o[:, :], [(cT[s][:, k, t * P:t * P + P], wvv[:, k, j * 512:j * 512 + 512])
                                              for k in range(KC)])
                        ins.then_inc(*pe.up(("Vp", s, t, j)))

            def turn_out(s):
                O = carve_a(s)[0][3]
                eng.wait_ge(*pe.at("O", s, AM - 1, "out"))
                for m in range(0, AM, 2):
                    o = take(("OT", s, m), ("OT", s, m, "out"))
                    for j in range(2):
                        for t in range(TT):
                            ins = nc.tensor.transpose(o[:, j * T + t * P:j * T + t * P + P],
                                                      O[:, t, (m + j) * P:(m + j) * P + P], ident[:, :])
                    ins.then_inc(*pe.up(("OT", s, m)))

            def router(s):
                eng.wait_ge(*pe.at("zT2", s, "out"))
                o = take(("route", s), ("route", s, "out"))
                for t in range(TT):
                    ins = group(o[:, t * NR:t * NR + NR],
                                [(zT[s][:, k, t * P:t * P + P], rw[:, k, :]) for k in range(KC)])
                ins.then_inc(*pe.up(("route", s)))

            def expert_up(s, e):
                o = take(("up", s, e), ("up", s, e, "out"))
                for j in range(2):
                    ins = group(o[:, j * T:j * T + T],
                                [(up[:, (e + j) * KC + k, :], zT[s][:, k, :]) for k in range(KC)])
                ins.then_inc(*pe.up(("up", s, e)))

            def expert_down(s, e):
                eng.wait_ge(*pe.at("up", s, e, "out"))
                act = abuf(s, e)
                for j in range(2):
                    if e + j < NSH:
                        if j == 0:
                            take(("shared", s), ("shared", s, "out"))
                        o = ps[:, bank(("shared", s)), :]
                        for t in range(TT):
                            if j == 0:
                                continue
                            for jj in range(NSH):
                                ins = mm(o[:, t * C:t * C + C], act[:, jj, t * P:t * P + P], down[:, jj, :],
                                         start=(jj == 0), stop=(jj == NSH - 1))
                        if j == NSH - 1:
                            ins.then_inc(*pe.up(("shared", s)))
                        continue
                    o = take(("dn", s, e + j), ("dn", s, e + j, "out"))
                    for t in range(TT):
                        ins = mm(o[:, t * C:t * C + C], act[:, j, t * P:t * P + P], down[:, e + j, :],
                                 start=True, stop=True)
                    ins.then_inc(*pe.up(("dn", s, e + j)))

            UNITS = [(s, 2 * m + e) for m in range(AM) for s in range(NS) for e in range(2)]
            done(pe, 0)
            loaded(pe, 0)
            with eng.Fori(0, TURNS) as g:
                pe.turn = g
                gate(pe, 0)
                pe.stage("rwkv")
                for s in range(NS):
                    rwkv_proj(s)
                for s in range(NS):
                    for h in range(RH + 2):
                        if h < RH:
                            rwkv_scores(s, h)
                        if h >= 2:
                            rwkv_mix(s, h - 2)
                for s in range(NS):
                    agT, ag = carve_r(s)[0][11], carve_r(s)[0][10]
                    transposes(s, "agT", ag, ("ag", s))
                    rowproj(s, "y", wo, agT, [("agT", s, "out")])
                pe.stage("attn")
                for s in range(NS):
                    transposes(s, "zT1", z[s], ("z1", s))
                for s in range(NS):
                    colproj(s, "K", wkk, cT[s], [("cT", s), ("z1", s)], 0, AM)
                    val_proj(s)
                    colproj(s, "Q", wq, zT[s], [("zT1", s, "out")], 0, AM)
                    o = take(("biasp", s), ("bias", s))
                    eng.wait_ge(*pe.at("mrow", s))
                    mm(o[:, 0:P], onesb[:, :], mrowb(s)[:, 0:P], start=True, stop=True)
                    ins = mm(o[:, P:SBLK], onesb[:, :], mrowb(s)[:, :], start=True, stop=True)
                    ins.then_inc(*pe.up(("biasp", s)))
                for n in range(len(UNITS) + 5):
                    if n < len(UNITS):
                        attn_scores(n, *UNITS[n])
                    if 0 <= n - 3 < len(UNITS):
                        attn_turn(n - 3, *UNITS[n - 3])
                    if 0 <= n - 5 < len(UNITS):
                        attn_values(n - 5, *UNITS[n - 5])
                for s in range(NS):
                    turn_out(s)
                    OT = carve_a(s)[0][0]
                    rowproj(s, "xo", woo, OT, [("OT", s, AM - 2, "out")], kc=AM)
                pe.stage("moe")
                for s in range(NS):
                    transposes(s, "zT2", z2[s], ("z2", s))
                    router(s)
                for e in range(0, NE + 2, 2):
                    for s in range(NS):
                        if e < NE:
                            expert_up(s, e)
                        if e >= 2:
                            expert_down(s, e - 2)
                done(pe, 0)
                pe.turn, pe.met = None, {}
                pending.clear()
            if stop <= 3:
                return

            pe.stage("setup1")
            for d in range(2):
                src, dst, rows, colsn = (tmpw[:, 0], w1T, FM, KC) if d == 0 else (tmpw[:, 1], w2T, KC, FM)
                srcv = src if d == 0 else src.rearrange("p m c -> p (m c)").rearrange("p (m c) -> p m c", m=KC)
                eng.wait_ge(*pe.at("signs", d))
                for cc in range(colsn):
                    for r0 in range(0, rows, 4):
                        n_ = min(4, rows - r0)
                        o = take(("wT", d, cc, r0), ("wT", d, cc, r0, "out"))
                        for j in range(n_):
                            ins = nc.tensor.transpose(o[:, j * P:j * P + P], srcv[:, r0 + j, cc * P:cc * P + P],
                                                      ident[:, :])
                        ins.then_inc(*pe.up(("wT", d, cc, r0)))
            eng.wait_ge(*pe.at("al2diag"))
            o = take("al2row", ("al2row_out",))
            for j in range(KC):
                ins = mm(o[:, j * P:j * P + P], onesq[:, :], dxs[0][:, 0, j * P:j * P + P], start=True, stop=True)
            ins.then_inc(*pe.up("al2row"))
            eng.wait_ge(*pe.at("al2row_out"))
            eng.wait_ge(*pe.at("wT", 1, FM - 1, 0, "out"))
            done(pe, 1)
            loaded(pe, 1)
            pending.clear()

            def cumsum(s, key, src, n):
                o = take((key, s), (key, s, "out"))
                mm(o[:, 0:n], le[:, 0:P], src[:, 0, :], start=True, stop=True)
                mm(o[:, n:2 * n], onesq[:, :], src[:, 0, :], start=True, stop=False)
                mm(o[:, n:2 * n], le[:, 0:P], src[:, 1, :], start=False, stop=True).then_inc(*pe.up((key, s)))

            def rows_of(s, key, src, n):
                o = take((key, s), (key, s, "out"))
                for t in range(TT):
                    ins = mm(o[0:n, t * P:t * P + P], src[:, t, :], ident[:, :], start=True, stop=True)
                ins.then_inc(*pe.up((key, s)))

            def mamba_dt(s):
                eng.wait_ge(*pe.at("zTa", s, "out"))
                o = take(("dt", s), ("dt", s, "out"))
                for t in range(TT):
                    ins = group(o[:, t * MH:t * MH + MH],
                                [(zT[s][:, k, t * P:t * P + P], win[:, k, 2 * DI + 2 * DS:]) for k in range(KC)])
                ins.then_inc(*pe.up(("dt", s)))

            def mamba_in(s):
                colproj(s, "xbc", win[:, :, DI:2 * DI + 2 * DS], zT[s], [], 0, CM)
                for t in range(TT):
                    o = take(("zg", s, t), ("zg", s, t, "out"))
                    ins = group(o, [(zT[s][:, k, t * P:t * P + P], win[:, k, 0:DI]) for k in range(KC)])
                    ins.then_inc(*pe.up(("zg", s, t)))

            def mamba_sums(s):
                eng.wait_ge(*pe.at("dA", s))
                cumsum(s, "cs", th(sm(s, 3), MH), MH)
                eng.wait_ge(*pe.at("cs", s, "out"))
                rows_of(s, "csr", th(sm(s, 4), MH), MH)

            def mamba_mid(s):
                xpad, xb = carve_m(s)[0:2]
                eng.wait_ge(*pe.at("conv", s, CM - 1))
                Bt, Ct = xb[:, DM, :], xb[:, DM + 1, :]
                o = take(("CB", s), ("CB", s, "out"))
                mm(o[:, 0:T], Bt[:, 0:P], Ct, start=True, stop=True)
                mm(o[:, T:SBLK], Bt[:, P:T], Ct[:, P:T], start=True, stop=True).then_inc(*pe.up(("CB", s)))
                for t in range(TT):
                    o = take(("xs", s, t), ("xs", s, t, "out"))
                    for m in range(DM):
                        ins = nc.tensor.transpose(o[:, m * P:m * P + P], xb[:, m, t * P:t * P + P], ident[:, :])
                    ins.then_inc(*pe.up(("xs", s, t)))

            def spread(s, key, src, n, h, mask=False):
                o = take((key, s, h), (key, s, h, "out"))
                if mask:
                    mm(o[:, 0:SBLK], identb[:, :], sbig[:, :], start=True, stop=False)
                mm(o[:, 0:T], srow[0:n, h, :], src[0:n, :], start=not mask, stop=not mask)
                ins = mm(o[:, T:SBLK], srow[0:n, h, :], src[0:n, P:T], start=not mask, stop=True)
                ins.then_inc(*pe.up((key, s, h)))

            def weighted(s, key, n, m_, val, wid, h, heads, ybanks):
                for t in range(TT):
                    if h == 0:
                        take((key, s, t), (key, s, t, "out"), ybanks[t])
                y0, y1 = (ps[:, b, h * wid:(h + 1) * wid] for b in ybanks)
                e = ebuf(n)[:, (h % 2) * SBLK:(h % 2 + 1) * SBLK]
                mm(y0, e[:, 0:P], val(0, h), start=True, stop=True)
                mm(y1, e[:, P:T], val(0, h), start=True, stop=False)
                ins = mm(y1, e[:, T:SBLK], val(1, h), start=False, stop=True)
                ins.then_inc(*pe.up((key, s, "head", h)))
                if h == heads - 1:
                    for t in range(TT):
                        pe.mark((key, s, t))

            def mamba_heads(order):
                for n in range(len(order) + 2):
                    if n < len(order):
                        s, pr = order[n]
                        eng.wait_ge(*pe.at("csr", s, "out"))
                        for h in (2 * pr, 2 * pr + 1):
                            spread(s, "csB", csT[s], MH, h)
                    if n >= 2:
                        s, pr = order[n - 2]
                        eng.wait_ge(*pe.at("M", s, pr))
                        eng.wait_ge(*pe.at("xdt", s))
                        xdt = carve_m(s)[4]
                        for h in (2 * pr, 2 * pr + 1):
                            weighted(s, "Y", n - 2, None, lambda t, h: xdt[:, t, h * MD:h * MD + MD], MD, h, MH,
                                     (6 - 2 * s, 7 - 2 * s))

            def mamba_out(s):
                y, yT = carve_m(s)[5:7]
                eng.wait_ge(*pe.at("yn", s))
                for m in range(0, DM, 2):
                    o = take(("yT", s, m), ("yT", s, m, "out"))
                    for j in range(2):
                        for t in range(TT):
                            ins = nc.tensor.transpose(o[:, j * T + t * P:j * T + t * P + P],
                                                      y[:, t, (m + j) * P:(m + j) * P + P], ident[:, :])
                    ins.then_inc(*pe.up(("yT", s, m)))
                rowproj(s, "mo", wout, yT, [("yT", s, DM - 2, "out")], kc=DM)

            def mlstm_gates(s):
                transposes(s, "zTb", z[s], ("z4", s))
                eng.wait_ge(*pe.at("zTb", s, "out"))
                eng.wait_ge(*pe.at("cT2", s))
                o = take(("gt", s), ("gt", s, "out"))
                for t in range(TT):
                    tk = slice(t * P, t * P + P)
                    ins = group(o[:, t * 8:t * 8 + 8],
                                [(zT[s][:, k, tk], gk[:, k, :]) for k in range(KC)] +
                                [(cT[s][:, k, tk], gk[:, (1 + i) * KC + k, :]) for i in range(2) for k in range(KC)])
                ins.then_inc(*pe.up(("gt", s)))

            def mlstm_sums(s):
                eng.wait_ge(*pe.at("lf", s))
                cumsum(s, "cs2", th(sm(s, 5, 8), LH), LH)

            def mlstm_rows(s):
                eng.wait_ge(*pe.at("a", s))
                rows_of(s, "ar", th(sm(s, 6, 8), LH), LH)

            def mlstm_cols(s):
                eng.wait_ge(*pe.at("mt", s))
                o = take(("mtok", s), ("mtok", s, "out"))
                for t in range(TT):
                    ins = mm(o[:, t * LH:t * LH + LH], csT[s][0:LH, t * P:t * P + P], ident[0:LH, 0:LH],
                             start=True, stop=True)
                ins.then_inc(*pe.up(("mtok", s)))

            def mlstm_heads(order):
                for n in range(len(order) + 3):
                    if n < len(order):
                        s, pr = order[n]
                        eng.wait_ge(*pe.at("mt", s))
                        for h in (2 * pr, 2 * pr + 1):
                            spread(s, "MB", csT[s], LH, h, mask=True)
                    if 0 <= n - 2 < len(order):
                        s, pr = order[n - 2]
                        for h in (2 * pr, 2 * pr + 1):
                            m, r = h // 2, slice(LD * (h % 2), LD * (h % 2) + LD)
                            o = take(("qk", s, h), ("qk", s, h, "out"))
                            mm(o[:, 0:T], cT[s][r, m, 0:P], zT[s][r, m, :], start=True, stop=True)
                            mm(o[:, T:SBLK], cT[s][r, m, P:T], zT[s][r, m, P:T], start=True, stop=True).then_inc(*pe.up(("qk", s, h)))
                    if n >= 3:
                        s, pr = order[n - 3]
                        eng.wait_ge(*pe.at("C", s, pr))
                        eng.wait_ge(*pe.at("v1", s))
                        for h in (2 * pr, 2 * pr + 1):
                            weighted(s, "H", n - 3, None,
                                     lambda t, h: v1[s][:, (t * LH + h) * (LD + 1):(t * LH + h + 1) * (LD + 1)],
                                     LD + 1, h, LH, (6 - 2 * s, 7 - 2 * s))

            MORDER = [(s, pr) for pr in range(MH // 2) for s in range(NS)]
            LORDER = [(s, pr) for pr in range(LH // 2) for s in range(NS)]
            with eng.Fori(0, TURNS) as g:
                pe.turn = g
                gate(pe, 1)
                NB[0] = 4
                spin[0] = 0
                pe.stage("mamba")
                for s in range(NS):
                    transposes(s, "zTa", xin[s], ("xin2", s))
                for f in (mamba_dt, mamba_in, mamba_sums, mamba_mid):
                    for s in range(NS):
                        f(s)
                mamba_heads(MORDER)
                for s in range(NS):
                    mamba_out(s)
                pe.stage("mlstm")
                for f in (mlstm_gates, mlstm_sums, mlstm_rows, mlstm_cols):
                    for s in range(NS):
                        f(s)
                mlstm_heads(LORDER)
                pe.stage("ffn")
                for s in range(NS):
                    transposes(s, "zTc", z2[s], ("z5", s))
                for s in range(NS):
                    colproj(s, "f1", w1T, zT[s], [("zTc", s, "out")], 0, FM)
                for s in range(NS):
                    rowproj(s, "f2", w2T, hTb(s), [("f1", s, FM - 2, "out")], kc=FM)
                done(pe, 1)
                pe.turn, pe.met = None, {}

        @block.scalar
        def _(eng):
            act = lane(eng, "act")
            A = nc.scalar.activation

            def psv(mark):
                return ps[:, bank(mark), :]

            def ln_rstd(s, key, n, e=0):
                eng.wait_ge(*act.at(key, s, "mv"))
                A(lnv[s][:, 0:n], mv[s][:, 0:n, 1], ACT.Ln, bias=eps[:, e:e + 1]).then_inc(*act.up())
                eng.wait_ge(*act.own())
                A(rstd[s][:, 0:n], lnv[s][:, 0:n], ACT.Exp, scale=-0.5).then_inc(*act.up((key, s, "rstd")))

            def evict(mark, dst, n=512, outmark=None, scale=1.0):
                eng.wait_ge(*act.at(*mark))
                A(dst, psv(mark)[:, 0:n], ACT.Copy, scale=scale).then_inc(*act.up(outmark or mark + ("out",)))

            act.stage("ready")
            eng.wait_ge(*act.at("lam"))
            A(t1, t1, ACT.Exp).then_inc(*act.up())
            eng.wait_ge(*act.own())
            A(t2, t1, ACT.Exp, scale=pcol[:, 2:3]).then_inc(*act.up())
            A(to_, t1, ACT.Exp, scale=pcol[:, 3:4]).then_inc(*act.up())
            eng.wait_ge(*act.own())
            A(t1, t1, ACT.Exp, scale=pcol[:, 1:2]).then_inc(*act.up())
            nc.scalar.preload_act_table_set("natural_log_exp_and_others")
            done(act, 0)
            loaded(act, 0)

            def rwkv(s):
                (xx, xr, xk, xv, xg, rT, vT, Ks, Kc, g, ag, agT), _ = carve_r(s)
                evict(("rT", s, 0), flat(rT))
                eng.wait_ge(*act.at("g", s))
                A(flat(g), psv(("g", s)), ACT.Exp, scale=-1.0).then_inc(*act.up(("g", s, "out")))

            UNITS = [(s, 2 * m + e) for m in range(AM) for s in range(NS) for e in range(2)]

            def attn_exp(n, s, h):
                eng.wait_ge(*act.at("max", s, h))
                src, nm = psv(("S", s, h)), nmax(n)
                pb = pbuf(n)
                if n >= 6:
                    eng.wait_ge(*act.at("PT", *UNITS[n - 6]))
                A(pb[:, 0:P], src[:, 0:P], ACT.Exp, bias=nm[:, 0:1]).then_inc(*act.up())
                A(pb[:, P:SBLK], src[:, P:SBLK], ACT.Exp, bias=nm[:, 1:2]).then_inc(*act.up(("E", s, h)))

            def attn_pt(n, s, h):
                if n % 2 == 0:
                    if n >= 6:
                        eng.wait_ge(*act.at("pv", *UNITS[n - 6]))
                    evict(("PT", s, h), ptbuf(n), SBLK)

            with eng.Fori(0, TURNS) as g:
                act.turn = g
                gate(act, 0)
                act.stage("rwkv")
                for s in range(NS):
                    rwkv(s)
                for s in range(NS):
                    for h in range(RH):
                        eng.wait_ge(*act.at("A", s, h, "out"))
                        if h >= 4:
                            eng.wait_ge(*act.at("mixed", s, h - 4))
                        elif s:
                            eng.wait_ge(*act.at(*(("mixed", s - 1, RH - 4 + h) if h < 3 else ("attn", s - 1))))
                        A(atb(h)[:, P:T], psv(("A", s, h))[:, P:T], ACT.Copy).then_inc(*act.up(("A", s, h, "out2")))
                for s in range(NS):
                    evict(("agT", s), flat(carve_r(s)[0][11]))
                for s in range(NS):
                    ln_rstd(s, "ln_y", TT)
                for s in range(NS):
                    ln_rstd(s, "ln_1", TT)
                act.stage("attn")
                for s in range(NS):
                    evict(("zT1", s), flat(zT[s]))
                for s in range(NS):
                    QT, KT, V, O = carve_a(s)[0]
                    for m in range(0, AM, 2):
                        evict(("K", s, m), flat(KT[:, m:m + 2, :]))
                    for m in range(0, AM, 2):
                        evict(("Q", s, m), flat(QT[:, m:m + 2, :]), scale=AD ** -0.5)
                for n in range(len(UNITS) + 4):
                    if n < len(UNITS):
                        attn_exp(n, *UNITS[n])
                    if 0 <= n - 3 < len(UNITS):
                        attn_pt(n - 3, *UNITS[n - 3])
                for s in range(NS):
                    OT = carve_a(s)[0][0]
                    for m in range(0, AM, 2):
                        evict(("OT", s, m), flat(OT[:, m:m + 2, :]))
                for s in range(NS):
                    ln_rstd(s, "ln_2", TT)
                act.stage("moe")
                for s in range(NS):
                    evict(("zT2", s), flat(zT[s]))
                for s in range(NS):
                    eng.wait_ge(*act.at("logit", s))
                    A(small[s][:, 0:TT * NR], small[s][:, 0:TT * NR], ACT.Exp).then_inc(*act.up(("prob", s)))
                for e in range(0, NE, 2):
                    for s in range(NS):
                        eng.wait_ge(*act.at("up", s, e))
                        if e >= 4:
                            eng.wait_ge(*act.at(*(("dn", s, e - 3) if e > 4 else ("shared", s))))
                        A(flat(abuf(s, e)), psv(("up", s, e)), ACT.Gelu).then_inc(*act.up(("up", s, e, "out")))
                nc.scalar.preload_act_table_set("natural_log_exp_and_others")
                for s in range(NS):
                    ln_rstd(s, "ln_3", TT)
                done(act, 0)
                act.turn, act.met = None, {}
            if stop <= 3:
                return

            act.stage("setup1")
            eng.wait_ge(*act.at("w12"))
            for d in range(2):
                eng.wait_ge(*act.at("alpha", d))
                A(flat(tmpw[:, d]), flat(tmpw[:, d]), ACT.Sign).then_inc(*act.up(("signs", d)))
            eng.wait_ge(*act.at("p2rows"))
            A(Arow, Arow, ACT.Exp).then_inc(*act.up())
            for d in range(2):
                rows, colsn, dst = (FM, KC, w1T) if d == 0 else (KC, FM, w2T)
                for cc in range(colsn):
                    for r0 in range(0, rows, 4):
                        n_ = min(4, rows - r0)
                        evict(("wT", d, cc, r0), dst[:, cc, r0 * P:(r0 + n_) * P], n_ * P)
            done(act, 1)
            loaded(act, 1)

            def softplus(s, key, x, e, l):
                eng.wait_ge(*act.at(key, s, "x"))
                A(e, x, ACT.Abs).then_inc(*act.up())
                eng.wait_ge(*act.own())
                A(e, e, ACT.Exp, scale=-1.0).then_inc(*act.up())
                eng.wait_ge(*act.own())
                A(l, e, ACT.Ln, bias=eps[:, 2:3]).then_inc(*act.up((key, s, "log")))

            def exps(order, srckey, dstkey, scale, free):
                for n in range(len(order)):
                    s, pr = order[n]
                    eng.wait_ge(*act.at(srckey, s, pr))
                    A(ebuf(n), ebuf(n), ACT.Exp, scale=scale).then_inc(*act.up((dstkey, s, pr)))

            MORDER = [(s, pr) for pr in range(MH // 2) for s in range(NS)]
            LORDER = [(s, pr) for pr in range(LH // 2) for s in range(NS)]
            with eng.Fori(0, TURNS) as g:
                act.turn = g
                gate(act, 1)
                act.stage("mamba")
                for s in range(NS):
                    evict(("zTa", s), flat(zT[s]))
                for s in range(NS):
                    softplus(s, "dtx", sm(s, 0), sm(s, 1), sm(s, 2))
                nc.scalar.preload_act_table_set("silu_and_others")
                for s in range(NS):
                    xpad, xb, sz, xs, xdt, y, yT = carve_m(s)
                    for m in range(0, CM, 2):
                        eng.wait_ge(*act.at("xbc", s, m))
                        src = psv(("xbc", s, m)).rearrange("p (a t) -> p a t", a=2)
                        A(xpad[:, m:m + 2, TAPS - 1:], src, ACT.Copy).then_inc(*act.up(("xpad", s, m)))
                        for j in range(2):
                            A(xb[:, m + j, :], src[:, j, :], ACT.Identity, scale=ck[:, m + j, TAPS - 1:TAPS],
                                  bias=cb[:, m + j:m + j + 1]).then_inc(*act.up(("tap3", s, m + j)))
                        act.mark(("xbc", s, m, "out"))
                    for t in range(TT):
                        eng.wait_ge(*act.at("zg", s, t))
                        A(sz[:, t, :], psv(("zg", s, t)), ACT.Silu).then_inc(*act.up(("zg", s, t, "out")))
                for s in range(NS):
                    xb = carve_m(s)[1]
                    for m in range(CM):
                        eng.wait_ge(*act.at("taps", s, m))
                        A(xb[:, m, :], xb[:, m, :], ACT.Silu).then_inc(*act.up(("conv", s, m)))
                nc.scalar.preload_act_table_set("natural_log_exp_and_others")
                for s in range(NS):
                    eng.wait_ge(*act.at("csr", s))
                    A(csT[s][0:MH, :], psv(("csr", s))[0:MH, 0:T], ACT.Copy).then_inc(*act.up(("csr", s, "out")))
                    xs = carve_m(s)[3]
                    for t in range(TT):
                        evict(("xs", s, t), xs[:, t, :])
                exps(MORDER, "Edec", "Ex", 1.0, None)
                for s in range(NS):
                    y, yT = carve_m(s)[5:7]
                    junk = carve_m(s)[4]
                    for t in range(TT):
                        eng.wait_ge(*act.at("y", s, t))
                        A(junk[:, t, :], y[:, t, :], ACT.Square, accum_out=sm(s, 7)[:, t:t + 1]).then_inc(*act.up())
                    eng.wait_ge(*act.own())
                    A(sm(s, 7)[:, 0:TT], sm(s, 7)[:, 0:TT], ACT.Ln, scale=1.0 / DI, bias=eps[:, 0:1]).then_inc(*act.up())
                    eng.wait_ge(*act.own())
                    A(sm(s, 7)[:, 0:TT], sm(s, 7)[:, 0:TT], ACT.Exp, scale=-0.5).then_inc(*act.up(("yr", s)))
                for s in range(NS):
                    y, yT = carve_m(s)[5:7]
                    for m in range(0, DM, 2):
                        eng.wait_ge(*act.at("yT", s, m))
                        for j in range(2):
                            A(yT[:, m + j, :], psv(("yT", s, m))[:, j * T:j * T + T], ACT.Copy,
                                  scale=nw[:, m + j:m + j + 1]).then_inc(*act.up(("yT", s, m, "out") if j else None))
                for s in range(NS):
                    ln_rstd(s, "ln_4", TT)
                act.stage("mlstm")
                for s in range(NS):
                    evict(("zTb", s), flat(zT[s]))
                for s in range(NS):
                    softplus(s, "fg", sm(s, 1, 8), sm(s, 2, 8), sm(s, 3, 8))
                for s in range(NS):
                    eng.wait_ge(*act.at("mc", s))
                    A(sm(s, 8, 8), sm(s, 8, 8), ACT.Exp, scale=-1.0).then_inc(*act.up(("nrm", s)))
                exps(LORDER, "D", "Dx", -1.0, None)
                for s in range(NS):
                    ln_rstd(s, "ln_h", TT * LH, 1)
                for s in range(NS):
                    ln_rstd(s, "ln_5", TT)
                act.stage("ffn")
                for s in range(NS):
                    evict(("zTc", s), flat(zT[s]))
                nc.scalar.preload_act_table_set("gelu_and_others")
                for s in range(NS):
                    for m in range(0, FM, 2):
                        eng.wait_ge(*act.at("f1", s, m))
                        for j in range(2):
                            A(hTb(s)[:, m + j, :], psv(("f1", s, m))[:, j * T:j * T + T], ACT.Gelu,
                                  scale=al1[:, m + j:m + j + 1], bias=b1[:, m + j:m + j + 1]).then_inc(*act.up(("f1", s, m, "out") if j else None))
                nc.scalar.preload_act_table_set("natural_log_exp_and_others")
                for s in range(NS):
                    ln_rstd(s, "ln_6", TT)
                done(act, 1)
                act.turn, act.met = None, {}

        @block.vector
        def _(eng):
            v = lane(eng, "dve")
            V_ = nc.vector

            def psv(mark):
                return ps[:, bank(mark), :]

            def settle():
                eng.wait_ge(*v.own())
                V_.tensor_copy(tick[:, 1:2], tick[:, 0:1]).then_inc(*v.up())

            def ln_stats(s, key, src, n=TT):
                for t in range(n):
                    V_.bn_stats(st6[s][:, t, :], src[:, t, :]).then_inc(*v.up())
                settle()
                for t in range(n):
                    V_.bn_aggr(mv[s][:, t, :], st6[s][:, t, :]).then_inc(*v.up((key, s, "mv") if t == n - 1 else None))

            def ln_apply(s, key, src, dst, mark=None):
                eng.wait_ge(*v.at(key, s, "rstd"))
                for t in range(TT):
                    V_.tensor_scalar(dst[:, t, :], src[:, t, :], mv[s][:, t, 0:1], rstd[s][:, t:t + 1],
                                       ALU.subtract, ALU.mult).then_inc(*v.up(mark if t == TT - 1 else None))

            v.stage("ready")
            for s in range(NS):
                V = carve_a(s)[0][2]
                V_.memset(V, 1.0).then_inc(*v.up())
            V_.memset(zrow[:, :], 0.0).then_inc(*v.up())
            V_.memset(tick[:, :], 0.0).then_inc(*v.up())
            done(v, 0)
            loaded(v, 0)

            def mixes(s):
                (xx, xr, xk, xv, xg, *_), _ = carve_r(s)
                x = xT[s]
                eng.wait_ge(*v.at("xT", s))
                V_.tensor_tensor(xx[:, :, 1:T], x[:, :, 0:T - 1], x[:, :, 1:T], ALU.subtract).then_inc(*v.up())
                V_.tensor_tensor(xx[:, :, 0:1], x[:, :, 1:2], x[:, :, 0:1], ALU.subtract).then_inc(*v.up())
                eng.wait_ge(*v.own())
                for i, (n, dst) in enumerate((("r", xr), ("v", xv), ("k", xk), ("g", xg))):
                    for k in range(KC):
                        V_.scalar_tensor_tensor(dst[:, k, :], xx[:, k, :], mix[:, i, k:k + 1], x[:, k, :],
                                                  ALU.mult, ALU.add).then_inc(*v.up((f"mix_{n}", s) if k == KC - 1 else None))

            def rwkv_evict(s):
                (xx, xr, xk, xv, xg, rT, vT, Ks, Kc, g, ag, agT), _ = carve_r(s)
                eng.wait_ge(*v.at("vT", s, 0))
                V_.tensor_copy(flat(vT), psv(("vT", s, 0))).then_inc(*v.up(("vT", s, 0, "out")))
                eng.wait_ge(*v.at("k", s))
                kk = psv(("k", s)).rearrange("p (t c) -> p t c", t=TT)
                V_.tensor_tensor(Kc, kk[:, 0, :], t2, ALU.mult).then_inc(*v.up())
                V_.tensor_tensor(Ks, kk, t1.unsqueeze(1).to_broadcast([P, TT, C]), ALU.mult).then_inc(*v.up(("k", s, "out")))
                v.mark(("ks", s))
                eng.wait_ge(*v.at("g", s, "out"))
                V_.tensor_scalar(flat(g), flat(g), 1.0, None, ALU.add).then_inc(*v.up())
                eng.wait_ge(*v.own())
                V_.reciprocal(flat(g), flat(g)).then_inc(*v.up())

            def rwkv_heads(s):
                vT = carve_r(s)[0][6]
                le2 = le[:, 0:P].unsqueeze(1).to_broadcast([P, 2, P])
                for h in range(RH + 1):
                    if h < RH:
                        if h >= 8:
                            eng.wait_ge(*v.at("A", s, h - 8))
                        elif s:
                            eng.wait_ge(*v.at("A", s - 1, h + 8))
                        else:
                            eng.wait_ge(*v.own())
                        V_.tensor_scalar(rot[:, h % 8, :], vT[:, h // 8, :], hcol[:, h % 8:h % 8 + 1], None,
                                           ALU.mult).then_inc(*v.up(("vh", s, h)))
                    if h >= 1:
                        q = h - 1
                        eng.wait_ge(*v.at("A", s, q))
                        if q >= 4:
                            eng.wait_ge(*v.at("mixed", s, q - 4))
                        elif s:
                            eng.wait_ge(*v.at(*(("mixed", s - 1, RH - 4 + q) if q < 3 else ("attn", s - 1))))
                        src = diag(psv(("A", s, q)))
                        V_.tensor_tensor(diag(pq[:, :], (6 + q % 4) * SBLK), src, le2, ALU.mult).then_inc(*v.up(("A", s, q, "out")))

            def rwkv_out(s):
                (xx, xr, xk, xv, xg, rT, vT, Ks, Kc, g, ag, agT), _ = carve_r(s)
                eng.wait_ge(*v.at("attn", s))
                V_.tensor_tensor(ag, psv(("attn", s)).rearrange("p (t c) -> p t c", t=TT),
                                   to_.unsqueeze(1).to_broadcast([P, TT, C]), ALU.mult).then_inc(*v.up(("attn", s, "out")))
                eng.wait_ge(*v.own())
                V_.tensor_tensor(flat(ag), flat(ag), flat(g), ALU.mult).then_inc(*v.up(("ag", s)))

            def ln_y(s):
                eng.wait_ge(*v.at("y", s))
                ln_stats(s, "ln_y", psv(("y", s)).rearrange("p (t c) -> p t c", t=TT))

            def ln_y2(s):
                src = psv(("y", s)).rearrange("p (t c) -> p t c", t=TT)
                ln_apply(s, "ln_y", src, z[s], ("y", s, "out"))
                eng.wait_ge(*v.own())
                V_.tensor_tensor(z[s][:, :, :], z[s][:, :, :], gam.unsqueeze(1).to_broadcast([P, TT, C]), ALU.mult).then_inc(*v.up())
                eng.wait_ge(*v.at("xin", s))
                eng.wait_ge(*v.at("xb", s))
                eng.wait_ge(*v.own())
                V_.tensor_tensor(z[s][:, :, :], z[s][:, :, :], xin[s][:, :, :], ALU.add).then_inc(*v.up())
                eng.wait_ge(*v.own())
                ln_stats(s, "ln_1", z[s])

            UNITS = [(s, 2 * m + e) for m in range(AM) for s in range(NS) for e in range(2)]

            def attn_max(n, s, h):
                eng.wait_ge(*v.at("S", s, h))
                if n >= 8:
                    eng.wait_ge(*v.at("E", *UNITS[n - 8]))
                src, nm = psv(("S", s, h)), nmax(n)
                V_.tensor_reduce(nm[:, 0:1], src[:, 0:P], AXX, ALU.max, negate=True).then_inc(*v.up())
                V_.tensor_reduce(nm[:, 1:2], src[:, P:SBLK], AXX, ALU.max, negate=True).then_inc(*v.up(("max", s, h)))

            def attn_pt(n, s, h):
                if n % 2 == 1:
                    eng.wait_ge(*v.at("PT", s, h))
                    if n >= 6:
                        eng.wait_ge(*v.at("pv", *UNITS[n - 6]))
                    V_.tensor_copy(ptbuf(n), psv(("PT", s, h))[:, 0:SBLK]).then_inc(*v.up(("PT", s, h, "out")))

            def attn_norm(n, s, h):
                if h % 2 == 0:
                    return
                O = carve_a(s)[0][3]
                eng.wait_ge(*v.at("O", s, h // 2))
                o = psv(("O", s, h // 2))[:, 0:4 * (AD + 1)].rearrange("p (t e d) -> p t e d", t=TT, e=2)
                rs = small[s][:, 128 + 4 * (h // 2 % 2):132 + 4 * (h // 2 % 2)].rearrange("p (t e) -> p t e", t=TT)
                V_.reciprocal(rs, o[:, :, :, AD]).then_inc(*v.up())
                eng.wait_ge(*v.own())
                dst = O[:, :, (h - 1) * AD:(h + 1) * AD].rearrange("p t (e d) -> p t e d", e=2)
                for t in range(TT):
                    V_.tensor_tensor(dst[:, t], o[:, t, :, 0:AD], rs[:, t, :].unsqueeze(2).to_broadcast([P, 2, AD]),
                                       ALU.mult).then_inc(*v.up(("O", s, h // 2, "out") if t == TT - 1 else None))

            def residual(s, key, base, dst, lnkey):
                eng.wait_ge(*v.at(key, s))
                V_.tensor_tensor(dst[:, :, :], psv((key, s)).rearrange("p (t c) -> p t c", t=TT), base, ALU.add).then_inc(*v.up((key, s, "out")))
                eng.wait_ge(*v.own())
                ln_stats(s, lnkey, dst)

            def bc(ap, n):
                return ap.unsqueeze(2).to_broadcast([P, TT, n])

            def route(s):
                f = small[s]

                def t3(i):
                    return f[:, i * TT * NR:(i + 1) * TT * NR].rearrange("p (t r) -> p t r", t=TT)
                lg, gt, eq, cum = t3(0), t3(1), t3(2), t3(3)
                red = f[:, 160:164]
                top = f[:, 176:192].rearrange("p (t r) -> p t r", t=TT)
                src = psv(("route", s))[:, 0:TT * NR].rearrange("p (t r) -> p t r", t=TT)
                eng.wait_ge(*v.at("route", s))
                V_.tensor_reduce(red[:, 0:2], src, AXX, ALU.max).then_inc(*v.up())
                eng.wait_ge(*v.own())
                V_.tensor_tensor(lg, src, bc(red[:, 0:2], NR), ALU.subtract).then_inc(*v.up(("route", s, "out")))
                v.mark(("logit", s))

            def route2(s):
                f = small[s]

                def t3(i):
                    return f[:, i * TT * NR:(i + 1) * TT * NR].rearrange("p (t r) -> p t r", t=TT)
                lg, gt, eq, cum = t3(0), t3(1), t3(2), t3(3)
                red = f[:, 160:164]
                top = f[:, 176:192].rearrange("p (t r) -> p t r", t=TT)
                eng.wait_ge(*v.at("prob", s))
                V_.tensor_reduce(red[:, 0:2], lg, AXX, ALU.add).then_inc(*v.up())
                eng.wait_ge(*v.own())
                V_.reciprocal(red[:, 0:2], red[:, 0:2]).then_inc(*v.up())
                eng.wait_ge(*v.own())
                V_.tensor_tensor(lg, lg, bc(red[:, 0:2], NR), ALU.mult).then_inc(*v.up())
                settle()
                for t in range(TT):
                    V_.max(top[:, t, :], lg[:, t, :]).then_inc(*v.up())
                eng.wait_ge(*v.own())
                thr = top[:, :, TOPK - 1:TOPK].to_broadcast([P, TT, NR])
                V_.tensor_tensor(gt, lg, thr, ALU.is_gt).then_inc(*v.up())
                V_.tensor_tensor(eq, lg, thr, ALU.is_equal).then_inc(*v.up())
                eng.wait_ge(*v.own())
                V_.tensor_reduce(red[:, 2:4], gt, AXX, ALU.add).then_inc(*v.up())
                eng.wait_ge(*v.own())
                for t in range(TT):
                    V_.tensor_tensor_scan(cum[:, t, :], onesq[:, 0:NR], eq[:, t, :], red[:, 2 + t:3 + t],
                                            ALU.mult, ALU.add).then_inc(*v.up())
                eng.wait_ge(*v.own())
                V_.scalar_tensor_tensor(eq, cum, float(TOPK), eq, ALU.is_le, ALU.mult).then_inc(*v.up())
                eng.wait_ge(*v.own())
                V_.tensor_tensor(gt, gt, eq, ALU.add).then_inc(*v.up())
                eng.wait_ge(*v.own())
                V_.tensor_tensor(lg, lg, gt, ALU.mult).then_inc(*v.up())

            def gated(s, e):
                src = psv(("dn", s, e))
                eng.wait_ge(*v.at("dn", s, e))
                for t in range(TT):
                    eng.wait_ge(*v.own())
                    gcol = small[s][:, t * NR + e - NSH:t * NR + e - NSH + 1]
                    V_.scalar_tensor_tensor(z[s][:, t, :], src[:, t * C:t * C + C], gcol, z[s][:, t, :],
                                              ALU.mult, ALU.add).then_inc(*v.up(("dn", s, e, "out") if t == TT - 1 else None))

            with eng.Fori(0, TURNS) as g:
                v.turn = g
                gate(v, 0)
                v.stage("rwkv")
                for s in range(NS):
                    mixes(s)
                for s in range(NS):
                    rwkv_evict(s)
                for s in range(NS):
                    rwkv_heads(s)
                for s in range(NS):
                    rwkv_out(s)
                for s in range(NS):
                    eng.wait_ge(*v.at("m8", s))
                    V_.tensor_scalar(mrowb(s), m8(s), BIG, -BIG, ALU.mult, ALU.add).then_inc(*v.up(("mrow", s)))
                for s in range(NS):
                    ln_y(s)
                for s in range(NS):
                    ln_y2(s)
                for s in range(NS):
                    ln_apply(s, "ln_1", z[s], z[s], ("z1", s))
                v.stage("attn")
                for s in range(NS):
                    V = carve_a(s)[0][2]
                    for t in range(TT):
                        for j in range(2):
                            m = ("Vp", s, t, j)
                            eng.wait_ge(*v.at(*m))
                            dst = V[:, (t * AH + j * 8) * (AD + 1):(t * AH + j * 8 + 8) * (AD + 1)]
                            V_.tensor_copy(dst.rearrange("p (h d) -> p h d", h=8)[:, :, 0:AD],
                                             psv(m).rearrange("p (h d) -> p h d", h=8)).then_inc(*v.up(m + ("out",)))
                    v.mark(("V", s, "out"))
                    eng.wait_ge(*v.at("biasp", s))
                    V_.tensor_copy(mbias(s), psv(("biasp", s))[:, 0:SBLK]).then_inc(*v.up())
                    eng.wait_ge(*v.own())
                    mb2 = mbias(s)
                    V_.tensor_tensor(mb2[:, 0:P], mb2[:, 0:P], qneg[:, :], ALU.min).then_inc(*v.up())
                    V_.tensor_tensor(mb2[:, T:SBLK], mb2[:, T:SBLK], qneg[:, :], ALU.min).then_inc(*v.up(("bias", s)))
                for n in range(len(UNITS) + 6):
                    if n < len(UNITS):
                        attn_max(n, *UNITS[n])
                    if 0 <= n - 3 < len(UNITS):
                        attn_pt(n - 3, *UNITS[n - 3])
                    if 0 <= n - 6 < len(UNITS):
                        attn_norm(n - 6, *UNITS[n - 6])
                for s in range(NS):
                    eng.wait_ge(*v.at("zb", s))
                    residual(s, "xo", z[s][:, :, :], z2[s], "ln_2")
                for s in range(NS):
                    ln_apply(s, "ln_2", z2[s], z2[s], ("z2", s))
                v.stage("moe")
                for s in range(NS):
                    route(s)
                for s in range(NS):
                    route2(s)
                for e in range(0, NE, 2):
                    for s in range(NS):
                        if e == 0:
                            eng.wait_ge(*v.at("shared", s))
                            V_.tensor_tensor(z[s][:, :, :], psv(("shared", s)).rearrange("p (t c) -> p t c", t=TT),
                                               z2[s][:, :, :], ALU.add).then_inc(*v.up(("shared", s, "out")))
                            continue
                        for j in range(2):
                            gated(s, e + j)
                for s in range(NS):
                    eng.wait_ge(*v.own())
                    ln_stats(s, "ln_3", z[s])
                for s in range(NS):
                    ln_apply(s, "ln_3", z[s], xin[s], ("z3", s))
                done(v, 0)
                v.turn, v.met = None, {}
            if stop <= 3:
                return

            v.stage("setup1")
            for s in range(NS):
                V_.memset(v1[s], 1.0).then_inc(*v.up(("ones1", s)))
                V_.memset(carve_m(s)[0][:, :, 0:TAPS - 1], 0.0).then_inc(*v.up())
            eng.wait_ge(*v.at("w12"))
            V_.tensor_reduce(al1, tmpw[:, 0], AXX, ALU.add, apply_absolute_value=True).then_inc(*v.up())
            V_.tensor_reduce(al2[:, 0:KC], tmpw[:, 1].rearrange("p m c -> p (m c)").rearrange(
                "p (m c) -> p m c", m=KC), AXX, ALU.add, apply_absolute_value=True).then_inc(*v.up())
            eng.wait_ge(*v.own())
            V_.tensor_scalar(al1, al1, 1.0 / C, None, ALU.mult).then_inc(*v.up(("alpha", 0)))
            V_.tensor_scalar(al2[:, 0:KC], al2[:, 0:KC], 1.0 / FH, None, ALU.mult).then_inc(*v.up(("alpha", 1)))
            eng.wait_ge(*v.own())
            for j in range(KC):
                V_.tensor_scalar(dxs[0][:, 0, j * P:j * P + P], ident[:, :], al2[:, j:j + 1], None, ALU.mult).then_inc(*v.up("al2diag" if j else None))
            eng.wait_ge(*v.at("al2row"))
            V_.tensor_copy(al2r, psv("al2row")[:, 0:C]).then_inc(*v.up("al2row_out"))
            done(v, 1)
            loaded(v, 1)

            def softplus_end(s, key, x, e, l, u, w, dst):
                eng.wait_ge(*v.at(key, s, "log"))
                V_.tensor_scalar(u, e, 1.0, 1.0, ALU.add, ALU.subtract).then_inc(*v.up())
                eng.wait_ge(*v.own())
                V_.tensor_scalar(w, u, 0.0, None, ALU.is_equal).then_inc(*v.up())
                eng.wait_ge(*v.own())
                V_.tensor_tensor(u, u, w, ALU.add).then_inc(*v.up())
                eng.wait_ge(*v.own())
                V_.reciprocal(u, u).then_inc(*v.up())
                eng.wait_ge(*v.own())
                V_.tensor_tensor(l, l, u, ALU.mult).then_inc(*v.up())
                eng.wait_ge(*v.own())
                V_.tensor_tensor(l, l, w, ALU.add).then_inc(*v.up())
                eng.wait_ge(*v.own())
                V_.tensor_tensor(l, l, e, ALU.mult).then_inc(*v.up())
                eng.wait_ge(*v.own())
                V_.scalar_tensor_tensor(dst, x, 0.0, l, ALU.max, ALU.add).then_inc(*v.up((key, s, "sp")))

            def rowb(r, n):
                return r.unsqueeze(1).to_broadcast([P, TT, n])

            def dt_in(s):
                eng.wait_ge(*v.at("dt", s))
                V_.tensor_tensor(th(sm(s, 0), MH), th(psv(("dt", s))[:, 0:2 * MH], MH), rowb(dtb, MH), ALU.add).then_inc(*v.up(("dt", s, "out")))
                v.mark(("dtx", s, "x"))

            def taps(s):
                xpad, xb = carve_m(s)[0:2]
                for m in range(CM):
                    eng.wait_ge(*v.at("tap3", s, m))
                    for k in range(TAPS - 1):
                        if k:
                            eng.wait_ge(*v.own())
                        V_.scalar_tensor_tensor(xb[:, m, :], xpad[:, m, k:k + T], ck[:, m, k:k + 1], xb[:, m, :],
                                                  ALU.mult, ALU.add).then_inc(*v.up(("taps", s, m) if k == TAPS - 2 else None))

            def mamba_mid(s):
                eng.wait_ge(*v.at("cs", s))
                V_.tensor_copy(sm(s, 4), psv(("cs", s))[:, 0:2 * MH]).then_inc(*v.up(("cs", s, "out")))

            def mamba_mid2(s):
                xs, xdt = carve_m(s)[3:5]
                eng.wait_ge(*v.at("CB", s))
                V_.tensor_tensor(cbm[s], psv(("CB", s))[:, 0:SBLK], le[:, :], ALU.mult).then_inc(*v.up(("CB", s, "out")))
                for t in range(TT):
                    eng.wait_ge(*v.at("xs", s, t, "out"))
                    V_.tensor_tensor(xdt[:, t, :].rearrange("p (h d) -> p h d", h=MH),
                                       xs[:, t, :].rearrange("p (h d) -> p h d", h=MH),
                                       th(sm(s, 9), MH)[:, t, :].unsqueeze(2).to_broadcast([P, MH, MD]), ALU.mult).then_inc(*v.up(("xdt", s) if t else None))

            def decays(order, key, ekey, ccol, op, wkey, last):
                for n in range(len(order) + 2):
                    if n < len(order):
                        s, pr = order[n]
                        if n >= 6:
                            s6, p6 = order[n - 6]
                            eng.wait_ge(*v.at(wkey, s6, "head", 2 * p6 + 1))
                        for j in range(2):
                            h = 2 * pr + j
                            e = ebuf(n)[:, j * SBLK:(j + 1) * SBLK]
                            eng.wait_ge(*v.at(key, s, h))
                            src = psv((key, s, h))
                            cc = ccol(s)
                            V_.tensor_scalar(e[:, 0:T], src[:, 0:T], cc[:, 0, h:h + 1], 0.0, ALU.subtract, op).then_inc(*v.up())
                            V_.tensor_scalar(e[:, T:SBLK], src[:, T:SBLK], cc[:, 1, h:h + 1], 0.0,
                                               ALU.subtract, op).then_inc(*v.up((key, s, h, "out")))
                        v.mark((ekey, s, pr))
                    if n >= 2:
                        last(n - 2, *order[n - 2])

            def mamba_product(n, s, pr):
                eng.wait_ge(*v.at("Ex", s, pr))
                e = ebuf(n).rearrange("p (j c) -> p j c", j=2)
                V_.tensor_tensor(e, e, cbm[s].unsqueeze(1).to_broadcast([P, 2, SBLK]), ALU.mult).then_inc(*v.up(("M", s, pr)))

            def mlstm_product(n, s, pr):
                eng.wait_ge(*v.at("Dx", s, pr))
                for j in range(2):
                    h = 2 * pr + j
                    e = ebuf(n)[:, j * SBLK:(j + 1) * SBLK]
                    eng.wait_ge(*v.at("qk", s, h))
                    V_.scalar_tensor_tensor(e, psv(("qk", s, h))[:, 0:SBLK], LD ** -0.5, e, ALU.mult, ALU.mult).then_inc(*v.up(("qk", s, h, "out")))
                v.mark(("C", s, pr))

            def mamba_y(s):
                xpad, xb, sz, xs, xdt, y, yT = carve_m(s)
                eng.wait_ge(*v.at("dx", s))
                for t in range(TT):
                    eng.wait_ge(*v.at("Y", s, t))
                    yb = ps[:, (6 - 2 * s) + t, :]
                    V_.tensor_tensor(y[:, t, :], yb, dxs[s][:, t, :], ALU.add).then_inc(*v.up(("Y", s, t, "out")))
                for t in range(TT):
                    eng.wait_ge(*v.own())
                    V_.tensor_tensor(y[:, t, :], y[:, t, :], sz[:, t, :], ALU.mult).then_inc(*v.up(("y", s, t)))

            def mlstm_in(s):
                eng.wait_ge(*v.at("gt", s))
                gts = th(sm(s, 0), 8)
                V_.tensor_tensor(gts, th(psv(("gt", s))[:, 0:16], 8), rowb(gb, 8), ALU.add).then_inc(*v.up(("gt", s, "out")))
                eng.wait_ge(*v.own())
                V_.tensor_scalar(th(sm(s, 1, 8), LH), gts[:, :, LH:2 * LH], -1.0, None, ALU.mult).then_inc(*v.up(("fg", s, "x")))

            def mlstm_lf(s):
                softplus_end(s, "fg", sm(s, 1, 8), sm(s, 2, 8), sm(s, 3, 8), sm(s, 4, 8), sm(s, 7, 8), sm(s, 5, 8))
                eng.wait_ge(*v.own())
                V_.tensor_scalar(sm(s, 5, 8), sm(s, 5, 8), -1.0, None, ALU.mult).then_inc(*v.up(("lf", s)))

            def mlstm_a(s):
                eng.wait_ge(*v.at("cs2", s))
                V_.tensor_copy(sm(s, 9, 8), psv(("cs2", s))[:, 0:8]).then_inc(*v.up(("cs2", s, "out")))
                eng.wait_ge(*v.own())
                V_.tensor_tensor(th(sm(s, 6, 8), LH), th(sm(s, 0), 8)[:, :, 0:LH], th(sm(s, 9, 8), LH),
                                   ALU.subtract).then_inc(*v.up(("a", s)))

            def mlstm_scan(s):
                eng.wait_ge(*v.at("ar", s))
                V_.tensor_tensor_scan(csT[s][0:LH, :], zrow[0:LH, :], psv(("ar", s))[0:LH, 0:T], -BIG,
                                        ALU.add, ALU.max).then_inc(*v.up(("ar", s, "out")))
                v.mark(("mt", s))

            def mlstm_mc(s):
                eng.wait_ge(*v.at("mtok", s))
                V_.tensor_tensor(sm(s, 8, 8), psv(("mtok", s))[:, 0:8], sm(s, 9, 8), ALU.add).then_inc(*v.up(("mtok", s, "out")))
                v.mark(("mc", s))

            def h4(x):
                return x.rearrange("p (h d) -> p h d", h=LH)

            def mlstm_h(s):
                hb = carve_m(s)[5]
                den = th(sm(s, 10, 8), LH)
                eng.wait_ge(*v.at("nrm", s))
                for t in range(TT):
                    eng.wait_ge(*v.at("H", s, t))
                    src = h4(ps[:, 6 - 2 * s + t, 0:LH * (LD + 1)])
                    rs = src[:, :, LD]
                    V_.tensor_scalar(den[:, t, :], rs, -1.0, None, ALU.mult).then_inc(*v.up())
                    eng.wait_ge(*v.own())
                    V_.tensor_tensor(den[:, t, :], rs, den[:, t, :], ALU.max).then_inc(*v.up())
                    eng.wait_ge(*v.own())
                    V_.tensor_tensor(den[:, t, :], den[:, t, :], th(sm(s, 8, 8), LH)[:, t, :], ALU.max).then_inc(*v.up())
                    eng.wait_ge(*v.own())
                    V_.tensor_scalar(den[:, t, :], den[:, t, :], ML_EPS, None, ALU.add).then_inc(*v.up())
                    eng.wait_ge(*v.own())
                    V_.reciprocal(den[:, t, :], den[:, t, :]).then_inc(*v.up())
                    eng.wait_ge(*v.own())
                    V_.tensor_tensor(h4(hb[:, t, 0:C]), src[:, :, 0:LD],
                                       den[:, t, :].unsqueeze(2).to_broadcast([P, LH, LD]), ALU.mult).then_inc(*v.up(("H", s, t, "out")))
                eng.wait_ge(*v.own())
                for t in range(TT):
                    for h in range(LH):
                        V_.bn_stats(st6[s][:, t * LH + h, :], hb[:, t, h * LD:(h + 1) * LD]).then_inc(*v.up())
                settle()
                for i in range(TT * LH):
                    V_.bn_aggr(mv[s][:, i, :], st6[s][:, i, :]).then_inc(*v.up(("ln_h", s, "mv") if i == TT * LH - 1 else None))

            def mlstm_h2(s):
                hb = carve_m(s)[5]
                eng.wait_ge(*v.at("ln_h", s, "rstd"))
                for t in range(TT):
                    x = h4(hb[:, t, 0:C])
                    V_.tensor_tensor(x, x, mv[s][:, t * LH:(t + 1) * LH, 0:1].to_broadcast([P, LH, LD]),
                                       ALU.subtract).then_inc(*v.up())
                eng.wait_ge(*v.own())
                for t in range(TT):
                    x = h4(hb[:, t, 0:C])
                    V_.tensor_tensor(x, x, rstd[s][:, t * LH:(t + 1) * LH].unsqueeze(2).to_broadcast([P, LH, LD]),
                                       ALU.mult).then_inc(*v.up())
                eng.wait_ge(*v.own())
                V_.tensor_tensor(hb[:, :, 0:C], hb[:, :, 0:C], rowb(onorm, C), ALU.mult).then_inc(*v.up())
                eng.wait_ge(*v.own())
                V_.tensor_tensor(z2[s][:, :, :], hb[:, :, 0:C], z[s][:, :, :], ALU.add).then_inc(*v.up())
                eng.wait_ge(*v.own())
                ln_stats(s, "ln_5", z2[s])

            MORDER = [(s, pr) for pr in range(MH // 2) for s in range(NS)]
            LORDER = [(s, pr) for pr in range(LH // 2) for s in range(NS)]
            with eng.Fori(0, TURNS) as g:
                v.turn = g
                gate(v, 1)
                v.stage("mamba")
                for s in range(NS):
                    dt_in(s)
                for s in range(NS):
                    softplus_end(s, "dtx", sm(s, 0), sm(s, 1), sm(s, 2), sm(s, 5), sm(s, 6), sm(s, 9))
                    eng.wait_ge(*v.own())
                    V_.scalar_tensor_tensor(th(sm(s, 3), MH), th(sm(s, 9), MH), -1.0, rowb(Arow, MH),
                                              ALU.mult, ALU.mult).then_inc(*v.up(("dA", s)))
                for s in range(NS):
                    mamba_mid(s)
                for s in range(NS):
                    taps(s)
                for s in range(NS):
                    mamba_mid2(s)
                decays(MORDER, "csB", "Edec", lambda s: th(sm(s, 4), MH), ALU.min, "Y", mamba_product)
                for s in range(NS):
                    mamba_y(s)
                for s in range(NS):
                    y = carve_m(s)[5]
                    eng.wait_ge(*v.at("yr", s))
                    for t in range(TT):
                        V_.tensor_scalar(y[:, t, :], y[:, t, :], sm(s, 7)[:, t:t + 1], None, ALU.mult).then_inc(*v.up(("yn", s) if t else None))
                for s in range(NS):
                    eng.wait_ge(*v.at("mo", s))
                    V_.scalar_tensor_tensor(z[s][:, :, :], xin[s][:, :, :], 2.0,
                                              psv(("mo", s)).rearrange("p (t c) -> p t c", t=TT),
                                              ALU.mult, ALU.add).then_inc(*v.up(("mo", s, "out")))
                    eng.wait_ge(*v.own())
                    ln_stats(s, "ln_4", z[s])
                for s in range(NS):
                    ln_apply(s, "ln_4", z[s], z[s], ("z4", s))
                v.stage("mlstm")
                for f in (mlstm_in, mlstm_lf, mlstm_a, mlstm_scan, mlstm_mc):
                    for s in range(NS):
                        f(s)
                decays(LORDER, "MB", "D", lambda s: th(sm(s, 6, 8), LH), ALU.max, "H", mlstm_product)
                for s in range(NS):
                    mlstm_h(s)
                for s in range(NS):
                    mlstm_h2(s)
                for s in range(NS):
                    ln_apply(s, "ln_5", z2[s], z2[s], ("z5", s))
                v.stage("ffn")
                for s in range(NS):
                    eng.wait_ge(*v.at("f2", s))
                    eng.wait_ge(*v.at("z5b", s))
                    V_.tensor_tensor(z[s][:, :, :], psv(("f2", s)).rearrange("p (t c) -> p t c", t=TT),
                                       rowb(al2r, C), ALU.mult).then_inc(*v.up(("f2", s, "out")))
                    eng.wait_ge(*v.own())
                    V_.tensor_tensor(z[s][:, :, :], z[s][:, :, :], z2[s][:, :, :], ALU.add).then_inc(*v.up())
                    eng.wait_ge(*v.own())
                    ln_stats(s, "ln_6", z[s])
                for s in range(NS):
                    ln_apply(s, "ln_6", z[s], xin[s], ("z6", s))
                done(v, 1)
                v.turn, v.met = None, {}

        @block.gpsimd
        def _(eng):
            po = lane(eng, "pool")
            G = nc.gpsimd
            po.stage("consts")
            G.memset(ident[:, :], 0.0).then_inc(*po.up())
            G.memset(onesq[:, :], 1.0).then_inc(*po.up())
            G.memset(le[:, :], 1.0).then_inc(*po.up())
            G.memset(qneg[:, :], 0.0).then_inc(*po.up())
            G.memset(sbig[:, :], 0.0).then_inc(*po.up())
            G.memset(hcol[:, :], 1.0).then_inc(*po.up())
            G.memset(srow[:, :, :], 0.0).then_inc(*po.up())
            G.memset(onesb[:, :], 1.0).then_inc(*po.up())
            for i, e in enumerate((LN_EPS, ML_EPS, 1.0)):
                G.memset(eps[:, i:i + 1], e).then_inc(*po.up())
            G.iota(pint[:, :], [[0, 1]], base=0, channel_multiplier=1).then_inc(*po.up())
            eng.wait_ge(*po.own())
            sel = G.affine_select
            sel(out=ident[:, :], in_=ident[:, :], compare_op=ALU.not_equal, fill=1.0, base=0,
                   pattern=[[-1, P]], channel_multiplier=1).then_inc(*po.up())
            for c in (0, T):
                sel(out=le[:, c:c + P], in_=le[:, c:c + P], compare_op=ALU.is_ge, fill=0.0, base=0,
                       pattern=[[1, P]], channel_multiplier=-1).then_inc(*po.up())
            sel(out=qneg[:, :], in_=qneg[:, :], compare_op=ALU.is_ge, fill=-BIG, base=0,
                   pattern=[[-1, P]], channel_multiplier=1).then_inc(*po.up())
            for c in (0, T):
                sel(out=sbig[:, c:c + P], in_=sbig[:, c:c + P], compare_op=ALU.is_ge, fill=BIG, base=0,
                       pattern=[[1, P]], channel_multiplier=-1).then_inc(*po.up())
            sel(out=srow[:, :, :], in_=srow[:, :, :], compare_op=ALU.not_equal, fill=1.0, base=0,
                   pattern=[[-1, 8], [0, P]], channel_multiplier=1).then_inc(*po.up())
            sel(out=hcol[:, :], in_=hcol[:, :], compare_op=ALU.is_ge, fill=0.0, base=0,
                   pattern=[[-RD, 8]], channel_multiplier=1).then_inc(*po.up())
            G.tensor_copy(pcol[:, 0:1], pint[:, :]).then_inc(*po.up())
            eng.wait_ge(*po.own())
            sel(out=hcol[:, :], in_=hcol[:, :], compare_op=ALU.is_ge, fill=0.0, base=RD - 1,
                   pattern=[[RD, 8]], channel_multiplier=-1).then_inc(*po.up())
            G.tensor_scalar(pcol[:, 1:2], pcol[:, 0:1], float(-MID), None, ALU.add).then_inc(*po.up())
            G.tensor_scalar(pcol[:, 2:3], pcol[:, 0:1], float(-P - MID), None, ALU.add).then_inc(*po.up())
            G.tensor_scalar(pcol[:, 3:4], pcol[:, 0:1], -1.0, float(MID), ALU.mult, ALU.add).then_inc(*po.up())
            G.tensor_copy(identb[:, :], ident[:, :]).then_inc(*po.up())
            eng.wait_ge(*po.own())
            po.stage("ready")
            eng.wait_ge(*po.at("tdma"))
            G.tensor_copy(srow[:, 0, 0:1], srow[:, 0, 0:1]).then_inc(*po.up("lam"))
            done(po, 0)
            loaded(po, 0)
            with eng.Fori(0, TURNS) as g:
                po.turn = g
                gate(po, 0)
                po.stage("rwkv")
                for s in range(NS):
                    eng.wait_ge(*po.at("xin", s))
                    G.tensor_tensor(xin[s][:, :, :], xin[s][:, :, :],
                                       bet.unsqueeze(1).to_broadcast([P, TT, C]), ALU.add).then_inc(*po.up(("xb", s)))
                po.stage("attn")
                for s in range(NS):
                    eng.wait_ge(*po.at("zT1", s))
                    G.tensor_tensor(z[s][:, :, :], z[s][:, :, :],
                                       bo_.unsqueeze(1).to_broadcast([P, TT, C]), ALU.add).then_inc(*po.up(("zb", s)))
                done(po, 0)
                po.turn, po.met = None, {}
            if stop <= 3:
                return

            done(po, 1)
            loaded(po, 1)
            with eng.Fori(0, TURNS) as g:
                po.turn = g
                gate(po, 1)
                po.stage("mamba")
                for s in range(NS):
                    xs = carve_m(s)[3]
                    for t in range(TT):
                        eng.wait_ge(*po.at("xs", s, t, "out"))
                        G.tensor_tensor(dxs[s][:, t, :], xs[:, t, :], drow, ALU.mult).then_inc(*po.up(("dx", s) if t else None))
                po.stage("ffn")
                for s in range(NS):
                    eng.wait_ge(*po.at("zTc", s))
                    G.tensor_tensor(z2[s][:, :, :], z2[s][:, :, :],
                                       b2r.unsqueeze(1).to_broadcast([P, TT, C]), ALU.add).then_inc(*po.up(("z5b", s)))
                done(po, 1)
                po.turn, po.met = None, {}

        @block.sync
        def _(eng):
            sp = lane(eng, "sp")

            def dma(dst, src, sem, mark=None):
                nc.sync.dma_start(dst, src).then_inc(*sp.up(mark, by=16, sem=sem))

            def written(name):
                count = sp.turn * 16 + 16
                for s in range(NS):
                    eng.wait_ge(sp.sem(f"{name}{s}"), count)

            for name in ("out_mid", "out_y"):
                for s in range(NS):
                    eng.drain().then_inc(sp.sem(f"{name}{s}"), 16)
            dma(t1, a["time_decay"].unsqueeze(0).to_broadcast([P, C]), "tdecay", "tdma")
            n = 0
            for d, s_ in ((wr, "W_r"), (wv, "W_v"), (wk, "W_k"), (wg, "W_g"), (wo, "W_o"), (wkk, "Wk"), (wvv, "Wv"),
                          (wq, "Wq"), (woo, "Wo"), (rw, "router"), (up, "up"), (down, "down")):
                dma(d, a[s_], "weights0")
            dma(mix[:, :, :], a["mixes"], "weights0")
            for d, s_ in ((gam, "gamma"), (bet, "beta"), (bo_, "bo")):
                dma(d, a[s_].unsqueeze(0).to_broadcast([P, C]), "weights0")
            eng.wait_ge(*sp.own())
            eng.wait_ge(sp.sem("tdecay"), 16)
            done(sp, 0)
            with eng.Fori(0, TURNS) as g:
                sp.turn = g
                gate(sp, 0)
                for s in range(NS):
                    b = g * NS + s
                    dma(xT[s][:, :, :], dyn(a["xT"], b), f"in_xT{s}", ("xT", s))
                written("out_mid")
                for s in range(NS):
                    b = g * NS + s
                    dma(xin[s][:, :, :], dyn(a["x"], b), f"in_x{s}", ("xin", s))
                    dma(m8(s), dyn(a["mask"], b), f"in_mask{s}", ("m8", s))
                    dma(cT[s][:, :, :], dyn(a["cT"], b), f"in_cT{s}", ("cT", s))
                for s in range(NS):
                    dst = dyn(xmid, g * NS + s)
                    eng.wait_ge(*sp.at("z3", s))
                    dma(dst, xin[s][:, :, :], f"out_mid{s}", ("mid", s))
                sp.turn, sp.met = None, {}
            for s in range(NS):
                eng.wait_ge(sp.sem(f"out_mid{s}"), 16 * TURNS + 16)
            if stop <= 3:
                return

            for e in ENGINES:
                eng.wait_ge(sp.sem(f"turned0_{e}"), TURNS + 1)
            dma(tmpw[:, 0], a["w1"], "w12")
            dma(flat(tmpw[:, 1]), a["w2"], "w12", "w12")
            for d, s_ in ((Arow, "A_log"), (dtb, "dt_bias"), (drow, "D"), (gb, "gate_b"), (onorm, "onorm"), (b2r, "b2")):
                dma(d, a[s_].unsqueeze(0).to_broadcast([P, d.shape[1]]), "rows1")
            sp.mark("p2rows")
            for d, s_ in ((win, "in_proj"), (wout, "out_proj"), (ck, "conv_w"), (cb, "conv_b"), (nw, "norm_w"),
                          (gk, "gate_k"), (b1, "b1")):
                dma(d, a[s_], "weights1")
            eng.wait_ge(*sp.own())
            eng.wait_ge(*sp.at("w12"))
            eng.wait_ge(*sp.at("p2rows"))
            done(sp, 1)
            with eng.Fori(0, TURNS) as g:
                sp.turn = g
                gate(sp, 1)
                for s in range(NS):
                    b = g * NS + s
                    dma(cT[s][:, :, :], dyn(a["cT"], b), f"in_cT2{s}", ("cT2", s))
                written("out_y")
                for s in range(NS):
                    b = g * NS + s
                    dma(xin[s][:, :, :], dyn(xmid, b), f"in_x2{s}", ("xin2", s))
                for s in range(NS):
                    b = g * NS + s
                    for t in range(TT):
                        dma(v1[s][:, t * LH * (LD + 1):(t + 1) * LH * (LD + 1)].rearrange(
                            "p (h d) -> p h d", h=LH)[:, :, 0:LD], dyn(a["c"], b)[:, t, :].rearrange(
                            "p (h d) -> p h d", h=LH), f"in_v{s}", ("v1", s) if t else None)
                for s in range(NS):
                    dst = dyn(out, g * NS + s)
                    eng.wait_ge(*sp.at("z6", s))
                    dma(dst, xin[s][:, :, :], f"out_y{s}", ("outd", s))
                sp.turn, sp.met = None, {}
            for s in range(NS):
                eng.wait_ge(sp.sem(f"out_y{s}"), 16 * TURNS + 16)


def laid_out(i):
    import numpy as np
    i = {k: np.asarray(v) for k, v in i.items()}

    def cols(w):
        w = np.ascontiguousarray(w.T)
        return w.reshape(-1, P, w.shape[1]).transpose(1, 0, 2)

    def tok(x):
        return x.reshape(B, TT, P, C).transpose(0, 2, 1, 3)

    def chan(x):
        return x.transpose(0, 2, 1).reshape(B, KC, P, T).transpose(0, 2, 1, 3)
    up = np.concatenate([i["L0_ffn_shared_up"], i["L0_ffn_routed_up"]])
    down = np.concatenate([i["L0_ffn_shared_down"], i["L0_ffn_routed_down"]])
    a = {
        "x": tok(i["x"]), "xT": chan(i["x"]), "cT": chan(i["ctx_1024"]),
        "mask": i["mask_BxS2_bf1"].view(np.uint8).reshape(B, 1, T)[:, 0],
        "time_decay": i["L0_attn_time_decay"],
        "mixes": np.stack([i["L0_attn_time_mix_" + n] for n in "rvkg"]).reshape(4, KC, P).transpose(2, 0, 1),
        "W_r": cols(i["L0_attn_W_r"]), "W_k": cols(i["L0_attn_W_k"]), "W_v": cols(i["L0_attn_W_v"]),
        "W_g": cols(i["L0_attn_W_g"]), "W_o": cols(i["L0_attn_W_o"]),
        "gamma": i["L0_attn_ln_gamma"], "beta": i["L0_attn_ln_beta"],
        "Wq": cols(i["L0_xattn_Wq"]), "Wk": cols(i["L0_xattn_Wk"]), "Wv": cols(i["L0_xattn_Wv"]),
        "Wo": cols(i["L0_xattn_Wo"]), "bo": i["L0_xattn_bo"],
        "up": up.reshape(NE, ED, KC, P).transpose(3, 0, 2, 1).reshape(P, NE * KC, ED),
        "down": down.transpose(2, 0, 1), "router": cols(i["L0_ffn_router_w"]),
        "c": tok(i["ctx_1024"]), "in_proj": cols(i["L1_attn_in_proj_w"]), "out_proj": cols(i["L1_attn_out_proj_w"]),
        "conv_w": i["L1_attn_conv_w"].reshape(CM, P, TAPS).transpose(1, 0, 2),
        "conv_b": i["L1_attn_conv_b"].reshape(CM, P).T, "dt_bias": i["L1_attn_dt_bias"],
        "A_log": i["L1_attn_A_log"], "D": np.repeat(i["L1_attn_D"], MD), "norm_w": i["L1_attn_norm_w"].reshape(DM, P).T,
        "gate_k": np.concatenate([i["L1_xattn_igate_kernel"], i["L1_xattn_fgate_kernel"]], 1)
        .reshape(3 * KC, P, 2 * LH).transpose(1, 0, 2),
        "gate_b": np.concatenate([i["L1_xattn_igate_bias"], i["L1_xattn_fgate_bias"]]),
        "onorm": i["L1_xattn_outnorm_scale"], "w1": i["L1_ffn_w1"].reshape(FM, P, C).transpose(1, 0, 2),
        "w2": i["L1_ffn_w2"].reshape(KC, P, FH).transpose(1, 0, 2).reshape(P, KC * FH),
        "b1": i["L1_ffn_b1"].reshape(FM, P).T, "b2": i["L1_ffn_b2"],
    }
    return {k: np.ascontiguousarray(v) for k, v in a.items()}


def program(nc, scratch, arrays, stop=9):
    def declare(nc):
        a = {k: nc.dram_tensor(f"in_{k}", v.shape, mybir.dt.from_np(v.dtype), kind="ExternalInput").ap()
             for k, v in arrays.items()}
        out = nc.dram_tensor("out", (B, P, TT, C), F32, kind="ExternalOutput").ap()
        return a, out, out if stop <= 3 else nc.dram_tensor("xmid", (B, P, TT, C), F32).ap()
    counted = Book()
    build(scratch, *declare(scratch), counted, stop)
    build(nc, *declare(nc), Book(counted), stop)


def kernel(**inputs):
    import concourse.bacc as bacc
    from concourse.bass_utils import run_bass_kernel_spmd
    nc, scratch = (bacc.Bacc("TRN2", target_bir_lowering=False, num_devices=1) for _ in range(2))
    arrays = laid_out(inputs)
    program(nc, scratch, arrays)
    r = run_bass_kernel_spmd(nc, [{"in_" + k: v for k, v in arrays.items()}], core_ids=[0])
    return r.results[0]["out"].transpose(0, 2, 1, 3).reshape(B, T, C)
```

```python
from contextlib import ExitStack

import concourse.bass as bass
from concourse import mybir

ALU = mybir.AluOpType
ACT = mybir.ActivationFunctionType
AXX = mybir.AxisListType.X
F32 = mybir.dt.float32
F16 = mybir.dt.float16
BF16 = mybir.dt.bfloat16
U8 = mybir.dt.uint8
I32 = mybir.dt.int32

P = 128
B, T, C = 8, 256, 256
NS = 2
TURNS = B // NS
TT = T // P
KC = C // P
LN_EPS, ML_EPS, RMS_EPS = 1e-5, 1e-6, 1e-5
RH, RD = 16, 16
AH, AD = 16, 64
INNER = AH * AD
AM = INNER // P
NSH, NR, ED, TOPK = 2, 16, 128, 4
NE = NSH + NR
DI, DS, MH, MD, TAPS = 512, 128, 8, 64, 4
CONV = DI + 2 * DS
CM = CONV // P
DM = DI // P
LH, LD = 4, 64
FH = 1024
FM = FH // P
BIG = 1e30
MID = P // 2
UNITS = [(s, h) for s in range(NS) for h in range(AH)]
OUT0 = AH + 6
SBLK = 3 * P


ORDER = [tuple(int(x) if x.isdigit() else x for x in w.split(".")) for w in """
    decay.0.0 decay.1.0 decay.0.1 scan.0.0 decay.0.2 decay.1.1 scan.1.0 decay.1.2 scan.0.1 scan.1.1 decay.0.3
    decay.1.3 scan.0.2 scan.0.3 y.0 norm.0 scan.1.2 scan.1.3 y.1 turn.0 norm.1 turn.1 out.0 ln4.0 out.1 gates.0
    ln4.1 forget.0 gates.1 gain.0 forget.1 rows.0 gain.1 cols.0 cell.0.0 score.0.0 rows.1 cell.0.1 score.0.1
    read.0.0 cols.1 cell.1.0 read.0.1 hidden.0 score.1.0 cell.1.1 score.1.1 read.1.0 read.1.1 hidden.1 heads.0
    ln5.0 heads.1 ln5.1 up.0 up.1 next.0 down.0 ln6.0 next.1 down.1 ln6.1""".split()]
PAIRS = [("Y" if w[0] == "decay" else "H", w[1], w[2]) for w in ORDER if w[0] in ("decay", "cell")]


class Book:

    def __init__(self, known=None):
        self.total, self.marks, self.banks = {}, {}, {}
        self.known = known


class Lane:

    def __init__(self, nc, eng, who, book, sems, ctx):
        self.nc, self.eng, self.who, self.book, self.sems, self.ctx = nc, eng, who, book, sems, ctx
        self.turn, self.met, self.cur, self.last = None, {}, None, None

    def sem(self, name):
        if name not in self.sems:
            self.sems[name] = self.ctx.enter_context(self.nc.semaphore(name))
        return self.sems[name]

    def stage(self, name):
        self.cur = f"{name}_{self.who}"

    def up(self, mark=None, by=1, sem=None):
        name = sem or self.cur
        n = self.book.total[name] = self.book.total.get(name, 0) + by
        self.last = (name, n, self.turn is not None)
        if mark is not None:
            self.mark(mark)
        return self.sem(name), by

    def mark(self, mark):
        mark = mark if isinstance(mark, tuple) else (mark,)
        assert mark not in self.book.marks, mark
        self.book.marks[mark] = self.last

    def at(self, *mark):
        return self.value(self.book.marks.get(mark) or (
            self.book.known.marks[mark] if self.book.known else ("ready_pool", 1, False)))

    def own(self):
        return self.value(self.last)

    def value(self, place):
        name, n, turned = place
        n = self.met[name] = max(n, self.met.get(name, 0))
        if turned and self.turn is not None:
            total = self.book.known.total.get(name, 1) if self.book.known else 1
            n = self.turn * total + n
        return self.sem(name), n


ENGINES = ("pe", "act", "dve", "pool")


def build(nc, a, out, xmid, book, stop=9):
    known = book.known
    with ExitStack() as ctx:
        sems = {}

        def sb(name, shape, dt=F32):
            return ctx.enter_context(nc.sbuf_tensor(name, shape, dt))

        ps = ctx.enter_context(nc.psum_tensor("ps", [P, 8, 512], F32))

        def bank(mark):
            return (book.banks.get(mark) if mark in book.banks else known.banks[mark] if known else 0)

        ident = sb("ident", [P, P])
        identb = sb("identb", [P, P], BF16)
        onesq = sb("onesq", [P, P])
        le = sb("le", [P, SBLK])
        qneg = sb("qneg", [P, P], BF16)
        sbig = sb("sbig", [P, SBLK], BF16)
        hcol = sb("hcol", [P, 8])
        srow = sb("srow", [96, 8, P], BF16)
        c3 = [sb(f"c3{s}", [96, T], BF16) for s in range(NS)]
        rest, rest1 = sb("rest", [8, T]), sb("rest1", [8, T], BF16)
        pcol = sb("pcol", [P, 4])
        pint = sb("pint", [P, 1], I32)
        eps = sb("eps", [P, 4])
        zrow = sb("zrow", [8, T])
        tick = sb("tick", [1, 2])
        onesb = sb("onesb", [1, P], BF16)
        xT = [sb(f"xT{s}", [P, KC, T]) for s in range(NS)]
        xin = [sb(f"xin{s}", [P, TT, C]) for s in range(NS)]
        cT = [sb(f"cT{s}", [P, KC, T]) for s in range(NS)]
        z = [sb(f"z{s}", [P, TT, C]) for s in range(NS)]
        zT = [sb(f"zT{s}", [P, KC, T]) for s in range(NS)]
        z2 = [sb(f"z2{s}", [P, TT, C]) for s in range(NS)]
        st6 = [sb(f"st6{s}", [P, 8, 6]) for s in range(NS)]
        mv = [sb(f"mv{s}", [P, 8, 2]) for s in range(NS)]
        lnv = [sb(f"lnv{s}", [P, 8]) for s in range(NS)]
        rstd = [sb(f"rstd{s}", [P, 8]) for s in range(NS)]
        ARENA = 2 * AM * T + TT * AH * (AD + 1) + TT * INNER
        arena = [sb(f"arena{s}", [P, ARENA]) for s in range(NS)]
        small = [sb(f"small{s}", [P, 256]) for s in range(NS)]
        WORDS = 21536
        wts = sb("wts", [P, WORDS])


        pq = sb("pq", [P, 12 * SBLK])
        rot = pq[:, 0:8 * T].rearrange("p (h t) -> p h t", h=8)
        nms = sb("nms", [P, 16])
        mb_ = [sb(f"mb{s}", [P, SBLK], BF16) for s in range(NS)]
        mr_ = [sb(f"mr{s}", [1, T], BF16) for s in range(NS)]
        m8_ = [sb(f"m8{s}", [1, T], U8) for s in range(NS)]

        def mbias(s):
            return mb_[s][:, :]

        def mrowb(s):
            return mr_[s][:, :]

        def m8(s):
            return m8_[s][:, :]

        def nmax(n):
            return nms[:, 2 * (n % 8):2 * (n % 8) + 2]

        def pbuf(n):
            return pq[:, (n % 6) * SBLK:(n % 6 + 1) * SBLK]

        def ptbuf(n):
            return pq[:, (6 + n % 6) * SBLK:(7 + n % 6) * SBLK]

        def atb(i):
            return pq[:, 8 * T + (i % 4) * 2 * T:8 * T + (i % 4 + 1) * 2 * T]

        def abuf(s, e):
            i = s * 2 + e // 2 % 2
            return pq[:, i * 2 * T:(i + 1) * 2 * T].rearrange("p (j t) -> p j t", j=2)

        def flat(x):
            return x.rearrange("p a b -> p (a b)") if len(x.shape) == 3 else x

        def diag(x, at=0):
            return x[:, at:at + 2 * T].rearrange("p (a b) -> p a b", b=T)[:, :, 0:P]

        def dyn(ap, b):
            return ap[bass.ds(b, 1)].rearrange("a p q r -> (a p) q r") if len(ap.shape) == 4 else ap[bass.ds(b, 1)]

        def carve_r(s):
            return carve(arena[s], [(KC, T)] * 7 + [(TT, C), (C,), (TT, C), (TT, C), (KC, T), (C,)])

        def carve_m(s):
            return carve(arena[s], [(CM, T + TAPS - 1), (CM, T), (TT, DI), (TT, DI), (TT, DI), (TT, DI), (DM, T)])[0]

        def ebuf(key, s, h):
            i = 2 * (PAIRS.index((key, s, h // 2)) % 6) + h % 2
            return pq[:, i * SBLK:(i + 1) * SBLK]

        def hTb(s):
            n = CM * (T + TAPS - 1)
            return arena[s][:, n:n + FM * T].rearrange("p (m t) -> p m t", m=FM)

        def sm(s, i, n=16):
            return small[s][:, 16 * i:16 * i + n]

        def th(x, n):
            return x.rearrange("p (t h) -> p t h", t=TT)

        def carve_a(s):
            (q, k, o, v), n = carve(arena[s], [(AM, T), (AM, T), (TT, INNER), (TT * AH * (AD + 1),)])
            return (q, k, v, o), n

        def carve(base, sizes):
            at, got = 0, []
            for shape in sizes:
                n = 1
                for d in shape:
                    n *= d
                v = base[:, at:at + n]
                if len(shape) == 2:
                    v = v.rearrange("p (a b) -> p a b", a=shape[0])
                if len(shape) == 3:
                    v = v.rearrange("p (a b c) -> p a b c", a=shape[0], b=shape[1])
                got.append(v)
                at += n
            return got, at

        (wr, wk, wv, wg, wo, wq, wkk, wvv, woo, up, down, rw, gam, bet, bo_, t1, t2, to_), n0 = carve(wts, [
            (KC, C)] * 5 + [(KC, INNER)] * 3 + [(AM, C), (NE * KC, ED), (NE, C), (KC, NR),
            (C,), (C,), (C,), (C,), (C,), (C,)])
        assert n0 <= WORDS, n0
        mix = sb("mix", [P, 4, KC])
        (win, wout, ck, cb, w1T, w2T, Arow, dtb, drow, nw, gk, gb, onorm, b1, al1, al2, al2r, b2r, spare1, tmpw), n1 = carve(wts, [
            (KC, 2 * DI + 2 * DS + MH), (DM, C), (CM, TAPS), (CM,), (KC, FH), (FM, C), (MH,), (MH,), (DI,),
            (DM,), (3 * KC, 2 * LH), (2 * LH,), (C,), (FM,), (FM,), (KC,), (C,), (C,), (2,), (2, FM, C)])
        ((cbm0, cbm1, ct0, ct1, v10, v11, dx0, dx1), n2) = carve(wts[:, n1:], [
            (SBLK,)] * 2 + [(T,)] * 2 + [(TT * LH * (LD + 1),)] * 2 + [(TT, DI)] * 2)
        assert n1 + n2 <= WORDS, (n1, n2)
        cbm, csT, v1, dxs = (cbm0, cbm1), (ct0, ct1), (v10, v11), (dx0, dx1)

        block = ctx.enter_context(nc.Block())

        def lane(eng, who):
            return Lane(nc, eng, who, book, sems, ctx)

        def gate(ln, phase):
            ln.met = {}
            count = ln.turn + 1
            for e in ENGINES:
                ln.eng.wait_ge(ln.sem(f"turned{phase}_{e}"), count)

        def loaded(ln, phase):
            ln.eng.wait_ge(ln.sem(f"turned{phase}_sp"), 1)

        def done(ln, phase):
            ln.eng.drain().then_inc(ln.sem(f"turned{phase}_{ln.who}"), 1)

        @block.tensor
        def _(eng):
            pe = lane(eng, "pe")
            mm = nc.tensor.matmul
            pending = {}
            spin, NB = [0], [6]

            def take(mark, drained, b=None):
                if b is None:
                    b = spin[0] % NB[0]
                    spin[0] += 1
                book.banks[mark] = b
                if b in pending:
                    for mark in pending[b]:
                        eng.wait_ge(*pe.at(*mark))
                pending[b] = drained if isinstance(drained, list) else [drained]
                return ps[:, b, :]

            def group(out_, pairs):
                for n, (l, r) in enumerate(pairs):
                    ins = mm(out_, l, r, start=(n == 0), stop=(n == len(pairs) - 1))
                return ins

            def transposes(s, key, src, srcmark, b=None):
                eng.wait_ge(*pe.at(*srcmark))
                o = take((key, s), (key, s, "out"), b)
                for k in range(KC):
                    for t in range(TT):
                        ins = nc.tensor.transpose(o[:, k * T + t * P:k * T + t * P + P],
                                                  src[:, t, k * P:k * P + P], ident[:, :])
                ins.then_inc(*pe.up((key, s)))

            def colproj(s, key, w, src, srcmark, m0, m1):
                for mark in srcmark:
                    eng.wait_ge(*pe.at(*mark))
                for m in range(m0, m1, 2):
                    o = take((key, s, m), (key, s, m, "out"))
                    for j in range(2):
                        ins = group(o[:, j * T:j * T + T],
                                    [(w[:, k, (m + j) * P:(m + j) * P + P], src[:, k, :]) for k in range(KC)])
                    ins.then_inc(*pe.up((key, s, m)))

            def rowproj(s, key, w, src, srcmark, b=None, kc=KC):
                for mark in srcmark:
                    eng.wait_ge(*pe.at(*mark))
                o = take((key, s), (key, s, "out"), b)
                for t in range(TT):
                    ins = group(o[:, t * C:t * C + C],
                                [(src[:, k, t * P:t * P + P], w[:, k, :]) for k in range(kc)])
                ins.then_inc(*pe.up((key, s)))

            def rwkv_proj(s):
                (xx, xr, xk, xv, xg, rT, vT, *_), _ = carve_r(s)
                colproj(s, "rT", wr, xr, [], 0, 2)
                colproj(s, "vT", wv, xv, [], 0, 2)
                rowproj(s, "k", wk, xk, [])
                rowproj(s, "g", wg, xg, [])

            def rwkv_tokens(s):
                vT = carve_r(s)[0][6]
                eng.wait_ge(*pe.at("vT", s, 0, "out"))
                o = take(("vt", s), ("vt", s, "out"))
                for m in range(KC):
                    ins = nc.tensor.transpose(o[:, m * P:m * P + P], vT[:, m, 0:P], ident[:, :])
                ins.then_inc(*pe.up(("vt", s)))

            def rwkv_state(s):
                Kc, vtok = carve_r(s)[0][8], carve_r(s)[0][12]
                eng.wait_ge(*pe.at("ks", s))
                eng.wait_ge(*pe.at("vt", s, "out"))
                o = take(("st", s), ("st", s, "out"))
                for m in range(KC):
                    ins = mm(o[:, m * P:m * P + P], vtok[:, m * P:m * P + P], Kc[:, m * P:m * P + P],
                             start=True, stop=True)
                ins.then_inc(*pe.up(("st", s)))

            def rwkv_cross(s):
                rT, st = carve_r(s)[0][5], carve_r(s)[0][0]
                eng.wait_ge(*pe.at("rT", s, 0, "out"))
                eng.wait_ge(*pe.at("st", s, "out"))
                o = take(("attn", s), ("attn", s, "out"), 6 + s)
                for m in range(KC):
                    ins = mm(o[:, C + m * P:C + m * P + P], rT[:, m, P:T], flat(st)[:, m * P:m * P + P],
                             start=(m == 0), stop=False)
                ins.then_inc(*pe.up(("cross", s)))

            def rwkv_scores(s, i):
                rT = carve_r(s)[0][5]
                eng.wait_ge(*pe.at("vh", s, 2 * i + 1))
                o = take(("A", s, i), ("A", s, i, "out"))
                for j in range(2):
                    h = 2 * i + j
                    for t in range(TT):
                        tk = slice(t * P, t * P + P)
                        ins = mm(o[:, j * T + t * P:j * T + t * P + P], rot[:, h % 8, tk], rT[:, h // 8, tk],
                                 start=True, stop=True)
                ins.then_inc(*pe.up(("A", s, i)))

            def rwkv_mix(s, i):
                Ks = carve_r(s)[0][7]
                eng.wait_ge(*pe.at("A", s, i, "out"))
                o, at = ps[:, 6 + s, :], atb(i)
                for j in range(2):
                    h = 2 * i + j
                    c = slice(h * RD, h * RD + RD)
                    mm(o[:, h * RD:h * RD + RD], at[:, j * T:j * T + P], Ks[:, 0, c], start=False, stop=False)
                    ins = mm(o[:, C + h * RD:C + h * RD + RD], at[:, j * T + P:j * T + T], Ks[:, 1, c],
                             start=False, stop=(h == RH - 1))
                ins.then_inc(*pe.up(("attn", s) if i == RH // 2 - 1 else ("mixed", s, i)))

            def attn_scores(n, s, m):
                QT, KT = carve_a(s)[0][0:2]
                eng.wait_ge(*pe.at("Q", s, m - m % 2, "out"))
                eng.wait_ge(*pe.at("K", s, m - m % 2, "out"))
                eng.wait_ge(*pe.at("bias", s))
                o = [take(("S", s, 2 * m + j), ("E", s, 2 * m + j), (n + j) % 4) for j in range(2)]
                r = [slice(64 * j, 64 * j + 64) for j in range(2)]
                for j in range(2):
                    mm(o[j][:, 0:SBLK], identb[:, :], mbias(s), start=True, stop=False)
                for j in range(2):
                    mm(o[j][:, 0:P], QT[r[j], m, 0:P], KT[r[j], m, 0:P], start=False, stop=False)
                for j in range(2):
                    ins = mm(o[j][:, P:SBLK], QT[r[j], m, P:T], KT[r[j], m, :], start=False, stop=True)
                    ins.then_inc(*pe.up(("S", s, 2 * m + j)))

            def attn_turn(n, s, h):
                eng.wait_ge(*pe.at("E", s, h))
                o = take(("PT", s, h), ("PT", s, h, "out"), 4 + n % 2)
                for j in range(3):
                    ins = nc.tensor.transpose(o[:, j * P:j * P + P], pbuf(n)[:, j * P:j * P + P], ident[:, :])
                ins.then_inc(*pe.up(("PT", s, h)))

            def attn_values(n, s, h):
                V = carve_a(s)[0][2]
                eng.wait_ge(*pe.at("PT", s, h, "out"))
                eng.wait_ge(*pe.at("V", s, "out"))
                if h % 2 == 0:
                    take(("O", s, h // 2), ("O", s, h // 2, "out"), 6 + (n // 2) % 2)
                o = ps[:, 6 + (n // 2) % 2, :]
                c0 = (h % 2) * (AD + 1)
                c1 = 2 * (AD + 1) + c0
                pt = ptbuf(n)
                v0 = V[:, h * (AD + 1):(h + 1) * (AD + 1)]
                v1 = V[:, (AH + h) * (AD + 1):(AH + h + 1) * (AD + 1)]
                mm(o[:, c0:c0 + AD + 1], pt[:, 0:P], v0, start=True, stop=True)
                mm(o[:, c1:c1 + AD + 1], pt[:, P:T], v0, start=True, stop=False)
                ins = mm(o[:, c1:c1 + AD + 1], pt[:, T:SBLK], v1, start=False, stop=True)
                ins.then_inc(*pe.up(("pv", s, h)))
                if h % 2:
                    pe.mark(("O", s, h // 2))

            def val_proj(s):
                eng.wait_ge(*pe.at("cT", s))
                for t in range(TT):
                    for j in range(2):
                        o = take(("Vp", s, t, j), ("Vp", s, t, j, "out"))
                        ins = group(o[:, :], [(cT[s][:, k, t * P:t * P + P], wvv[:, k, j * 512:j * 512 + 512])
                                              for k in range(KC)])
                        ins.then_inc(*pe.up(("Vp", s, t, j)))

            def turn_out(s, m, b=None):
                O = carve_a(s)[0][3]
                eng.wait_ge(*pe.at("O", s, m + 1, "out"))
                o = take(("OT", s, m), ("OT", s, m, "out"), b)
                for j in range(2):
                    for t in range(TT):
                        ins = nc.tensor.transpose(o[:, j * T + t * P:j * T + t * P + P],
                                                  O[:, t, (m + j) * P:(m + j) * P + P], ident[:, :])
                ins.then_inc(*pe.up(("OT", s, m)))

            def out_proj(s, b=None):
                rowproj(s, "xo", woo, carve_a(s)[0][0], [("OT", s, AM - 2, "out")], b, kc=AM)

            def router(s, b=None):
                eng.wait_ge(*pe.at("zT2", s, "out"))
                o = take(("route", s), ("route", s, "out"), b)
                for t in range(TT):
                    ins = group(o[:, t * NR:t * NR + NR],
                                [(zT[s][:, k, t * P:t * P + P], rw[:, k, :]) for k in range(KC)])
                ins.then_inc(*pe.up(("route", s)))

            def expert_up(s, e):
                o = take(("up", s, e), ("up", s, e, "out"))
                for j in range(2):
                    ins = group(o[:, j * T:j * T + T],
                                [(up[:, (e + j) * KC + k, :], zT[s][:, k, :]) for k in range(KC)])
                ins.then_inc(*pe.up(("up", s, e)))

            def expert_down(s, e):
                eng.wait_ge(*pe.at("up", s, e, "out"))
                act = abuf(s, e)
                for j in range(2):
                    if e + j < NSH:
                        if j == 0:
                            take(("shared", s), ("shared", s, "out"))
                        o = ps[:, bank(("shared", s)), :]
                        for t in range(TT):
                            if j == 0:
                                continue
                            for jj in range(NSH):
                                ins = mm(o[:, t * C:t * C + C], act[:, jj, t * P:t * P + P], down[:, jj, :],
                                         start=(jj == 0), stop=(jj == NSH - 1))
                        if j == NSH - 1:
                            ins.then_inc(*pe.up(("shared", s)))
                        continue
                    o = take(("dn", s, e + j), ("dn", s, e + j, "out"))
                    for t in range(TT):
                        ins = mm(o[:, t * C:t * C + C], act[:, j, t * P:t * P + P], down[:, e + j, :],
                                 start=True, stop=True)
                    ins.then_inc(*pe.up(("dn", s, e + j)))

            done(pe, 0)
            loaded(pe, 0)
            with eng.Fori(0, TURNS) as g:
                pe.turn = g
                gate(pe, 0)
                pe.stage("rwkv")
                for f in (rwkv_proj, rwkv_tokens, rwkv_state, rwkv_cross):
                    for s in range(NS):
                        f(s)
                for s in range(NS):
                    for i in range(RH // 2 + 2):
                        if i < RH // 2:
                            rwkv_scores(s, i)
                        if i >= 2:
                            rwkv_mix(s, i - 2)
                transposes(0, "agT", carve_r(0)[0][10], ("ag", 0))
                transposes(1, "agT", carve_r(1)[0][10], ("ag", 1))
                for s in range(NS):
                    rowproj(s, "y", wo, carve_r(s)[0][11], [("agT", s, "out")])
                pe.stage("attn")
                eng.wait_ge(*pe.at("rest"))
                for s in range(NS):
                    colproj(s, "K", wkk, cT[s], [("cT", s), ("y", s)], 0, AM)
                    val_proj(s)
                for s in range(NS):
                    o = take(("biasp", s), ("bias", s))
                    eng.wait_ge(*pe.at("mrow", s))
                    mm(o[:, 0:P], onesb[:, :], mrowb(s)[:, 0:P], start=True, stop=True)
                    ins = mm(o[:, P:SBLK], onesb[:, :], mrowb(s)[:, :], start=True, stop=True)
                    ins.then_inc(*pe.up(("biasp", s)))
                for s in range(NS):
                    transposes(s, "zT1", z[s], ("z1", s))
                for s in range(NS):
                    colproj(s, "Q", wq, zT[s], [("zT1", s, "out")], 0, AM)
                for n in range(len(UNITS) + 5):
                    if n < len(UNITS) and n % 2 == 0:
                        attn_scores(n, UNITS[n][0], UNITS[n][1] // 2)
                    if 0 <= n - 3 < len(UNITS):
                        attn_turn(n - 3, *UNITS[n - 3])
                    if 0 <= n - 5 < len(UNITS):
                        attn_values(n - 5, *UNITS[n - 5])
                    if OUT0 <= n < OUT0 + AM // 2:
                        turn_out(0, 2 * (n - OUT0), 4 + n % 2)
                    if n == OUT0 + AM // 2:
                        out_proj(0, 4 + n % 2)
                    if n == OUT0 + 7:
                        transposes(0, "zT2", z2[0], ("z2", 0), 4 + n % 2)
                    if n == OUT0 + 9:
                        router(0, 4 + n % 2)
                pe.stage("moe")
                for s in range(NS):
                    for e in range(0, NE + 2, 2):
                        if e < NE:
                            expert_up(s, e)
                        if e >= 2:
                            expert_down(s, e - 2)
                        if s == 0:
                            if e == 0:
                                for m in range(0, AM, 2):
                                    turn_out(1, m)
                            if e == 2:
                                out_proj(1)
                            if e == 8:
                                transposes(1, "zT2", z2[1], ("z2", 1))
                            if e == 12:
                                router(1)
                done(pe, 0)
                pe.turn, pe.met = None, {}
                pending.clear()
            if stop <= 3:
                return

            pe.stage("setup1")
            for d in range(2):
                src, dst, rows, colsn = (tmpw[:, 0], w1T, FM, KC) if d == 0 else (tmpw[:, 1], w2T, KC, FM)
                srcv = src if d == 0 else src.rearrange("p m c -> p (m c)").rearrange("p (m c) -> p m c", m=KC)
                eng.wait_ge(*pe.at("signs", d))
                for cc in range(colsn):
                    for r0 in range(0, rows, 4):
                        n_ = min(4, rows - r0)
                        o = take(("wT", d, cc, r0), ("wT", d, cc, r0, "out"))
                        for j in range(n_):
                            ins = nc.tensor.transpose(o[:, j * P:j * P + P], srcv[:, r0 + j, cc * P:cc * P + P],
                                                      ident[:, :])
                        ins.then_inc(*pe.up(("wT", d, cc, r0)))
            eng.wait_ge(*pe.at("al2diag"))
            o = take("al2row", ("al2row_out",))
            for j in range(KC):
                ins = mm(o[:, j * P:j * P + P], onesq[:, :], dxs[0][:, 0, j * P:j * P + P], start=True, stop=True)
            ins.then_inc(*pe.up("al2row"))
            eng.wait_ge(*pe.at("al2row_out"))
            eng.wait_ge(*pe.at("wT", 1, FM - 1, 0, "out"))
            for s in range(NS):
                o = take(("zTa0", s), ("zTa0", s, "out"))
                eng.wait_ge(*pe.at("first_x2", s))
                for k in range(KC):
                    for t in range(TT):
                        ins = nc.tensor.transpose(o[:, k * T + t * P:k * T + t * P + P],
                                                  xin[s][:, t, k * P:k * P + P], ident[:, :])
                ins.then_inc(*pe.up(("zTa0", s)))
            done(pe, 1)
            loaded(pe, 1)
            pending.clear()

            def cumsum(s, key, src, n):
                o = take((key, s), (key, s, "out"))
                mm(o[:, 0:n], le[:, 0:P], src[:, 0, :], start=True, stop=True)
                mm(o[:, n:2 * n], onesq[:, :], src[:, 0, :], start=True, stop=False)
                mm(o[:, n:2 * n], le[:, 0:P], src[:, 1, :], start=False, stop=True).then_inc(*pe.up((key, s)))

            def rows_of(s, key, src, n):
                o = take((key, s), (key, s, "out"))
                for t in range(TT):
                    ins = mm(o[0:n, t * P:t * P + P], src[:, t, :], ident[:, :], start=True, stop=True)
                ins.then_inc(*pe.up((key, s)))

            def mamba_dt(s):
                o = take(("dt", s), ("dt", s, "out"))
                for t in range(TT):
                    ins = group(o[:, t * MH:t * MH + MH],
                                [(xT[s][:, k, t * P:t * P + P], win[:, k, 2 * DI + 2 * DS:]) for k in range(KC)])
                ins.then_inc(*pe.up(("dt", s)))

            def mamba_in(s):
                colproj(s, "xbc", win[:, :, DI:2 * DI + 2 * DS], xT[s], [], 0, CM)
                for t in range(TT):
                    o = take(("zg", s, t), ("zg", s, t, "out"))
                    ins = group(o, [(xT[s][:, k, t * P:t * P + P], win[:, k, 0:DI]) for k in range(KC)])
                    ins.then_inc(*pe.up(("zg", s, t)))

            def mamba_sums(s):
                eng.wait_ge(*pe.at("dA", s))
                cumsum(s, "cs", th(sm(s, 3), MH), MH)
                eng.wait_ge(*pe.at("cs", s, "out"))
                rows_of(s, "csr", th(sm(s, 4), MH), MH)

            def mamba_mid(s):
                xpad, xb = carve_m(s)[0:2]
                eng.wait_ge(*pe.at("conv", s, CM - 1))
                Bt, Ct = xb[:, DM, :], xb[:, DM + 1, :]
                o = take(("CB", s), ("CB", s, "out"))
                mm(o[:, 0:T], Bt[:, 0:P], Ct, start=True, stop=True)
                mm(o[:, T:SBLK], Bt[:, P:T], Ct[:, P:T], start=True, stop=True).then_inc(*pe.up(("CB", s)))
                for t in range(TT):
                    o = take(("xs", s, t), ("xs", s, t, "out"))
                    for m in range(DM):
                        ins = nc.tensor.transpose(o[:, m * P:m * P + P], xb[:, m, t * P:t * P + P], ident[:, :])
                    ins.then_inc(*pe.up(("xs", s, t)))

            def spread(s, key, h):
                o = take((key, s, h), (key, s, h, "out"))
                mm(o[:, 0:SBLK], identb[:, :], sbig[:, :], start=True, stop=False)
                mm(o[:, 0:T], srow[:, h, :], c3[s][:, :], start=False, stop=False)
                ins = mm(o[:, T:SBLK], srow[:, h, :], c3[s][:, P:T], start=False, stop=True)
                ins.then_inc(*pe.up((key, s, h)))

            def weighted(s, key, val, wid, h, heads):
                for t in range(TT):
                    if h == 0:
                        take((key, s, t), (key, s, t, "out"), 6 - 2 * s + t)
                y0, y1 = (ps[:, 6 - 2 * s + t, h * wid:(h + 1) * wid] for t in range(TT))
                e = ebuf(key, s, h)
                mm(y0, e[:, 0:P], val(0, h), start=True, stop=True)
                mm(y1, e[:, P:T], val(0, h), start=True, stop=False)
                ins = mm(y1, e[:, T:SBLK], val(1, h), start=False, stop=True)
                ins.then_inc(*pe.up((key, s, "head", h)))
                if h == heads - 1:
                    for t in range(TT):
                        pe.mark((key, s, t))

            def mamba_decay(s, pr):
                eng.wait_ge(*pe.at("csr3", s))
                for h in (2 * pr, 2 * pr + 1):
                    spread(s, "csB", h)

            def mamba_scan(s, pr):
                eng.wait_ge(*pe.at("M", s, pr))
                eng.wait_ge(*pe.at("xdt", s))
                xdt = carve_m(s)[4]
                for h in (2 * pr, 2 * pr + 1):
                    weighted(s, "Y", lambda t, h: xdt[:, t, h * MD:h * MD + MD], MD, h, MH)

            def mamba_turn(s):
                y = carve_m(s)[5]
                eng.wait_ge(*pe.at("yn", s))
                for m in range(0, DM, 2):
                    o = take(("yT", s, m), ("yT", s, m, "out"))
                    for j in range(2):
                        for t in range(TT):
                            ins = nc.tensor.transpose(o[:, j * T + t * P:j * T + t * P + P],
                                                      y[:, t, (m + j) * P:(m + j) * P + P], ident[:, :])
                    ins.then_inc(*pe.up(("yT", s, m)))

            def mamba_out(s):
                rowproj(s, "mo", wout, carve_m(s)[6], [("yT", s, DM - 2, "out")], kc=DM)

            def mlstm_gates(s):
                transposes(s, "zTb", z[s], ("z4", s))
                eng.wait_ge(*pe.at("zTb", s, "out"))
                eng.wait_ge(*pe.at("cT2", s))
                o = take(("gt", s), ("gt", s, "out"))
                for t in range(TT):
                    tk = slice(t * P, t * P + P)
                    ins = group(o[:, t * 8:t * 8 + 8],
                                [(zT[s][:, k, tk], gk[:, k, :]) for k in range(KC)] +
                                [(cT[s][:, k, tk], gk[:, (1 + i) * KC + k, :]) for i in range(2) for k in range(KC)])
                ins.then_inc(*pe.up(("gt", s)))

            def mlstm_sums(s):
                eng.wait_ge(*pe.at("lf", s))
                cumsum(s, "cs2", th(sm(s, 5, 8), LH), LH)

            def mlstm_rows(s):
                eng.wait_ge(*pe.at("a", s))
                rows_of(s, "ar", th(sm(s, 6, 8), LH), LH)

            def mlstm_cols(s):
                eng.wait_ge(*pe.at("mt", s))
                o = take(("mtok", s), ("mtok", s, "out"))
                for t in range(TT):
                    ins = mm(o[:, t * LH:t * LH + LH], csT[s][0:LH, t * P:t * P + P], ident[0:LH, 0:LH],
                             start=True, stop=True)
                ins.then_inc(*pe.up(("mtok", s)))

            def mlstm_cell(s, pr):
                eng.wait_ge(*pe.at("mt3", s))
                for h in (2 * pr, 2 * pr + 1):
                    spread(s, "MB", h)

            def mlstm_score(s, pr):
                for h in (2 * pr, 2 * pr + 1):
                    m, r = h // 2, slice(LD * (h % 2), LD * (h % 2) + LD)
                    o = take(("qk", s, h), ("qk", s, h, "out"))
                    mm(o[:, 0:T], cT[s][r, m, 0:P], zT[s][r, m, :], start=True, stop=True)
                    ins = mm(o[:, T:SBLK], cT[s][r, m, P:T], zT[s][r, m, P:T], start=True, stop=True)
                    ins.then_inc(*pe.up(("qk", s, h)))

            def mlstm_read(s, pr):
                eng.wait_ge(*pe.at("C", s, pr))
                eng.wait_ge(*pe.at("v1", s))
                for h in (2 * pr, 2 * pr + 1):
                    weighted(s, "H", lambda t, h: v1[s][:, (t * LH + h) * (LD + 1):(t * LH + h + 1) * (LD + 1)],
                             LD + 1, h, LH)

            with eng.Fori(0, TURNS) as g:
                pe.turn = g
                gate(pe, 1)
                NB[0] = 4
                spin[0] = 0
                pe.stage("mamba")
                for f in (mamba_dt, mamba_in, mamba_sums, mamba_mid):
                    for s in range(NS):
                        f(s)
                for step, s, *pr in ORDER:
                    if step == "decay":
                        mamba_decay(s, *pr)
                    if step == "scan":
                        mamba_scan(s, *pr)
                    if step == "turn":
                        mamba_turn(s)
                    if step == "out":
                        mamba_out(s)
                    if step == "gates":
                        mlstm_gates(s)
                    if step == "gain":
                        mlstm_sums(s)
                    if step == "rows":
                        mlstm_rows(s)
                    if step == "cols":
                        mlstm_cols(s)
                    if step == "cell":
                        mlstm_cell(s, *pr)
                    if step == "score":
                        mlstm_score(s, *pr)
                    if step == "read":
                        mlstm_read(s, *pr)
                    if step == "up":
                        transposes(s, "zTc", z2[s], ("z5", s))
                        colproj(s, "f1", w1T, zT[s], [("zTc", s, "out")], 0, FM)
                    if step == "next":
                        transposes(s, "zTa", xin[s], ("xin2", s))
                    if step == "down":
                        rowproj(s, "f2", w2T, hTb(s), [("f1", s, FM - 2, "out")], kc=FM)
                done(pe, 1)
                pe.turn, pe.met = None, {}

        @block.scalar
        def _(eng):
            act = lane(eng, "act")
            A = nc.scalar.activation

            def psv(mark):
                return ps[:, bank(mark), :]

            def ln_rstd(s, key, n, e=0):
                eng.wait_ge(*act.at(key, s, "mv"))
                A(lnv[s][:, 0:n], mv[s][:, 0:n, 1], ACT.Ln, bias=eps[:, e:e + 1]).then_inc(*act.up())
                eng.wait_ge(*act.own())
                A(rstd[s][:, 0:n], lnv[s][:, 0:n], ACT.Exp, scale=-0.5).then_inc(*act.up((key, s, "rstd")))

            def evict(mark, dst, n=512, outmark=None, scale=1.0):
                eng.wait_ge(*act.at(*mark))
                A(dst, psv(mark)[:, 0:n], ACT.Copy, scale=scale).then_inc(*act.up(outmark or mark + ("out",)))

            act.stage("ready")
            eng.wait_ge(*act.at("lam"))
            A(t1, t1, ACT.Exp).then_inc(*act.up())
            eng.wait_ge(*act.own())
            A(t2, t1, ACT.Exp, scale=pcol[:, 2:3]).then_inc(*act.up())
            A(to_, t1, ACT.Exp, scale=pcol[:, 3:4]).then_inc(*act.up())
            eng.wait_ge(*act.own())
            A(t1, t1, ACT.Exp, scale=pcol[:, 1:2]).then_inc(*act.up())
            nc.scalar.preload_act_table_set("natural_log_exp_and_others")
            done(act, 0)
            loaded(act, 0)

            def rwkv(s):
                (xx, xr, xk, xv, xg, rT, vT, Ks, Kc, g, ag, agT, vtok), _ = carve_r(s)
                evict(("rT", s, 0), flat(rT))
                eng.wait_ge(*act.at("g", s))
                A(flat(g), psv(("g", s)), ACT.Exp, scale=-1.0).then_inc(*act.up(("g", s, "out")))

            def attn_exp(n, s, h):
                eng.wait_ge(*act.at("max", s, h))
                src, nm = psv(("S", s, h)), nmax(n)
                pb = pbuf(n)
                if n >= 6:
                    eng.wait_ge(*act.at("PT", *UNITS[n - 6]))
                A(pb[:, 0:P], src[:, 0:P], ACT.Exp, bias=nm[:, 0:1]).then_inc(*act.up())
                A(pb[:, P:SBLK], src[:, P:SBLK], ACT.Exp, bias=nm[:, 1:2]).then_inc(*act.up(("E", s, h)))

            def gates(s):
                eng.wait_ge(*act.at("logit", s))
                A(small[s][:, 0:TT * NR], small[s][:, 0:TT * NR], ACT.Exp).then_inc(*act.up(("prob", s)))

            def attn_pt(n, s, h):
                if n % 2 == 0:
                    if n >= 6:
                        eng.wait_ge(*act.at("pv", *UNITS[n - 6]))
                    evict(("PT", s, h), ptbuf(n), SBLK)

            with eng.Fori(0, TURNS) as g:
                act.turn = g
                gate(act, 0)
                act.stage("rwkv")
                for s in range(NS):
                    rwkv(s)
                for s in range(NS):
                    evict(("vt", s), carve_r(s)[0][12], C)
                for s in range(NS):
                    vT = carve_r(s)[0][6]
                    eng.wait_ge(*act.at("vT", s, 0, "out"))
                    for h in range(RH):
                        if h >= 8:
                            eng.wait_ge(*act.at("A", s, (h - 8) // 2))
                        elif s:
                            eng.wait_ge(*act.at("A", s - 1, (h + 8) // 2))
                        A(rot[:, h % 8, :], vT[:, h // 8, :], ACT.Copy, scale=hcol[:, h % 8:h % 8 + 1]).then_inc(
                            *act.up(("vh", s, h)))
                    gt = flat(carve_r(s)[0][9])
                    A(gt, gt, ACT.Ln, bias=eps[:, 2:3]).then_inc(*act.up())
                    eng.wait_ge(*act.own())
                    A(gt, gt, ACT.Exp, scale=-1.0).then_inc(*act.up(("gate", s)))
                for s in range(NS):
                    evict(("agT", s), flat(carve_r(s)[0][11]))
                for s in range(NS):
                    ln_rstd(s, "ln_y", TT)
                act.stage("attn")
                for s in range(NS):
                    QT, KT, V, O = carve_a(s)[0]
                    for m in range(0, AM, 2):
                        evict(("K", s, m), flat(KT[:, m:m + 2, :]))
                    if s == 0:
                        for s_ in range(NS):
                            ln_rstd(s_, "ln_1", TT)
                    for t in range(TT):
                        for j in range(2):
                            eng.wait_ge(*act.at("Vp", s, t, j))
                            dst = V[:, (t * AH + j * 8) * (AD + 1):(t * AH + j * 8 + 8) * (AD + 1)]
                            A(dst.rearrange("p (h d) -> p h d", h=8)[:, :, 0:AD],
                              psv(("Vp", s, t, j)).rearrange("p (h d) -> p h d", h=8), ACT.Copy).then_inc(
                                *act.up(("Vp", s, t, j, "out")))
                    act.mark(("V", s, "out"))
                for s in range(NS):
                    evict(("zT1", s), flat(zT[s]))
                for s in range(NS):
                    QT = carve_a(s)[0][0]
                    for m in range(0, AM, 2):
                        evict(("Q", s, m), flat(QT[:, m:m + 2, :]), scale=AD ** -0.5)
                for n in range(len(UNITS) + 4):
                    if n < len(UNITS):
                        attn_exp(n, *UNITS[n])
                    if 0 <= n - 3 < len(UNITS):
                        attn_pt(n - 3, *UNITS[n - 3])
                    if OUT0 <= n < OUT0 + AM // 2:
                        m = 2 * (n - OUT0)
                        evict(("OT", 0, m), flat(carve_a(0)[0][0][:, m:m + 2, :]))
                    if n == OUT0 + 5:
                        ln_rstd(0, "ln_2", TT)
                    if n == OUT0 + 7:
                        evict(("zT2", 0), flat(zT[0]))
                    if n == OUT0 + 10:
                        gates(0)
                act.stage("moe")
                for s in range(NS):
                    for e in range(0, NE, 2):
                        eng.wait_ge(*act.at("up", s, e))
                        if e >= 4:
                            eng.wait_ge(*act.at(*(("dn", s, e - 3) if e > 4 else ("shared", s))))
                        A(flat(abuf(s, e)), psv(("up", s, e)), ACT.Gelu).then_inc(*act.up(("up", s, e, "out")))
                        if s == 0:
                            if e == 0:
                                for m in range(0, AM, 2):
                                    evict(("OT", 1, m), flat(carve_a(1)[0][0][:, m:m + 2, :]))
                            if e == 4:
                                ln_rstd(1, "ln_2", TT)
                            if e == 8:
                                evict(("zT2", 1), flat(zT[1]))
                            if e == 12:
                                gates(1)
                done(act, 0)
                nc.scalar.preload_act_table_set("natural_log_exp_and_others")
                for s in range(NS):
                    ln_rstd(s, "ln_3", TT)
                act.turn, act.met = None, {}
            if stop <= 3:
                return

            act.stage("setup1")
            eng.wait_ge(*act.at("w12"))
            for d in range(2):
                eng.wait_ge(*act.at("alpha", d))
                A(flat(tmpw[:, d]), flat(tmpw[:, d]), ACT.Sign).then_inc(*act.up(("signs", d)))
            eng.wait_ge(*act.at("p2rows"))
            A(Arow, Arow, ACT.Exp).then_inc(*act.up())
            for d in range(2):
                rows, colsn, dst = (FM, KC, w1T) if d == 0 else (KC, FM, w2T)
                for cc in range(colsn):
                    for r0 in range(0, rows, 4):
                        n_ = min(4, rows - r0)
                        evict(("wT", d, cc, r0), dst[:, cc, r0 * P:(r0 + n_) * P], n_ * P)
            for s in range(NS):
                evict(("zTa0", s), flat(xT[s]))
            done(act, 1)
            loaded(act, 1)

            def softplus(s, key, x, e, l):
                eng.wait_ge(*act.at(key, s, "x"))
                A(e, x, ACT.Abs).then_inc(*act.up())
                eng.wait_ge(*act.own())
                A(e, e, ACT.Exp, scale=-1.0).then_inc(*act.up())
                eng.wait_ge(*act.own())
                A(l, e, ACT.Ln, bias=eps[:, 2:3]).then_inc(*act.up((key, s, "log")))

            def decays(key, outkey, ccol, wkey, s, pr):
                n = PAIRS.index((wkey, s, pr))
                if n >= 6:
                    k6, s6, p6 = PAIRS[n - 6]
                    eng.wait_ge(*act.at(k6, s6, "head", 2 * p6 + 1))
                for h in (2 * pr, 2 * pr + 1):
                    e = ebuf(wkey, s, h)
                    eng.wait_ge(*act.at(key, s, h))
                    src, cc = psv((key, s, h)), ccol
                    A(e[:, 0:T], src[:, 0:T], ACT.Exp, scale=-1.0, bias=cc[:, 0, h:h + 1]).then_inc(*act.up())
                    A(e[:, T:SBLK], src[:, T:SBLK], ACT.Exp, scale=-1.0, bias=cc[:, 1, h:h + 1]).then_inc(
                        *act.up((key, s, h, "out")))
                act.mark((outkey, s, pr))

            with eng.Fori(0, TURNS) as g:
                act.turn = g
                gate(act, 1)
                act.stage("mamba")
                for s in range(NS):
                    softplus(s, "dtx", sm(s, 0), sm(s, 1), sm(s, 2))
                nc.scalar.preload_act_table_set("silu_and_others")
                for s in range(NS):
                    xpad, xb, sz, xs, xdt, y, yT = carve_m(s)
                    for m in range(0, CM, 2):
                        eng.wait_ge(*act.at("xbc", s, m))
                        src = psv(("xbc", s, m)).rearrange("p (a t) -> p a t", a=2)
                        A(xpad[:, m:m + 2, TAPS - 1:], src, ACT.Copy).then_inc(*act.up(("xpad", s, m)))
                        for j in range(2):
                            A(xb[:, m + j, :], src[:, j, :], ACT.Identity, scale=ck[:, m + j, TAPS - 1:TAPS],
                                  bias=cb[:, m + j:m + j + 1]).then_inc(*act.up(("tap3", s, m + j)))
                        act.mark(("xbc", s, m, "out"))
                    for t in range(TT):
                        eng.wait_ge(*act.at("zg", s, t))
                        A(sz[:, t, :], psv(("zg", s, t)), ACT.Silu).then_inc(*act.up(("zg", s, t, "out")))
                for s in range(NS):
                    xb = carve_m(s)[1]
                    for m in range(CM):
                        eng.wait_ge(*act.at("taps", s, m))
                        A(xb[:, m, :], xb[:, m, :], ACT.Silu).then_inc(*act.up(("conv", s, m)))
                nc.scalar.preload_act_table_set("natural_log_exp_and_others")
                for s in range(NS):
                    xs = carve_m(s)[3]
                    for t in range(TT):
                        evict(("xs", s, t), xs[:, t, :])
                loaded_set = ["natural_log_exp_and_others"]

                def tables(name):
                    if loaded_set[0] != name:
                        nc.scalar.preload_act_table_set(name)
                        loaded_set[0] = name

                for step, s, *pr in ORDER:
                    if step == "decay":
                        decays("csB", "Ex", th(sm(s, 4), MH), "Y", s, *pr)
                    if step == "y":
                        y, junk = carve_m(s)[5], carve_m(s)[4]
                        for t in range(TT):
                            eng.wait_ge(*act.at("y", s, t))
                            A(junk[:, t, :], y[:, t, :], ACT.Square, accum_out=sm(s, 7)[:, t:t + 1]).then_inc(*act.up())
                        eng.wait_ge(*act.own())
                        A(sm(s, 7)[:, 0:TT], sm(s, 7)[:, 0:TT], ACT.Ln, scale=1.0 / DI, bias=eps[:, 0:1]).then_inc(
                            *act.up())
                        eng.wait_ge(*act.own())
                        A(sm(s, 7)[:, 0:TT], sm(s, 7)[:, 0:TT], ACT.Exp, scale=-0.5).then_inc(*act.up(("yr", s)))
                    if step == "turn":
                        yT = carve_m(s)[6]
                        for m in range(0, DM, 2):
                            eng.wait_ge(*act.at("yT", s, m))
                            for j in range(2):
                                A(yT[:, m + j, :], psv(("yT", s, m))[:, j * T:j * T + T], ACT.Copy,
                                  scale=nw[:, m + j:m + j + 1]).then_inc(
                                    *act.up(("yT", s, m, "out") if j else None))
                    if step == "ln4":
                        ln_rstd(s, "ln_4", TT)
                    if step == "gates":
                        evict(("zTb", s), flat(zT[s]))
                    if step == "forget":
                        softplus(s, "fg", sm(s, 1, 8), sm(s, 2, 8), sm(s, 3, 8))
                    if step == "cols":
                        eng.wait_ge(*act.at("mc", s))
                        A(sm(s, 8, 8), sm(s, 8, 8), ACT.Exp, scale=-1.0).then_inc(*act.up(("nrm", s)))
                    if step == "cell":
                        tables("natural_log_exp_and_others")
                        decays("MB", "Dx", th(sm(s, 6, 8), LH), "H", s, *pr)
                    if step == "heads":
                        tables("natural_log_exp_and_others")
                        ln_rstd(s, "ln_h", TT * LH, 1)
                    if step == "ln5":
                        tables("natural_log_exp_and_others")
                        ln_rstd(s, "ln_5", TT)
                    if step == "up":
                        evict(("zTc", s), flat(zT[s]))
                        tables("gelu_and_others")
                        for m in range(0, FM, 2):
                            eng.wait_ge(*act.at("f1", s, m))
                            for j in range(2):
                                A(hTb(s)[:, m + j, :], psv(("f1", s, m))[:, j * T:j * T + T], ACT.Gelu,
                                  scale=al1[:, m + j:m + j + 1], bias=b1[:, m + j:m + j + 1]).then_inc(
                                    *act.up(("f1", s, m, "out") if j else None))
                    if step == "next":
                        evict(("zTa", s), flat(xT[s]))
                        if s == NS - 1:
                            done(act, 1)
                    if step == "ln6":
                        tables("natural_log_exp_and_others")
                        ln_rstd(s, "ln_6", TT)
                act.turn, act.met = None, {}

        @block.vector
        def _(eng):
            v = lane(eng, "dve")
            V_ = nc.vector

            def psv(mark):
                return ps[:, bank(mark), :]

            def settle():
                eng.wait_ge(*v.own())
                V_.tensor_copy(tick[:, 1:2], tick[:, 0:1]).then_inc(*v.up())

            def ln_stats(s, key, src, n=TT):
                for t in range(n):
                    V_.bn_stats(st6[s][:, t, :], src[:, t, :]).then_inc(*v.up())
                settle()
                for t in range(n):
                    V_.bn_aggr(mv[s][:, t, :], st6[s][:, t, :]).then_inc(*v.up((key, s, "mv") if t == n - 1 else None))

            def ln_apply(s, key, src, dst, mark=None):
                eng.wait_ge(*v.at(key, s, "rstd"))
                for t in range(TT):
                    V_.tensor_scalar(dst[:, t, :], src[:, t, :], mv[s][:, t, 0:1], rstd[s][:, t:t + 1],
                                       ALU.subtract, ALU.mult).then_inc(*v.up(mark if t == TT - 1 else None))

            v.stage("ready")
            for s in range(NS):
                V = carve_a(s)[0][2]
                V_.memset(V, 1.0).then_inc(*v.up())
            V_.memset(zrow[:, :], 0.0).then_inc(*v.up())
            V_.memset(tick[:, :], 0.0).then_inc(*v.up())
            for s in range(NS):
                V_.memset(c3[s][:, :], 0.0).then_inc(*v.up())

            def mixes(s):
                (xx, xr, xk, xv, xg, *_), _ = carve_r(s)
                x = xT[s]
                V_.tensor_tensor(xx[:, :, 1:T], x[:, :, 0:T - 1], x[:, :, 1:T], ALU.subtract).then_inc(*v.up())
                V_.tensor_tensor(xx[:, :, 0:1], x[:, :, 1:2], x[:, :, 0:1], ALU.subtract).then_inc(*v.up())
                eng.wait_ge(*v.own())
                for i, (n, dst) in enumerate((("r", xr), ("v", xv), ("k", xk), ("g", xg))):
                    for k in range(KC):
                        V_.scalar_tensor_tensor(dst[:, k, :], xx[:, k, :], mix[:, i, k:k + 1], x[:, k, :],
                                                  ALU.mult, ALU.add).then_inc(*v.up())

            def rwkv_evict(s):
                (xx, xr, xk, xv, xg, rT, vT, Ks, Kc, g, ag, agT, vtok), _ = carve_r(s)
                eng.wait_ge(*v.at("vT", s, 0))
                V_.tensor_copy(flat(vT), psv(("vT", s, 0))).then_inc(*v.up(("vT", s, 0, "out")))
                eng.wait_ge(*v.at("k", s))
                kk = psv(("k", s)).rearrange("p (t c) -> p t c", t=TT)
                V_.tensor_tensor(Kc, kk[:, 0, :], t2, ALU.mult).then_inc(*v.up())
                V_.tensor_tensor(Ks, kk, t1.unsqueeze(1).to_broadcast([P, TT, C]), ALU.mult).then_inc(*v.up(("k", s, "out")))
                v.mark(("ks", s))

            def rwkv_state(s):
                st = flat(carve_r(s)[0][0])
                eng.wait_ge(*v.at("st", s))
                for m in range(KC):
                    V_.tensor_tensor(st[:, m * P:m * P + P].rearrange("p (h d) -> p h d", h=8),
                                     psv(("st", s))[:, m * P:m * P + P].rearrange("p (h d) -> p h d", h=8),
                                     hcol[:, :].unsqueeze(2).to_broadcast([P, 8, RD]), ALU.mult).then_inc(
                        *v.up(("st", s, "out") if m == KC - 1 else None))

            def rwkv_heads(s):
                for i in range(RH // 2):
                    eng.wait_ge(*v.at("A", s, i))
                    if i >= 4:
                        eng.wait_ge(*v.at("mixed", s, i - 4))
                    elif s:
                        eng.wait_ge(*v.at(*(("mixed", s - 1, RH // 2 - 4 + i) if i < 3 else ("attn", s - 1))))
                    V_.tensor_tensor(atb(i).rearrange("p (b t) -> p b t", b=4),
                                     psv(("A", s, i)).rearrange("p (b t) -> p b t", b=4),
                                     le[:, 0:P].unsqueeze(1).to_broadcast([P, 4, P]), ALU.mult).then_inc(
                        *v.up(("A", s, i, "out")))

            def rwkv_out(s):
                (xx, xr, xk, xv, xg, rT, vT, Ks, Kc, g, ag, agT, vtok), _ = carve_r(s)
                eng.wait_ge(*v.at("attn", s))
                eng.wait_ge(*v.at("gate", s))
                V_.tensor_tensor(ag, psv(("attn", s)).rearrange("p (t c) -> p t c", t=TT),
                                   to_.unsqueeze(1).to_broadcast([P, TT, C]), ALU.mult).then_inc(*v.up(("attn", s, "out")))
                eng.wait_ge(*v.own())
                V_.tensor_tensor(flat(ag), flat(ag), flat(g), ALU.mult).then_inc(*v.up(("ag", s)))

            def ln_y(s):
                eng.wait_ge(*v.at("y", s))
                ln_stats(s, "ln_y", psv(("y", s)).rearrange("p (t c) -> p t c", t=TT))

            def ln_y2(s):
                src = psv(("y", s)).rearrange("p (t c) -> p t c", t=TT)
                ln_apply(s, "ln_y", src, z[s], ("y", s, "out"))
                eng.wait_ge(*v.own())
                V_.tensor_tensor(z[s][:, :, :], z[s][:, :, :], gam.unsqueeze(1).to_broadcast([P, TT, C]), ALU.mult).then_inc(*v.up())
                eng.wait_ge(*v.at("xin", s))
                eng.wait_ge(*v.at("xb", s))
                eng.wait_ge(*v.own())
                V_.tensor_tensor(z[s][:, :, :], z[s][:, :, :], xin[s][:, :, :], ALU.add).then_inc(*v.up())
                eng.wait_ge(*v.own())
                ln_stats(s, "ln_1", z[s])

            def attn_max(n, s, h):
                eng.wait_ge(*v.at("S", s, h))
                if n >= 8:
                    eng.wait_ge(*v.at("E", *UNITS[n - 8]))
                src, nm = psv(("S", s, h)), nmax(n)
                V_.tensor_reduce(nm[:, 0:1], src[:, 0:P], AXX, ALU.max, negate=True).then_inc(*v.up())
                V_.tensor_reduce(nm[:, 1:2], src[:, P:SBLK], AXX, ALU.max, negate=True).then_inc(*v.up(("max", s, h)))

            def attn_pt(n, s, h):
                if n % 2 == 1:
                    eng.wait_ge(*v.at("PT", s, h))
                    if n >= 6:
                        eng.wait_ge(*v.at("pv", *UNITS[n - 6]))
                    V_.tensor_copy(ptbuf(n), psv(("PT", s, h))[:, 0:SBLK]).then_inc(*v.up(("PT", s, h, "out")))

            def attn_norm(n, s, h):
                if h % 2 == 0:
                    return
                O = carve_a(s)[0][3]
                eng.wait_ge(*v.at("O", s, h // 2))
                o = psv(("O", s, h // 2))[:, 0:4 * (AD + 1)].rearrange("p (t e d) -> p t e d", t=TT, e=2)
                rs = small[s][:, 128 + 4 * (h // 2 % 2):132 + 4 * (h // 2 % 2)].rearrange("p (t e) -> p t e", t=TT)
                V_.reciprocal(rs, o[:, :, :, AD]).then_inc(*v.up())
                eng.wait_ge(*v.own())
                dst = O[:, :, (h - 1) * AD:(h + 1) * AD].rearrange("p t (e d) -> p t e d", e=2)
                for t in range(TT):
                    V_.tensor_tensor(dst[:, t], o[:, t, :, 0:AD], rs[:, t, :].unsqueeze(2).to_broadcast([P, 2, AD]),
                                       ALU.mult).then_inc(*v.up(("O", s, h // 2, "out") if t == TT - 1 else None))

            def residual(s, key, base, dst, lnkey):
                eng.wait_ge(*v.at("zb", s))
                eng.wait_ge(*v.at(key, s))
                V_.tensor_tensor(dst[:, :, :], psv((key, s)).rearrange("p (t c) -> p t c", t=TT), base, ALU.add).then_inc(*v.up((key, s, "out")))
                eng.wait_ge(*v.own())
                ln_stats(s, lnkey, dst)

            def bc(ap, n):
                return ap.unsqueeze(2).to_broadcast([P, TT, n])

            def route(s):
                f = small[s]

                def t3(i):
                    return f[:, i * TT * NR:(i + 1) * TT * NR].rearrange("p (t r) -> p t r", t=TT)
                lg, gt, eq, cum = t3(0), t3(1), t3(2), t3(3)
                red = f[:, 160:164]
                top = f[:, 176:192].rearrange("p (t r) -> p t r", t=TT)
                src = psv(("route", s))[:, 0:TT * NR].rearrange("p (t r) -> p t r", t=TT)
                eng.wait_ge(*v.at("route", s))
                V_.tensor_reduce(red[:, 0:2], src, AXX, ALU.max).then_inc(*v.up())
                eng.wait_ge(*v.own())
                V_.tensor_tensor(lg, src, bc(red[:, 0:2], NR), ALU.subtract).then_inc(*v.up(("route", s, "out")))
                v.mark(("logit", s))

            def route2(s):
                f = small[s]

                def t3(i):
                    return f[:, i * TT * NR:(i + 1) * TT * NR].rearrange("p (t r) -> p t r", t=TT)
                lg, gt, eq, cum = t3(0), t3(1), t3(2), t3(3)
                red = f[:, 160:164]
                top = f[:, 176:192].rearrange("p (t r) -> p t r", t=TT)
                eng.wait_ge(*v.at("prob", s))
                V_.tensor_reduce(red[:, 0:2], lg, AXX, ALU.add).then_inc(*v.up())
                eng.wait_ge(*v.own())
                V_.reciprocal(red[:, 0:2], red[:, 0:2]).then_inc(*v.up())
                eng.wait_ge(*v.own())
                V_.tensor_tensor(lg, lg, bc(red[:, 0:2], NR), ALU.mult).then_inc(*v.up())
                settle()
                for t in range(TT):
                    V_.max(top[:, t, :], lg[:, t, :]).then_inc(*v.up())
                eng.wait_ge(*v.own())
                thr = top[:, :, TOPK - 1:TOPK].to_broadcast([P, TT, NR])
                V_.tensor_tensor(gt, lg, thr, ALU.is_gt).then_inc(*v.up())
                V_.tensor_tensor(eq, lg, thr, ALU.is_equal).then_inc(*v.up())
                eng.wait_ge(*v.own())
                V_.tensor_reduce(red[:, 2:4], gt, AXX, ALU.add).then_inc(*v.up())
                eng.wait_ge(*v.own())
                for t in range(TT):
                    V_.tensor_tensor_scan(cum[:, t, :], onesq[:, 0:NR], eq[:, t, :], red[:, 2 + t:3 + t],
                                            ALU.mult, ALU.add).then_inc(*v.up())
                eng.wait_ge(*v.own())
                V_.scalar_tensor_tensor(eq, cum, float(TOPK), eq, ALU.is_le, ALU.mult).then_inc(*v.up())
                eng.wait_ge(*v.own())
                V_.tensor_tensor(gt, gt, eq, ALU.add).then_inc(*v.up())
                eng.wait_ge(*v.own())
                V_.tensor_tensor(lg, lg, gt, ALU.mult).then_inc(*v.up())

            def gated(s, e):
                src = psv(("dn", s, e))
                eng.wait_ge(*v.at("dn", s, e))
                for t in range(TT):
                    eng.wait_ge(*v.own())
                    gcol = small[s][:, t * NR + e - NSH:t * NR + e - NSH + 1]
                    V_.scalar_tensor_tensor(z[s][:, t, :], src[:, t * C:t * C + C], gcol, z[s][:, t, :],
                                              ALU.mult, ALU.add).then_inc(*v.up(("dn", s, e, "out") if t == TT - 1 else None))

            eng.wait_ge(v.sem("first_x"), 16 * (NS + 1))
            for s in range(NS):
                mixes(s)
            done(v, 0)
            loaded(v, 0)
            with eng.Fori(0, TURNS) as g:
                v.turn = g
                gate(v, 0)
                v.stage("rwkv")
                for f in (rwkv_evict, rwkv_state):
                    for s in range(NS):
                        f(s)
                for s in range(NS):
                    rwkv_heads(s)
                    rwkv_out(s)
                for s in range(NS):
                    eng.wait_ge(*v.at("m8", s))
                    V_.tensor_scalar(mrowb(s), m8(s), BIG, -BIG, ALU.mult, ALU.add).then_inc(*v.up(("mrow", s)))
                for s in range(NS):
                    ln_y(s)
                for s in range(NS):
                    ln_y2(s)
                for s in range(NS):
                    ln_apply(s, "ln_1", z[s], z[s], ("z1", s))
                v.stage("attn")
                for s in range(NS):
                    eng.wait_ge(*v.at("biasp", s))
                    V_.tensor_copy(mbias(s), psv(("biasp", s))[:, 0:SBLK]).then_inc(*v.up())
                    eng.wait_ge(*v.own())
                    mb2 = mbias(s)
                    V_.tensor_tensor(mb2[:, 0:P], mb2[:, 0:P], qneg[:, :], ALU.min).then_inc(*v.up())
                    V_.tensor_tensor(mb2[:, T:SBLK], mb2[:, T:SBLK], qneg[:, :], ALU.min).then_inc(
                        *v.up(("bias", s)))
                for n in range(len(UNITS) + 6):
                    if n < len(UNITS):
                        attn_max(n, *UNITS[n])
                    if 0 <= n - 3 < len(UNITS):
                        attn_pt(n - 3, *UNITS[n - 3])
                    if 0 <= n - 6 < len(UNITS):
                        attn_norm(n - 6, *UNITS[n - 6])
                    if n == OUT0 + 4:
                        residual(0, "xo", z[0][:, :, :], z2[0], "ln_2")
                    if n == OUT0 + 6:
                        ln_apply(0, "ln_2", z2[0], z2[0], ("z2", 0))
                    if n == OUT0 + 9:
                        route(0)
                    if n == OUT0 + 11:
                        route2(0)
                v.stage("moe")
                for s in range(NS):
                    for e in range(0, NE, 2):
                        if e == 0:
                            eng.wait_ge(*v.at("shared", s))
                            V_.tensor_tensor(z[s][:, :, :], psv(("shared", s)).rearrange("p (t c) -> p t c", t=TT),
                                             z2[s][:, :, :], ALU.add).then_inc(*v.up(("shared", s, "out")))
                        else:
                            for j in range(2):
                                gated(s, e + j)
                        if s == 1 and e in (4, 10):
                            s_ = (4, 10).index(e)
                            eng.wait_ge(*v.at("xT", s_))
                            mixes(s_)
                        if s == 0:
                            if e == 0:
                                residual(1, "xo", z[1][:, :, :], z2[1], "ln_2")
                            if e == 2:
                                ln_apply(1, "ln_2", z2[1], z2[1], ("z2", 1))
                            if e == 10:
                                route(1)
                            if e == 12:
                                route2(1)
                    if s == 1:
                        done(v, 0)
                    eng.wait_ge(*v.own())
                    ln_stats(s, "ln_3", z[s])
                for s in range(NS):
                    ln_apply(s, "ln_3", z[s], xin[s], ("z3", s))
                v.turn, v.met = None, {}
            if stop <= 3:
                return

            v.stage("setup1")
            for s in range(NS):
                V_.memset(v1[s], 1.0).then_inc(*v.up(("ones1", s)))
                V_.memset(carve_m(s)[0][:, :, 0:TAPS - 1], 0.0).then_inc(*v.up())
            eng.wait_ge(*v.at("w12"))
            V_.tensor_reduce(al1, tmpw[:, 0], AXX, ALU.add, apply_absolute_value=True).then_inc(*v.up())
            V_.tensor_reduce(al2[:, 0:KC], tmpw[:, 1].rearrange("p m c -> p (m c)").rearrange(
                "p (m c) -> p m c", m=KC), AXX, ALU.add, apply_absolute_value=True).then_inc(*v.up())
            eng.wait_ge(*v.own())
            V_.tensor_scalar(al1, al1, 1.0 / C, None, ALU.mult).then_inc(*v.up(("alpha", 0)))
            V_.tensor_scalar(al2[:, 0:KC], al2[:, 0:KC], 1.0 / FH, None, ALU.mult).then_inc(*v.up(("alpha", 1)))
            eng.wait_ge(*v.own())
            for j in range(KC):
                V_.tensor_scalar(dxs[0][:, 0, j * P:j * P + P], ident[:, :], al2[:, j:j + 1], None, ALU.mult).then_inc(*v.up("al2diag" if j else None))
            eng.wait_ge(*v.at("al2row"))
            V_.tensor_copy(al2r, psv("al2row")[:, 0:C]).then_inc(*v.up("al2row_out"))
            done(v, 1)
            loaded(v, 1)

            def softplus_end(s, key, x, e, l, u, w, dst):
                eng.wait_ge(*v.at(key, s, "log"))
                V_.tensor_scalar(u, e, 1.0, 1.0, ALU.add, ALU.subtract).then_inc(*v.up())
                eng.wait_ge(*v.own())
                V_.tensor_scalar(w, u, 0.0, None, ALU.is_equal).then_inc(*v.up())
                eng.wait_ge(*v.own())
                V_.tensor_tensor(u, u, w, ALU.add).then_inc(*v.up())
                eng.wait_ge(*v.own())
                V_.reciprocal(u, u).then_inc(*v.up())
                eng.wait_ge(*v.own())
                V_.tensor_tensor(l, l, u, ALU.mult).then_inc(*v.up())
                eng.wait_ge(*v.own())
                V_.tensor_tensor(l, l, w, ALU.add).then_inc(*v.up())
                eng.wait_ge(*v.own())
                V_.tensor_tensor(l, l, e, ALU.mult).then_inc(*v.up())
                eng.wait_ge(*v.own())
                V_.scalar_tensor_tensor(dst, x, 0.0, l, ALU.max, ALU.add).then_inc(*v.up((key, s, "sp")))

            def rowb(r, n):
                return r.unsqueeze(1).to_broadcast([P, TT, n])

            def dt_in(s):
                eng.wait_ge(*v.at("dt", s))
                V_.tensor_tensor(th(sm(s, 0), MH), th(psv(("dt", s))[:, 0:2 * MH], MH), rowb(dtb, MH), ALU.add).then_inc(*v.up(("dt", s, "out")))
                v.mark(("dtx", s, "x"))

            def taps(s):
                xpad, xb = carve_m(s)[0:2]
                for m in range(CM):
                    eng.wait_ge(*v.at("tap3", s, m))
                    for k in range(TAPS - 1):
                        if k:
                            eng.wait_ge(*v.own())
                        V_.scalar_tensor_tensor(xb[:, m, :], xpad[:, m, k:k + T], ck[:, m, k:k + 1], xb[:, m, :],
                                                  ALU.mult, ALU.add).then_inc(*v.up(("taps", s, m) if k == TAPS - 2 else None))

            def mamba_mid(s):
                eng.wait_ge(*v.at("cs", s))
                V_.tensor_scalar(sm(s, 4), psv(("cs", s))[:, 0:2 * MH], -1.0, None, ALU.mult).then_inc(
                    *v.up(("cs", s, "out")))

            def parts(s, src, n, marks):
                V_.tensor_copy(c3[s][0:n, :], src).then_inc(*v.up())
                eng.wait_ge(*v.own())
                V_.tensor_tensor(rest[0:n, :], src, c3[s][0:n, :], ALU.subtract).then_inc(*v.up(marks[0]))
                eng.wait_ge(*v.own())
                V_.tensor_copy(rest1[0:n, :], rest[0:n, :]).then_inc(*v.up())
                eng.wait_ge(*v.own())
                V_.tensor_copy(c3[s][32:32 + n, :], rest1[0:n, :]).then_inc(*v.up())
                V_.tensor_tensor(c3[s][64:64 + n, :], rest[0:n, :], rest1[0:n, :], ALU.subtract).then_inc(
                    *v.up(marks[1]))

            def mamba_rows(s):
                eng.wait_ge(*v.at("csr", s))
                parts(s, psv(("csr", s))[0:MH, 0:T], MH, [("csr", s, "out"), ("csr3", s)])

            def mamba_mid2(s):
                xs, xdt = carve_m(s)[3:5]
                eng.wait_ge(*v.at("CB", s))
                V_.tensor_tensor(cbm[s], psv(("CB", s))[:, 0:SBLK], le[:, :], ALU.mult).then_inc(*v.up(("CB", s, "out")))
                for t in range(TT):
                    eng.wait_ge(*v.at("xs", s, t, "out"))
                    V_.tensor_tensor(xdt[:, t, :].rearrange("p (h d) -> p h d", h=MH),
                                       xs[:, t, :].rearrange("p (h d) -> p h d", h=MH),
                                       th(sm(s, 9), MH)[:, t, :].unsqueeze(2).to_broadcast([P, MH, MD]), ALU.mult).then_inc(*v.up(("xdt", s) if t else None))

            def pair(key, s, pr):
                i = PAIRS.index((key, s, pr)) % 6
                return pq[:, 2 * i * SBLK:2 * (i + 1) * SBLK]

            def mamba_product(s, pr):
                eng.wait_ge(*v.at("Ex", s, pr))
                e = pair("Y", s, pr).rearrange("p (j c) -> p j c", j=2)
                V_.tensor_tensor(e, e, cbm[s].unsqueeze(1).to_broadcast([P, 2, SBLK]), ALU.mult).then_inc(
                    *v.up(("M", s, pr)))

            def mlstm_product(s, pr):
                eng.wait_ge(*v.at("Dx", s, pr))
                for h in (2 * pr, 2 * pr + 1):
                    e = ebuf("H", s, h)
                    eng.wait_ge(*v.at("qk", s, h))
                    V_.scalar_tensor_tensor(e, psv(("qk", s, h))[:, 0:SBLK], LD ** -0.5, e, ALU.mult,
                                            ALU.mult).then_inc(*v.up(("qk", s, h, "out")))
                v.mark(("C", s, pr))

            def mamba_y(s):
                xpad, xb, sz, xs, xdt, y, yT = carve_m(s)
                eng.wait_ge(*v.at("dx", s))
                for t in range(TT):
                    eng.wait_ge(*v.at("Y", s, t))
                    yb = ps[:, (6 - 2 * s) + t, :]
                    V_.tensor_tensor(y[:, t, :], yb, dxs[s][:, t, :], ALU.add).then_inc(*v.up(("Y", s, t, "out")))
                for t in range(TT):
                    eng.wait_ge(*v.own())
                    V_.tensor_tensor(y[:, t, :], y[:, t, :], sz[:, t, :], ALU.mult).then_inc(*v.up(("y", s, t)))

            def mlstm_in(s):
                eng.wait_ge(*v.at("gt", s))
                gts = th(sm(s, 0), 8)
                V_.tensor_tensor(gts, th(psv(("gt", s))[:, 0:16], 8), rowb(gb, 8), ALU.add).then_inc(*v.up(("gt", s, "out")))
                eng.wait_ge(*v.own())
                V_.tensor_scalar(th(sm(s, 1, 8), LH), gts[:, :, LH:2 * LH], -1.0, None, ALU.mult).then_inc(*v.up(("fg", s, "x")))

            def mlstm_lf(s):
                softplus_end(s, "fg", sm(s, 1, 8), sm(s, 2, 8), sm(s, 3, 8), sm(s, 4, 8), sm(s, 7, 8), sm(s, 5, 8))
                eng.wait_ge(*v.own())
                V_.tensor_scalar(sm(s, 5, 8), sm(s, 5, 8), -1.0, None, ALU.mult).then_inc(*v.up(("lf", s)))

            def mlstm_a(s):
                eng.wait_ge(*v.at("cs2", s))
                V_.tensor_copy(sm(s, 9, 8), psv(("cs2", s))[:, 0:8]).then_inc(*v.up(("cs2", s, "out")))
                eng.wait_ge(*v.own())
                V_.tensor_tensor(th(sm(s, 6, 8), LH), th(sm(s, 0), 8)[:, :, 0:LH], th(sm(s, 9, 8), LH),
                                   ALU.subtract).then_inc(*v.up(("a", s)))

            def mlstm_scan(s):
                eng.wait_ge(*v.at("ar", s))
                V_.tensor_tensor_scan(csT[s][0:LH, :], zrow[0:LH, :], psv(("ar", s))[0:LH, 0:T], -BIG,
                                        ALU.add, ALU.max).then_inc(*v.up(("ar", s, "out")))
                v.mark(("mt", s))
                eng.wait_ge(*v.own())
                parts(s, csT[s][0:LH, :], LH, [None, ("mt3", s)])

            def mlstm_mc(s):
                eng.wait_ge(*v.at("mtok", s))
                V_.tensor_tensor(sm(s, 8, 8), psv(("mtok", s))[:, 0:8], sm(s, 9, 8), ALU.add).then_inc(*v.up(("mtok", s, "out")))
                v.mark(("mc", s))

            def h4(x):
                return x.rearrange("p (h d) -> p h d", h=LH)

            def mlstm_h(s):
                hb = carve_m(s)[5]
                den = th(sm(s, 10, 8), LH)
                eng.wait_ge(*v.at("nrm", s))
                for t in range(TT):
                    eng.wait_ge(*v.at("H", s, t))
                    src = h4(ps[:, 6 - 2 * s + t, 0:LH * (LD + 1)])
                    rs = src[:, :, LD]
                    V_.tensor_scalar(den[:, t, :], rs, -1.0, None, ALU.mult).then_inc(*v.up())
                    eng.wait_ge(*v.own())
                    V_.tensor_tensor(den[:, t, :], rs, den[:, t, :], ALU.max).then_inc(*v.up())
                    eng.wait_ge(*v.own())
                    V_.tensor_tensor(den[:, t, :], den[:, t, :], th(sm(s, 8, 8), LH)[:, t, :], ALU.max).then_inc(*v.up())
                    eng.wait_ge(*v.own())
                    V_.tensor_scalar(den[:, t, :], den[:, t, :], ML_EPS, None, ALU.add).then_inc(*v.up())
                    eng.wait_ge(*v.own())
                    V_.reciprocal(den[:, t, :], den[:, t, :]).then_inc(*v.up())
                    eng.wait_ge(*v.own())
                    V_.tensor_tensor(h4(hb[:, t, 0:C]), src[:, :, 0:LD],
                                       den[:, t, :].unsqueeze(2).to_broadcast([P, LH, LD]), ALU.mult).then_inc(*v.up(("H", s, t, "out")))
                eng.wait_ge(*v.own())
                for t in range(TT):
                    for h in range(LH):
                        V_.bn_stats(st6[s][:, t * LH + h, :], hb[:, t, h * LD:(h + 1) * LD]).then_inc(*v.up())
                settle()
                for i in range(TT * LH):
                    V_.bn_aggr(mv[s][:, i, :], st6[s][:, i, :]).then_inc(*v.up(("ln_h", s, "mv") if i == TT * LH - 1 else None))

            def mlstm_h2(s):
                hb = carve_m(s)[5]
                eng.wait_ge(*v.at("ln_h", s, "rstd"))
                for t in range(TT):
                    x = h4(hb[:, t, 0:C])
                    V_.tensor_tensor(x, x, mv[s][:, t * LH:(t + 1) * LH, 0:1].to_broadcast([P, LH, LD]),
                                       ALU.subtract).then_inc(*v.up())
                eng.wait_ge(*v.own())
                for t in range(TT):
                    x = h4(hb[:, t, 0:C])
                    V_.tensor_tensor(x, x, rstd[s][:, t * LH:(t + 1) * LH].unsqueeze(2).to_broadcast([P, LH, LD]),
                                       ALU.mult).then_inc(*v.up())
                eng.wait_ge(*v.own())
                V_.tensor_tensor(hb[:, :, 0:C], hb[:, :, 0:C], rowb(onorm, C), ALU.mult).then_inc(*v.up())
                eng.wait_ge(*v.own())
                V_.tensor_tensor(z2[s][:, :, :], hb[:, :, 0:C], z[s][:, :, :], ALU.add).then_inc(*v.up())
                eng.wait_ge(*v.own())
                ln_stats(s, "ln_5", z2[s])

            with eng.Fori(0, TURNS) as g:
                v.turn = g
                gate(v, 1)
                v.stage("mamba")
                for s in range(NS):
                    dt_in(s)
                for s in range(NS):
                    softplus_end(s, "dtx", sm(s, 0), sm(s, 1), sm(s, 2), sm(s, 5), sm(s, 6), sm(s, 9))
                    eng.wait_ge(*v.own())
                    V_.scalar_tensor_tensor(th(sm(s, 3), MH), th(sm(s, 9), MH), -1.0, rowb(Arow, MH),
                                              ALU.mult, ALU.mult).then_inc(*v.up(("dA", s)))
                for f in (taps, mamba_mid, mamba_rows, mamba_mid2):
                    for s in range(NS):
                        f(s)
                for step, s, *pr in ORDER:
                    if step == "decay":
                        mamba_product(s, *pr)
                    if step == "y":
                        mamba_y(s)
                    if step == "norm":
                        y = carve_m(s)[5]
                        eng.wait_ge(*v.at("yr", s))
                        for t in range(TT):
                            V_.tensor_scalar(y[:, t, :], y[:, t, :], sm(s, 7)[:, t:t + 1], None, ALU.mult).then_inc(
                                *v.up(("yn", s) if t else None))
                    if step == "out":
                        eng.wait_ge(v.sem(f"out_y{s}"), v.turn * 16 + 16)
                        eng.wait_ge(*v.at("mo", s))
                        V_.scalar_tensor_tensor(z[s][:, :, :], xin[s][:, :, :], 2.0,
                                                psv(("mo", s)).rearrange("p (t c) -> p t c", t=TT),
                                                ALU.mult, ALU.add).then_inc(*v.up(("mo", s, "out")))
                        eng.wait_ge(*v.own())
                        ln_stats(s, "ln_4", z[s])
                    if step == "ln4":
                        ln_apply(s, "ln_4", z[s], z[s], ("z4", s))
                    if step == "gates":
                        mlstm_in(s)
                    if step == "forget":
                        mlstm_lf(s)
                    if step == "gain":
                        mlstm_a(s)
                    if step == "rows":
                        mlstm_scan(s)
                    if step == "cols":
                        mlstm_mc(s)
                    if step == "score":
                        mlstm_product(s, *pr)
                    if step == "hidden":
                        mlstm_h(s)
                    if step == "heads":
                        mlstm_h2(s)
                    if step == "ln5":
                        ln_apply(s, "ln_5", z2[s], z2[s], ("z5", s))
                    if step == "down":
                        eng.wait_ge(*v.at("f2", s))
                        V_.tensor_tensor(z[s][:, :, :], psv(("f2", s)).rearrange("p (t c) -> p t c", t=TT),
                                         rowb(al2r, C), ALU.mult).then_inc(*v.up(("f2", s, "out")))
                        if s == NS - 1:
                            done(v, 1)
                        eng.wait_ge(*v.at("z5b", s))
                        eng.wait_ge(*v.own())
                        V_.tensor_tensor(z[s][:, :, :], z[s][:, :, :], z2[s][:, :, :], ALU.add).then_inc(*v.up())
                        eng.wait_ge(*v.own())
                        ln_stats(s, "ln_6", z[s])
                    if step == "ln6":
                        ln_apply(s, "ln_6", z[s], z[s], ("z6", s))
                v.turn, v.met = None, {}

        @block.gpsimd
        def _(eng):
            po = lane(eng, "pool")
            G = nc.gpsimd
            po.stage("consts")
            G.memset(ident[:, :], 0.0).then_inc(*po.up())
            G.memset(onesq[:, :], 1.0).then_inc(*po.up())
            G.memset(le[:, :], 1.0).then_inc(*po.up())
            G.memset(qneg[:, :], 0.0).then_inc(*po.up())
            G.memset(sbig[:, :], 0.0).then_inc(*po.up())
            G.memset(hcol[:, :], 1.0).then_inc(*po.up())
            G.memset(srow[:, :, :], 0.0).then_inc(*po.up())
            G.memset(onesb[:, :], 1.0).then_inc(*po.up())
            for i, e in enumerate((LN_EPS, ML_EPS, 1.0)):
                G.memset(eps[:, i:i + 1], e).then_inc(*po.up())
            G.iota(pint[:, :], [[0, 1]], base=0, channel_multiplier=1).then_inc(*po.up())
            eng.wait_ge(*po.own())
            sel = G.affine_select
            sel(out=ident[:, :], in_=ident[:, :], compare_op=ALU.not_equal, fill=1.0, base=0,
                   pattern=[[-1, P]], channel_multiplier=1).then_inc(*po.up())
            for c in (0, T):
                sel(out=le[:, c:c + P], in_=le[:, c:c + P], compare_op=ALU.is_ge, fill=0.0, base=0,
                       pattern=[[1, P]], channel_multiplier=-1).then_inc(*po.up())
            sel(out=qneg[:, :], in_=qneg[:, :], compare_op=ALU.is_ge, fill=-BIG, base=0,
                   pattern=[[-1, P]], channel_multiplier=1).then_inc(*po.up())
            for c in (0, T):
                sel(out=sbig[:, c:c + P], in_=sbig[:, c:c + P], compare_op=ALU.is_ge, fill=BIG, base=0,
                       pattern=[[1, P]], channel_multiplier=-1).then_inc(*po.up())
            for q in range(3):
                if q:
                    eng.wait_ge(*po.own())
                sel(out=srow[:, :, :], in_=srow[:, :, :], compare_op=ALU.not_equal, fill=1.0, base=-32 * q,
                    pattern=[[-1, 8], [0, P]], channel_multiplier=1).then_inc(*po.up())
            sel(out=hcol[:, :], in_=hcol[:, :], compare_op=ALU.is_ge, fill=0.0, base=0,
                   pattern=[[-RD, 8]], channel_multiplier=1).then_inc(*po.up())
            G.tensor_copy(pcol[:, 0:1], pint[:, :]).then_inc(*po.up())
            eng.wait_ge(*po.own())
            sel(out=hcol[:, :], in_=hcol[:, :], compare_op=ALU.is_ge, fill=0.0, base=RD - 1,
                   pattern=[[RD, 8]], channel_multiplier=-1).then_inc(*po.up())
            G.tensor_scalar(pcol[:, 1:2], pcol[:, 0:1], float(-MID), None, ALU.add).then_inc(*po.up())
            G.tensor_scalar(pcol[:, 2:3], pcol[:, 0:1], float(-P - MID), None, ALU.add).then_inc(*po.up())
            G.tensor_scalar(pcol[:, 3:4], pcol[:, 0:1], -1.0, float(MID), ALU.mult, ALU.add).then_inc(*po.up())
            G.tensor_copy(identb[:, :], ident[:, :]).then_inc(*po.up())
            eng.wait_ge(*po.own())
            po.stage("ready")
            eng.wait_ge(*po.at("tdma"))
            G.tensor_copy(srow[:, 0, 0:1], srow[:, 0, 0:1]).then_inc(*po.up("lam"))
            done(po, 0)
            loaded(po, 0)
            with eng.Fori(0, TURNS) as g:
                po.turn = g
                gate(po, 0)
                po.stage("rwkv")
                for s in range(NS):
                    eng.wait_ge(*po.at("xin", s))
                    G.tensor_tensor(xin[s][:, :, :], xin[s][:, :, :],
                                       bet.unsqueeze(1).to_broadcast([P, TT, C]), ALU.add).then_inc(*po.up(("xb", s)))
                po.stage("attn")
                for s in range(NS):
                    eng.wait_ge(*po.at("zT1", s))
                    G.tensor_tensor(z[s][:, :, :], z[s][:, :, :],
                                       bo_.unsqueeze(1).to_broadcast([P, TT, C]), ALU.add).then_inc(*po.up(("zb", s)))
                done(po, 0)
                po.turn, po.met = None, {}
            if stop <= 3:
                return

            done(po, 1)
            loaded(po, 1)
            with eng.Fori(0, TURNS) as g:
                po.turn = g
                gate(po, 1)
                po.stage("mamba")
                for s in range(NS):
                    xs = carve_m(s)[3]
                    for t in range(TT):
                        eng.wait_ge(*po.at("xs", s, t, "out"))
                        G.tensor_tensor(dxs[s][:, t, :], xs[:, t, :], drow, ALU.mult).then_inc(*po.up(("dx", s) if t else None))
                po.stage("ffn")
                for s in range(NS):
                    eng.wait_ge(*po.at("zTc", s))
                    G.tensor_tensor(z2[s][:, :, :], z2[s][:, :, :],
                                       b2r.unsqueeze(1).to_broadcast([P, TT, C]), ALU.add).then_inc(*po.up(("z5b", s)))
                done(po, 1)
                po.turn, po.met = None, {}

        @block.sync
        def _(eng):
            sp = lane(eng, "sp")

            def dma(dst, src, sem, mark=None):
                nc.sync.dma_start(dst, src).then_inc(*sp.up(mark, by=16, sem=sem))

            def written(name):
                count = sp.turn * 16 + 16
                for s in range(NS):
                    eng.wait_ge(sp.sem(f"{name}{s}"), count)

            for name in ("out_mid", "out_y"):
                for s in range(NS):
                    eng.drain().then_inc(sp.sem(f"{name}{s}"), 16)
            for s in range(NS):
                dma(xT[s][:, :, :], a["xT"][B - NS + s], "first_x")
            dma(mix[:, :, :], a["mixes"], "first_x")
            dma(t1, a["time_decay"].unsqueeze(0).to_broadcast([P, C]), "tdecay", "tdma")
            for d, s_ in ((wr, "W_r"), (wv, "W_v"), (wk, "W_k"), (wg, "W_g"), (wo, "W_o")):
                dma(d, a[s_], "weights0")
            for d, s_ in ((gam, "gamma"), (bet, "beta"), (bo_, "bo")):
                dma(d, a[s_].unsqueeze(0).to_broadcast([P, C]), "weights0")
            eng.wait_ge(*sp.own())
            eng.wait_ge(sp.sem("tdecay"), 16)
            done(sp, 0)
            for d, s_ in ((wkk, "Wk"), (wvv, "Wv"), (wq, "Wq"), (woo, "Wo"), (rw, "router"), (up, "up"),
                          (down, "down")):
                dma(d, a[s_], "weights_rest")
            sp.mark("rest")
            with eng.Fori(0, TURNS) as g:
                sp.turn = g
                gate(sp, 0)
                for s in range(NS):
                    b = g * NS + s
                    dma(xT[s][:, :, :], dyn(a["xT"], b), f"in_xT{s}", ("xT", s))
                written("out_mid")
                for s in range(NS):
                    b = g * NS + s
                    dma(xin[s][:, :, :], dyn(a["x"], b), f"in_x{s}", ("xin", s))
                    dma(m8(s), dyn(a["mask"], b), f"in_mask{s}", ("m8", s))
                    dma(cT[s][:, :, :], dyn(a["cT"], b), f"in_cT{s}", ("cT", s))
                for s in range(NS):
                    dst = dyn(xmid, g * NS + s)
                    eng.wait_ge(*sp.at("z3", s))
                    dma(dst, xin[s][:, :, :], f"out_mid{s}", ("mid", s))
                sp.turn, sp.met = None, {}
            for e in ENGINES:
                eng.wait_ge(sp.sem(f"turned0_{e}"), TURNS + 1)
            dma(tmpw[:, 0], a["w1"], "w12")
            dma(flat(tmpw[:, 1]), a["w2"], "w12", "w12")
            for d, s_ in ((Arow, "A_log"), (dtb, "dt_bias"), (drow, "D"), (gb, "gate_b"), (onorm, "onorm"), (b2r, "b2")):
                dma(d, a[s_].unsqueeze(0).to_broadcast([P, d.shape[1]]), "rows1")
            sp.mark("p2rows")
            for d, s_ in ((win, "in_proj"), (wout, "out_proj"), (ck, "conv_w"), (cb, "conv_b"), (nw, "norm_w"),
                          (gk, "gate_k"), (b1, "b1")):
                dma(d, a[s_], "weights1")
            sp.mark("p2weights")
            for s in range(NS):
                eng.wait_ge(sp.sem(f"out_mid{s}"), 16 * TURNS + 16)
            dma(xmid[B:B + NS], xmid[0:NS], "wrap", "wrap")
            for s in range(NS):
                dma(xin[s][:, :, :], xmid[s], f"first_x2_{s}", ("first_x2", s))
            eng.wait_ge(*sp.at("p2weights"))
            eng.wait_ge(*sp.at("w12"))
            eng.wait_ge(*sp.at("p2rows"))
            eng.wait_ge(*sp.at("wrap"))
            done(sp, 1)
            with eng.Fori(0, TURNS) as g:
                sp.turn = g
                gate(sp, 1)
                for s in range(NS):
                    b = g * NS + s
                    dma(cT[s][:, :, :], dyn(a["cT"], b), f"in_cT2{s}", ("cT2", s))
                for s in range(NS):
                    b = g * NS + s
                    for t in range(TT):
                        dma(v1[s][:, t * LH * (LD + 1):(t + 1) * LH * (LD + 1)].rearrange(
                            "p (h d) -> p h d", h=LH)[:, :, 0:LD], dyn(a["c"], b)[:, t, :].rearrange(
                            "p (h d) -> p h d", h=LH), f"in_v{s}", ("v1", s) if t else None)
                for s in range(NS):
                    src = dyn(xmid, g * NS + NS + s)
                    eng.wait_ge(*sp.at("mo", s, "out"))
                    dma(xin[s][:, :, :], src, f"in_x2{s}", ("xin2", s))
                for s in range(NS):
                    dst = dyn(out, g * NS + s)
                    eng.wait_ge(*sp.at("z6", s))
                    dma(dst, z[s][:, :, :], f"out_y{s}", ("outd", s))
                sp.turn, sp.met = None, {}
            for s in range(NS):
                eng.wait_ge(sp.sem(f"out_y{s}"), 16 * TURNS + 16)


def laid_out(i):
    import numpy as np
    i = {k: np.asarray(v) for k, v in i.items()}

    def cols(w):
        w = np.ascontiguousarray(w.T)
        return w.reshape(-1, P, w.shape[1]).transpose(1, 0, 2)

    def tok(x):
        return x.reshape(B, TT, P, C).transpose(0, 2, 1, 3)

    def chan(x):
        return x.transpose(0, 2, 1).reshape(B, KC, P, T).transpose(0, 2, 1, 3)
    up = np.concatenate([i["L0_ffn_shared_up"], i["L0_ffn_routed_up"]])
    down = np.concatenate([i["L0_ffn_shared_down"], i["L0_ffn_routed_down"]])
    a = {
        "x": tok(i["x"]), "xT": np.roll(chan(i["x"]), -NS, axis=0), "cT": chan(i["ctx_1024"]),
        "mask": i["mask_BxS2_bf1"].view(np.uint8).reshape(B, 1, T)[:, 0],
        "time_decay": i["L0_attn_time_decay"],
        "mixes": np.stack([i["L0_attn_time_mix_" + n] for n in "rvkg"]).reshape(4, KC, P).transpose(2, 0, 1),
        "W_r": cols(i["L0_attn_W_r"]), "W_k": cols(i["L0_attn_W_k"]), "W_v": cols(i["L0_attn_W_v"]),
        "W_g": cols(i["L0_attn_W_g"]), "W_o": cols(i["L0_attn_W_o"]),
        "gamma": i["L0_attn_ln_gamma"], "beta": i["L0_attn_ln_beta"],
        "Wq": cols(i["L0_xattn_Wq"]), "Wk": cols(i["L0_xattn_Wk"]), "Wv": cols(i["L0_xattn_Wv"]),
        "Wo": cols(i["L0_xattn_Wo"]), "bo": i["L0_xattn_bo"],
        "up": up.reshape(NE, ED, KC, P).transpose(3, 0, 2, 1).reshape(P, NE * KC, ED),
        "down": down.transpose(2, 0, 1), "router": cols(i["L0_ffn_router_w"]),
        "c": tok(i["ctx_1024"]), "in_proj": cols(i["L1_attn_in_proj_w"]), "out_proj": cols(i["L1_attn_out_proj_w"]),
        "conv_w": i["L1_attn_conv_w"].reshape(CM, P, TAPS).transpose(1, 0, 2),
        "conv_b": i["L1_attn_conv_b"].reshape(CM, P).T, "dt_bias": i["L1_attn_dt_bias"],
        "A_log": i["L1_attn_A_log"], "D": np.repeat(i["L1_attn_D"], MD), "norm_w": i["L1_attn_norm_w"].reshape(DM, P).T,
        "gate_k": np.concatenate([i["L1_xattn_igate_kernel"], i["L1_xattn_fgate_kernel"]], 1)
        .reshape(3 * KC, P, 2 * LH).transpose(1, 0, 2),
        "gate_b": np.concatenate([i["L1_xattn_igate_bias"], i["L1_xattn_fgate_bias"]]),
        "onorm": i["L1_xattn_outnorm_scale"], "w1": i["L1_ffn_w1"].reshape(FM, P, C).transpose(1, 0, 2),
        "w2": i["L1_ffn_w2"].reshape(KC, P, FH).transpose(1, 0, 2).reshape(P, KC * FH),
        "b1": i["L1_ffn_b1"].reshape(FM, P).T, "b2": i["L1_ffn_b2"],
    }
    return {k: np.ascontiguousarray(v) for k, v in a.items()}


def program(nc, scratch, arrays, stop=9):
    def declare(nc):
        a = {k: nc.dram_tensor(f"in_{k}", v.shape, mybir.dt.from_np(v.dtype), kind="ExternalInput").ap()
             for k, v in arrays.items()}
        out = nc.dram_tensor("out", (B, P, TT, C), F32, kind="ExternalOutput").ap()
        return a, out, out if stop <= 3 else nc.dram_tensor("xmid", (B + NS, P, TT, C), F32).ap()
    counted = Book()
    build(scratch, *declare(scratch), counted, stop)
    build(nc, *declare(nc), Book(counted), stop)


def kernel(**inputs):
    import concourse.bacc as bacc
    from concourse.bass_utils import run_bass_kernel_spmd
    nc, scratch = (bacc.Bacc("TRN2", target_bir_lowering=False, num_devices=1) for _ in range(2))
    arrays = laid_out(inputs)
    program(nc, scratch, arrays)
    r = run_bass_kernel_spmd(nc, [{"in_" + k: v for k, v in arrays.items()}], core_ids=[0])
    return r.results[0]["out"].transpose(0, 2, 1, 3).reshape(B, T, C)
```
